# Optimizing a Trainium2 kernel written in Bass

```python
import numpy as np
import jax
import jax.numpy as jnp

def _softmax(x, axis=-1):
    return jax.nn.softmax(x, axis=axis)

def _gelu(x):
    return jax.nn.gelu(x, approximate=True)

def _silu(x):
    return jax.nn.silu(x)

def _sigmoid(x):
    return jax.nn.sigmoid(x)

def _layernorm(x, axis=-1, eps=1e-05):
    m = jnp.mean(x, axis=axis, keepdims=True)
    v = jnp.var(x, axis=axis, keepdims=True)
    return (x - m) / jnp.sqrt(v + eps)

def _scatter_add(tgt, idx, src, axis=0):
    return tgt.at[idx].add(src)

def _segment_sum(src, seg, n):
    return jax.ops.segment_sum(src, seg, n)
kernel_name = 'mk_flamingo_gated_d2_seqx_r4_a7a548'

def setup_inputs(seed: int=0):
    np.random.seed(seed)
    _w = jnp.asarray

    def _rec_inputs():
        import jax
        import jax.numpy as jnp
        _rk = jax.random.key(seed)
        x = -0.0002928 + 1 * jax.random.normal(jax.random.fold_in(_rk, 1), (16, 256, 256), jnp.float32)
        _lenS = 256 - jax.random.randint(jax.random.fold_in(_rk, 7), (16,), 0, max(1, 256 // 4) + 1, jnp.int32)
        _lenS2 = 256 - jax.random.randint(jax.random.fold_in(_rk, 8), (16,), 0, max(1, 256 // 4) + 1, jnp.int32)
        _ctx_1024P = jax.random.normal(jax.random.fold_in(_rk, 11), (16, 16, 256), jnp.float32)
        _ctx_1024c = jax.random.dirichlet(jax.random.fold_in(_rk, 511), 0.3 * jnp.ones((16,), jnp.float32), (16, 256))
        _ctx_1024t = jnp.einsum('bsk,bkd->bsd', _ctx_1024c, _ctx_1024P)
        _ctx_1024t = _ctx_1024t * jax.lax.rsqrt(jnp.mean(jnp.square(_ctx_1024t)) + 1e-12) * 0.953939
        ctx_1024 = -1.39393e-06 + 0.999914 * (_ctx_1024t + 0.3 * jax.random.normal(jax.random.fold_in(_rk, 611), (16, 256, 256), jnp.float32))
        _g = jax.random.normal(jax.random.fold_in(_rk, 9001), (2, 2), jnp.float32)
        _g = jnp.sign(_g) * jnp.maximum(jnp.abs(_g), 1.0) + (_g == 0) * 1.0
        g_xattn = _g[0]
        g_ffn = _g[1]
        return (x, ctx_1024, g_xattn, g_ffn)
    x, ctx_1024, g_xattn, g_ffn = _rec_inputs()

    def _L0_xattn_setup():
        import jax, jax.numpy as jnp
        import numpy as np
        B, S, D, NH = (2, 512, 256, 8)
        DH = D // NH
        EPS = 1e-06
        LN_EPS = 1e-05

        def _mlstm_cell(q, k, v, igate_w, igate_b, fgate_w, fgate_b, ln_scale):
            Slen = q.shape[0]
            ifg = jnp.concatenate([q, k, v], axis=-1)
            ig = (ifg @ igate_w.T + igate_b).T
            fg = (ifg @ fgate_w.T + fgate_b).T
            qh = q.reshape(Slen, NH, DH).transpose(1, 0, 2)
            kh = k.reshape(Slen, NH, DH).transpose(1, 0, 2)
            vh = v.reshape(Slen, NH, DH).transpose(1, 0, 2)
            log_f = jax.nn.log_sigmoid(fg)
            cs = jnp.cumsum(log_f, axis=1)
            fg_mat = cs[:, :, None] - cs[:, None, :]
            mask = jnp.tril(jnp.ones((Slen, Slen), dtype=bool))
            log_fg_mat = jnp.where(mask, fg_mat, -jnp.inf)
            log_D = log_fg_mat + ig[:, None, :]
            max_log_D = jnp.max(log_D, axis=-1, keepdims=True)
            D_mat = jnp.exp(log_D - max_log_D)
            qk = jnp.einsum('hsd,htd->hst', qh, kh) / np.sqrt(DH)
            C = qk * D_mat
            normalizer = jnp.maximum(jnp.abs(C.sum(axis=-1, keepdims=True)), jnp.exp(-max_log_D))
            h = jnp.einsum('hst,htd->hsd', C / (normalizer + EPS), vh)
            h = h.transpose(1, 0, 2).reshape(Slen, D)
            mu = h.mean(axis=-1, keepdims=True)
            var = h.var(axis=-1, keepdims=True)
            return (h - mu) / jnp.sqrt(var + LN_EPS) * ln_scale
        key = jax.random.key(seed)
        ks = jax.random.split(key, 8)
        rnd = lambda k, sh, s=1.0: jax.random.normal(k, sh, dtype=jnp.float32) * s
        return {'q': rnd(ks[0], (B, S, D)), 'k': rnd(ks[1], (B, S, D)), 'v': rnd(ks[2], (B, S, D)), 'igate_w': rnd(ks[3], (NH, 3 * D), 0.02), 'igate_b': jnp.linspace(3.0, 6.0, NH, dtype=jnp.float32), 'fgate_w': rnd(ks[4], (NH, 3 * D), 0.02), 'fgate_b': rnd(ks[5], (NH,), 0.3162278), 'ln_scale': jnp.ones((D,), dtype=jnp.float32)}
    _L0_xattn_all = _L0_xattn_setup()
    _L0_xattn_in = {k: v for k, v in _L0_xattn_all.items() if k in ('igate_w', 'igate_b', 'fgate_w', 'fgate_b', 'ln_scale')}
    del _L0_xattn_all

    def _L0_ffn_setup():
        import jax, jax.numpy as jnp
        import numpy as np
        BITS = 8
        LORA_RANK = 16
        LORA_ALPHA = 32
        SCALING = LORA_ALPHA / LORA_RANK

        def fake_quant_weight(w, bits=BITS):
            qmax = 2.0 ** (bits - 1) - 1
            scale = jnp.max(jnp.abs(w)) / qmax
            wq = jnp.clip(jnp.round(w / scale), -qmax - 1, qmax) * scale
            return w + jax.lax.stop_gradient(wq - w)

        def qat_lora_linear(x, W, b, A, B):
            Wq = fake_quant_weight(W)
            base = jnp.einsum('bsi,oi->bso', x, Wq) + b
            lora = jnp.einsum('bsr,or->bso', jnp.einsum('bsi,ri->bsr', x, A), B)
            return base + SCALING * lora
        key = jax.random.key(seed)
        ks = jax.random.split(key, 9)
        d, f = (256, 1024)
        s_in = 1.0 / np.sqrt(d)
        s_ff = 1.0 / np.sqrt(f)
        return {'hidden_states': jax.random.normal(ks[0], (4, 512, d), jnp.float32), 'W_fc': jax.random.normal(ks[1], (f, d), jnp.float32) * s_in, 'b_fc': jnp.zeros((f,), jnp.float32), 'A_fc': jax.random.normal(ks[2], (LORA_RANK, d), jnp.float32) * s_in, 'B_fc': jnp.zeros((f, LORA_RANK), jnp.float32), 'W_proj': jax.random.normal(ks[3], (d, f), jnp.float32) * s_ff, 'b_proj': jnp.zeros((d,), jnp.float32), 'A_proj': jax.random.normal(ks[4], (LORA_RANK, f), jnp.float32) * s_ff, 'B_proj': jnp.zeros((d, LORA_RANK), jnp.float32)}
    _L0_ffn_all = _L0_ffn_setup()
    _L0_ffn_in = {k: v for k, v in _L0_ffn_all.items() if k in ('W_fc', 'b_fc', 'A_fc', 'B_fc', 'W_proj', 'b_proj', 'A_proj', 'B_proj')}
    del _L0_ffn_all

    def _L1_xattn_setup():
        import jax, jax.numpy as jnp
        import numpy as np
        HIDDEN = 256
        NUM_HEADS = 16
        HEAD_DIM = HIDDEN // NUM_HEADS
        key = jax.random.key(seed)
        k1, k2, k3, k4, k5 = jax.random.split(key, 5)
        B, S, T, H = (2, 512, 512, HIDDEN)
        scale = 0.02
        return {'query': jax.random.normal(k1, (B, S, H), dtype=jnp.float32), 'key_value': jax.random.normal(k2, (B, T, H), dtype=jnp.float32), 'Wq': jax.random.normal(k3, (H, H), dtype=jnp.float32) * scale, 'Wkv': jax.random.normal(k4, (H, 2 * H), dtype=jnp.float32) * scale, 'Wc': jax.random.normal(k5, (H, H), dtype=jnp.float32) * scale}
    _L1_xattn_all = _L1_xattn_setup()
    _L1_xattn_in = {k: v for k, v in _L1_xattn_all.items() if k in ('Wq', 'Wkv', 'Wc')}
    del _L1_xattn_all

    def _L1_ffn_setup():
        import jax, jax.numpy as jnp
        import numpy as np
        TOP_K = 2

        def gelu(x):
            return jax.nn.gelu(x, approximate=False)
        key = jax.random.key(seed)
        ks = jax.random.split(key, 6)
        B, L, D, H, E, S = (4, 512, 256, 512, 8, 2)
        sd = 0.02
        return {'x': jax.random.normal(ks[0], (B, L, D), dtype=jnp.float32), 'router_w': jax.random.normal(ks[1], (D, E), dtype=jnp.float32) * sd, 'router_b': jnp.zeros((E,), dtype=jnp.float32), 'w1': jax.random.normal(ks[2], (E, D, H), dtype=jnp.float32) * sd, 'b1': jnp.zeros((E, H), dtype=jnp.float32), 'w2': jax.random.normal(ks[3], (E, H, D), dtype=jnp.float32) * sd, 'b2': jnp.zeros((E, D), dtype=jnp.float32), 'sw1': jax.random.normal(ks[4], (S, D, H), dtype=jnp.float32) * sd, 'sb1': jnp.zeros((S, H), dtype=jnp.float32), 'sw2': jax.random.normal(ks[5], (S, H, D), dtype=jnp.float32) * sd, 'sb2': jnp.zeros((S, D), dtype=jnp.float32)}
    _L1_ffn_all = _L1_ffn_setup()
    _L1_ffn_in = {k: v for k, v in _L1_ffn_all.items() if k in ('router_w', 'router_b', 'w1', 'b1', 'w2', 'b2', 'sw1', 'sb1', 'sw2', 'sb2')}
    del _L1_ffn_all
    return {'x': x, 'ctx_1024': ctx_1024, 'g_xattn': g_xattn, 'g_ffn': g_ffn, 'L0_xattn_igate_w': _L0_xattn_in['igate_w'], 'L0_xattn_igate_b': _L0_xattn_in['igate_b'], 'L0_xattn_fgate_w': _L0_xattn_in['fgate_w'], 'L0_xattn_fgate_b': _L0_xattn_in['fgate_b'], 'L0_xattn_ln_scale': _L0_xattn_in['ln_scale'], 'L0_ffn_W_fc': _L0_ffn_in['W_fc'], 'L0_ffn_b_fc': _L0_ffn_in['b_fc'], 'L0_ffn_A_fc': _L0_ffn_in['A_fc'], 'L0_ffn_B_fc': _L0_ffn_in['B_fc'], 'L0_ffn_W_proj': _L0_ffn_in['W_proj'], 'L0_ffn_b_proj': _L0_ffn_in['b_proj'], 'L0_ffn_A_proj': _L0_ffn_in['A_proj'], 'L0_ffn_B_proj': _L0_ffn_in['B_proj'], 'L1_xattn_Wq': _L1_xattn_in['Wq'], 'L1_xattn_Wkv': _L1_xattn_in['Wkv'], 'L1_xattn_Wc': _L1_xattn_in['Wc'], 'L1_ffn_router_w': _L1_ffn_in['router_w'], 'L1_ffn_router_b': _L1_ffn_in['router_b'], 'L1_ffn_w1': _L1_ffn_in['w1'], 'L1_ffn_b1': _L1_ffn_in['b1'], 'L1_ffn_w2': _L1_ffn_in['w2'], 'L1_ffn_b2': _L1_ffn_in['b2'], 'L1_ffn_sw1': _L1_ffn_in['sw1'], 'L1_ffn_sb1': _L1_ffn_in['sb1'], 'L1_ffn_sw2': _L1_ffn_in['sw2'], 'L1_ffn_sb2': _L1_ffn_in['sb2']}

def reference(x, ctx_1024, g_xattn, g_ffn, L0_xattn_igate_w, L0_xattn_igate_b, L0_xattn_fgate_w, L0_xattn_fgate_b, L0_xattn_ln_scale, L0_ffn_W_fc, L0_ffn_b_fc, L0_ffn_A_fc, L0_ffn_B_fc, L0_ffn_W_proj, L0_ffn_b_proj, L0_ffn_A_proj, L0_ffn_B_proj, L1_xattn_Wq, L1_xattn_Wkv, L1_xattn_Wc, L1_ffn_router_w, L1_ffn_router_b, L1_ffn_w1, L1_ffn_b1, L1_ffn_w2, L1_ffn_b2, L1_ffn_sw1, L1_ffn_sb1, L1_ffn_sw2, L1_ffn_sb2):
    import jax
    import jax.numpy as jnp

    def _L0_xattn_ref(q, k, v, igate_w, igate_b, fgate_w, fgate_b, ln_scale):
        import jax, jax.numpy as jnp
        import numpy as np
        B, S, D, NH = (2, 512, 256, 8)
        DH = D // NH
        EPS = 1e-06
        LN_EPS = 1e-05

        def _mlstm_cell(q, k, v, igate_w, igate_b, fgate_w, fgate_b, ln_scale):
            Slen = q.shape[0]
            ifg = jnp.concatenate([q, k, v], axis=-1)
            ig = (ifg @ igate_w.T + igate_b).T
            fg = (ifg @ fgate_w.T + fgate_b).T
            qh = q.reshape(Slen, NH, DH).transpose(1, 0, 2)
            kh = k.reshape(Slen, NH, DH).transpose(1, 0, 2)
            vh = v.reshape(Slen, NH, DH).transpose(1, 0, 2)
            log_f = jax.nn.log_sigmoid(fg)
            cs = jnp.cumsum(log_f, axis=1)
            fg_mat = cs[:, :, None] - cs[:, None, :]
            mask = jnp.tril(jnp.ones((Slen, Slen), dtype=bool))
            log_fg_mat = jnp.where(mask, fg_mat, -jnp.inf)
            log_D = log_fg_mat + ig[:, None, :]
            max_log_D = jnp.max(log_D, axis=-1, keepdims=True)
            D_mat = jnp.exp(log_D - max_log_D)
            qk = jnp.einsum('hsd,htd->hst', qh, kh) / np.sqrt(DH)
            C = qk * D_mat
            normalizer = jnp.maximum(jnp.abs(C.sum(axis=-1, keepdims=True)), jnp.exp(-max_log_D))
            h = jnp.einsum('hst,htd->hsd', C / (normalizer + EPS), vh)
            h = h.transpose(1, 0, 2).reshape(Slen, D)
            mu = h.mean(axis=-1, keepdims=True)
            var = h.var(axis=-1, keepdims=True)
            return (h - mu) / jnp.sqrt(var + LN_EPS) * ln_scale
        return jax.vmap(lambda qq, kk, vv: _mlstm_cell(qq, kk, vv, igate_w, igate_b, fgate_w, fgate_b, ln_scale))(q, k, v)

    def _L0_ffn_ref(hidden_states, W_fc, b_fc, A_fc, B_fc, W_proj, b_proj, A_proj, B_proj):
        import jax, jax.numpy as jnp
        import numpy as np
        BITS = 8
        LORA_RANK = 16
        LORA_ALPHA = 32
        SCALING = LORA_ALPHA / LORA_RANK

        def fake_quant_weight(w, bits=BITS):
            qmax = 2.0 ** (bits - 1) - 1
            scale = jnp.max(jnp.abs(w)) / qmax
            wq = jnp.clip(jnp.round(w / scale), -qmax - 1, qmax) * scale
            return w + jax.lax.stop_gradient(wq - w)

        def qat_lora_linear(x, W, b, A, B):
            Wq = fake_quant_weight(W)
            base = jnp.einsum('bsi,oi->bso', x, Wq) + b
            lora = jnp.einsum('bsr,or->bso', jnp.einsum('bsi,ri->bsr', x, A), B)
            return base + SCALING * lora
        h = qat_lora_linear(hidden_states, W_fc, b_fc, A_fc, B_fc)
        h = jax.nn.gelu(h, approximate=False)
        h = qat_lora_linear(h, W_proj, b_proj, A_proj, B_proj)
        return h

    def _L1_xattn_ref(query, key_value, Wq, Wkv, Wc):
        import jax, jax.numpy as jnp
        import numpy as np
        HIDDEN = 256
        NUM_HEADS = 16
        HEAD_DIM = HIDDEN // NUM_HEADS
        B, S, H = query.shape
        T = key_value.shape[1]
        nh, hd = (NUM_HEADS, HEAD_DIM)
        q = query @ Wq
        kv = key_value @ Wkv
        k, v = (kv[..., :H], kv[..., H:])
        q = q.reshape(B, S, nh, hd).transpose(0, 2, 1, 3)
        k = k.reshape(B, T, nh, hd).transpose(0, 2, 1, 3)
        v = v.reshape(B, T, nh, hd).transpose(0, 2, 1, 3)
        scale = hd ** (-0.5)
        scores = jnp.einsum('bhsd,bhtd->bhst', q * scale, k)
        probs = jax.nn.softmax(scores, axis=-1)
        y = jnp.einsum('bhst,bhtd->bhsd', probs, v)
        y = y.transpose(0, 2, 1, 3).reshape(B, S, H)
        return y @ Wc

    def _L1_ffn_ref(x, router_w, router_b, w1, b1, w2, b2, sw1, sb1, sw2, sb2):
        import jax, jax.numpy as jnp
        import numpy as np
        TOP_K = 2

        def gelu(x):
            return jax.nn.gelu(x, approximate=False)
        B, L, D = x.shape
        E = router_b.shape[0]
        S = sw1.shape[0]
        xf = x.reshape(-1, D)
        sh = gelu(jnp.einsum('nd,sdh->snh', xf, sw1) + sb1[:, None, :])
        shared_out = (jnp.einsum('snh,shd->nd', sh, sw2) + sb2.sum(0)) / S
        gates = xf @ router_w + router_b
        topv, topi = jax.lax.top_k(gates, TOP_K)
        probs = jax.nn.softmax(topv, axis=-1)
        comb = jnp.einsum('nke,nk->ne', jax.nn.one_hot(topi, E, dtype=xf.dtype), probs)
        h = gelu(jnp.einsum('nd,edh->enh', xf, w1) + b1[:, None, :])
        y = jnp.einsum('enh,ehd->end', h, w2) + b2[:, None, :]
        moe_out = jnp.einsum('ne,end->nd', comb, y)
        return (shared_out + moe_out).reshape(B, L, D)
    x = x + jnp.tanh(g_xattn[0]) * _L0_xattn_ref(_layernorm(x, axis=-1), ctx_1024, ctx_1024, L0_xattn_igate_w, L0_xattn_igate_b, L0_xattn_fgate_w, L0_xattn_fgate_b, L0_xattn_ln_scale)
    x = x + jnp.tanh(g_ffn[0]) * _L0_ffn_ref(_layernorm(x, axis=-1), L0_ffn_W_fc, L0_ffn_b_fc, L0_ffn_A_fc, L0_ffn_B_fc, L0_ffn_W_proj, L0_ffn_b_proj, L0_ffn_A_proj, L0_ffn_B_proj)
    x = x + jnp.tanh(g_xattn[1]) * _L1_xattn_ref(_layernorm(x, axis=-1), ctx_1024, L1_xattn_Wq, L1_xattn_Wkv, L1_xattn_Wc)
    x = x + jnp.tanh(g_ffn[1]) * _L1_ffn_ref(_layernorm(x, axis=-1), L1_ffn_router_w, L1_ffn_router_b, L1_ffn_w1, L1_ffn_b1, L1_ffn_w2, L1_ffn_b2, L1_ffn_sw1, L1_ffn_sb1, L1_ffn_sw2, L1_ffn_sb2)
    return x

_drawn_inputs = setup_inputs


def setup_inputs(seed=0):
    import zlib

    import numpy as np

    out = dict(_drawn_inputs(seed))
    spreads = {'g_ffn': (-1.0, 0.6),
     'L0_xattn_ln_scale': (1.0, 0.2),
     'L0_ffn_b_fc': (0.0, 0.1),
     'L0_ffn_B_fc': (0.0, 0.1),
     'L0_ffn_b_proj': (0.0, 0.1),
     'L0_ffn_B_proj': (0.0, 0.1),
     'L1_ffn_router_b': (0.0, 0.304),
     'L1_ffn_b1': (0.0, 0.8),
     'L1_ffn_b2': (0.0, 0.1),
     'L1_ffn_sb1': (0.0, 0.8),
     'L1_ffn_sb2': (0.0, 0.1)}
    factors = {'L1_xattn_Wq': 38.701}
    for name, (base, spread) in spreads.items():
        noise = np.random.default_rng([zlib.crc32(name.encode()), seed]).standard_normal(out[name].shape)
        drawn = base * np.exp(spread * noise) if base else spread * noise
        out[name] = jnp.asarray(drawn.astype(out[name].dtype))
    for name, factor in factors.items():
        out[name] = (out[name] * factor).astype(out[name].dtype)
    return out
```

```python
from contextlib import ExitStack

import numpy as np
import concourse.bass as bass
from concourse import mybir
from concourse.alu_op_type import AluOpType as ALU

F32 = mybir.dt.float32
F32R = mybir.dt.float32r
BF16 = mybir.dt.bfloat16
ACT = mybir.ActivationFunctionType
AX = mybir.AxisListType
RMAX = bass.bass_isa.ReduceOp.max
P = 128
LN_EPS = 1e-5
MLSTM_EPS = 1e-6
ROUND = 1.5 * 2.0 ** 23
QMAX = 127.0


def three_passes(tensor, out, lhs, rhs, start, stop):
    (lhs_hi, lhs_lo), (rhs_hi, rhs_lo) = lhs, rhs
    tensor.matmul(out, lhs_hi, rhs_hi, start=start, stop=False)
    tensor.matmul(out, lhs_hi, rhs_lo, start=False, stop=False)
    return tensor.matmul(out, lhs_lo, rhs_hi, start=False, stop=stop)


def after(engine, semaphore, value):
    if not isinstance(value, int) or value > 0:
        engine.wait_ge(semaphore, value)


def alone(engine, semaphore, value, passed):
    if not isinstance(value, int) or value > 0:
        engine.wait_ge(semaphore, value)
        engine.sem_inc(passed, 1)


class Chain:

    def __init__(self, engine, semaphore, per, passed=None):
        self.engine, self.semaphore, self.per, self.passed = engine, semaphore, per, passed

    def begin(self, n):
        self.base, self.step = n * self.per, 0

    def __call__(self, instruction):
        self.step += 1
        assert self.step <= self.per
        instruction.then_inc(self.semaphore, 1)
        if self.passed is None:
            self.engine.wait_ge(self.semaphore, self.base + self.step)
        else:
            alone(self.engine, self.semaphore, self.base + self.step, self.passed)


def phase_setup(nc, x, gates, x_all, tanh_g, ident, half_neg):
    with ExitStack() as ctx:
        gate_raw = ctx.enter_context(nc.sbuf_tensor("gate_raw", [P, 4], F32))
        x_loaded = ctx.enter_context(nc.semaphore("x_loaded"))
        gates_loaded = ctx.enter_context(nc.semaphore("gates_loaded"))
        filled = ctx.enter_context(nc.semaphore("setup_filled"))
        tanh_done = ctx.enter_context(nc.semaphore("tanh_done"))
        block = ctx.enter_context(nc.Block())
        xv = x.rearrange("b (j p) d -> p (b j) d", p=P)

        @block.sync
        def _(sync):
            for c in range(4):
                sync.dma_start(x_all[:, 8 * c:8 * c + 8, :], xv[:, 8 * c:8 * c + 8, :]).then_inc(x_loaded, 16)
            sync.wait_ge(x_loaded, 64)

        @block.scalar
        def _(act):
            act.dma_start(gate_raw[:], gates.partition_broadcast(P)).then_inc(gates_loaded, 16)
            act.wait_ge(gates_loaded, 16)
            act.activation(tanh_g[:], gate_raw[:], ACT.Tanh).then_inc(tanh_done, 1)
            act.wait_ge(tanh_done, 1)

        @block.gpsimd
        def _(pool):
            pool.memset(half_neg[:], -0.5).then_inc(filled, 1)
            pool.memset(ident[:], 0.0).then_inc(filled, 1)
            pool.wait_ge(filled, 2)
            pool.affine_select(out=ident[:], in_=ident[:], compare_op=ALU.not_equal, fill=1.0, base=0,
                               pattern=[[-1, P]], channel_multiplier=1).then_inc(filled, 1)
            pool.wait_ge(filled, 3)


def phase_mlstm(nc, x_all, tanh_g, ident, half_neg, passed, ctx_in, ctx_t, gate_w, gate_b, ln_scale):
    B, S, D, H = 16, 256, 256, 8
    DH = D // H
    J = S // P
    LO = 32
    SCALE = float(DH) ** -0.5
    W = S + P
    R = 2
    with ExitStack() as ctx:
        def sb(name, shape, dt=F32):
            return ctx.enter_context(nc.sbuf_tensor("a_" + name, shape, dt))

        def sem(name):
            return ctx.enter_context(nc.semaphore("a_" + name))

        wg_raw, wg, gb = sb("wg_raw", [P, 6, 2 * H]), sb("wg", [P, 4, 2 * H]), sb("gb", [1, 2 * H])
        ln_s = sb("ln_s", [P, D])
        tri = sb("tri", [P, S])
        mask = sb("mask", [P, P], BF16)
        ident_b = sb("ident_b", [P, P], BF16)
        minus_i = sb("minus_i", [H, H])
        sel_raw = sb("sel_raw", [LO + H, H, P])
        sel = sb("sel", [LO + H, H, P], F32R)
        c_raw = [sb(f"c_raw{i}", [P, J, D]) for i in range(R)]
        kt = [sb(f"kt{i}", [P, J, S]) for i in range(R)]
        va = [sb(f"va{i}", [P, J, H, DH + 1]) for i in range(R)]
        qt = [sb(f"qt{i}", [P, J, S]) for i in range(R)]
        z = sb("z", [P, J, D])
        stats, mean_var, rstd = sb("stats", [P, J, 6]), sb("mean_var", [P, J, 2]), sb("rstd", [P, J])
        gsb = [sb(f"gsb{i}", [P, J, 2 * H]) for i in range(R)]
        fabs, fmin, lnt = sb("fabs", [P, J, H]), sb("fmin", [P, J, H]), sb("lnt", [P, J, H])
        a_row, m_row = sb("a_row", [H, S]), sb("m_row", [H, S])
        m_split = [sb(f"m_split{i}", [LO + H, S], F32R) for i in range(R)]
        a_tok = [sb(f"a_tok{i}", [P, J, H]) for i in range(R)]
        thr = [sb(f"thr{i}", [P, J, H]) for i in range(R)]
        decay = [sb(f"decay{i}", [P, W]) for i in range(R)]
        c_mat = [sb(f"c_mat{i}", [P, W]) for i in range(R)]
        nrm, rn = sb("nrm", [P, J, H]), sb("rn", [P, J, H])
        hn = sb("hn", [P, J, H, DH])
        h_stats, h_mv, h_rstd = sb("h_stats", [P, J, 6]), sb("h_mv", [P, J, 2]), sb("h_rstd", [P, J])
        hz = sb("hz", [P, J, D])
        qk = [ctx.enter_context(nc.psum_tensor(f"a_qk{i}", [P, 512], F32)) for i in range(R)]
        ex = [ctx.enter_context(nc.psum_tensor(f"a_ex{i}", [P, 512], F32)) for i in range(R)]
        hp = ctx.enter_context(nc.psum_tensor("a_hp", [P, J, 512], F32))
        tz = ctx.enter_context(nc.psum_tensor("a_tz", [P, J, S], F32))
        misc = ctx.enter_context(nc.psum_tensor("a_misc", [P, 512], F32))
        g_ps = misc[:, 0:J * 2 * H].rearrange("p (j g) -> p j g", j=J)
        row_ps = misc[0:H, 64:64 + S]
        tok_ps = misc[:, 384:384 + J * H].rearrange("p (j g) -> p j g", j=J)
        nm_ps = misc[:, 448:448 + J * H].rearrange("p (j g) -> p j g", j=J)
        hv = hp[:, :, 0:H * (DH + 1)].rearrange("p j (h d) -> p j h d", d=DH + 1)

        const_loaded, built, ready = sem("const_loaded"), sem("built"), sem("ready")
        c_loaded = [sem(f"c_loaded{i}") for i in range(R)]
        va_done = sem("va_done")
        stats_done, mv_done, var_eps, rstd_done = sem("stats_done"), sem("mv_done"), sem("var_eps"), sem("rstd_done")
        z_done, tz_done, qt_done = sem("z_done"), sem("tz_done"), sem("qt_done")
        gates_done, gates_read, fabs_done = sem("gates_done"), sem("gates_read"), sem("fabs_done")
        exp_done, ln_done, soft_done = sem("exp_done"), sem("ln_done"), sem("soft_done")
        cum_done, a_row_done, a_tok_done = sem("cum_done"), sem("a_row_done"), sem("a_tok_done")
        m_done, m_hi_done, m_split_done = sem("m_done"), sem("m_hi_done"), sem("m_split_done")
        nm_done, thr_done = sem("nm_done"), sem("thr_done")
        qk_done, decay_done, c_done, cv_done = sem("qk_done"), sem("decay_done"), sem("c_done"), sem("cv_done")
        post, hp_read, h_stats_done, h_mv_done = sem("post"), sem("hp_read"), sem("h_stats_done"), sem("h_mv_done")
        h_var_eps, h_rstd_done, hz_done = sem("h_var_eps"), sem("h_rstd_done"), sem("hz_done")
        scaled, x_done = sem("scaled"), sem("x_done")
        block = ctx.enter_context(nc.Block())
        cv = ctx_in.rearrange("b (j p) d -> b p j d", p=P)

        def all_batches(engine, body):
            body(0, 0)
            with engine.Fori(0, (B - 2) // 2) as i:
                for u in range(2):
                    body(2 * i + (1 + u), (1 + u) % 2)
            body(B - 1, (B - 1) % 2)

        def first(n):
            return isinstance(n, int) and n == 0

        def last(n):
            return isinstance(n, int) and n == B - 1

        @block.sync
        def _(sync):
            sync.dma_start(wg_raw[:], gate_w).then_inc(const_loaded, 16)
            sync.dma_start(gb[:], gate_b.rearrange("(a n) -> a n", a=1)).then_inc(const_loaded, 16)
            sync.dma_start(ln_s[:], ln_scale.partition_broadcast(P)).then_inc(const_loaded, 16)

            def load(n, u):
                if not (isinstance(n, int) and n < R):
                    sync.wait_ge(cv_done, (n - 1) * H)
                    sync.wait_ge(va_done, n - 1)
                sync.dma_start(kt[u][:], ctx_t[:, :, bass.ds(n * S, S)]).then_inc(c_loaded[u], 16)
                sync.dma_start(c_raw[u][:], cv[bass.ds(n, 1)].rearrange("b p j d -> p (b j) d")).then_inc(c_loaded[u], 16)

            load(0, 0)
            load(1, 1)
            with sync.Fori(0, (B - R) // 2) as i:
                for u in range(2):
                    load(2 * i + (2 + u), u)

        @block.gpsimd
        def _(pool):
            pool.memset(tri[:], 1.0).then_inc(built, 1)
            pool.memset(mask[:], 0.0).then_inc(built, 1)
            pool.memset(minus_i[:], 0.0).then_inc(built, 1)
            pool.memset(sel_raw[:], 0.0).then_inc(built, 1)
            for i in range(R):
                pool.memset(va[i][:, :, :, DH:DH + 1], 1.0).then_inc(built, 1)
                pool.memset(m_split[i][:].bitcast(F32), 0.0).then_inc(built, 1)
            pool.tensor_copy(ident_b[:], ident[:]).then_inc(built, 1)
            FILLS = 4 + 2 * R + 1
            pool.wait_ge(built, FILLS)
            pool.affine_select(out=tri[:], in_=tri[:], compare_op=ALU.is_ge, fill=0.0, base=0,
                               pattern=[[1, S]], channel_multiplier=-1).then_inc(built, 1)
            pool.affine_select(out=mask[:], in_=mask[:], compare_op=ALU.is_ge, fill=-1e30, base=0,
                               pattern=[[1, P]], channel_multiplier=-1).then_inc(built, 1)
            pool.affine_select(out=minus_i[:], in_=minus_i[:], compare_op=ALU.not_equal, fill=-1.0, base=0,
                               pattern=[[-1, H]], channel_multiplier=1).then_inc(built, 1)
            for k in range(2):
                pool.affine_select(out=sel_raw[:], in_=sel_raw[:], compare_op=ALU.not_equal, fill=-1.0, base=-LO * k,
                                   pattern=[[-1, H], [0, P]], channel_multiplier=1).then_inc(built, 1)
                pool.wait_ge(built, FILLS + 4 + k)

            def values(n, u, loads):
                pool.wait_ge(c_loaded[u], 32 * loads)
                alone(pool, cv_done, (n - 1) * H, passed)
                pool.tensor_copy(va[u][:, :, :, 0:DH], c_raw[u][:].rearrange("p j (h d) -> p j h d", d=DH)).then_inc(va_done, 1)

            def rstds(n):
                alone(pool, mv_done, J * n + J, passed)
                pool.tensor_scalar(rstd[:], mean_var[:, :, 1], LN_EPS, None, ALU.add).then_inc(var_eps, 1)
                pool.wait_ge(var_eps, n + 1)
                pool.tensor_tensor(rstd[:], rstd[:], half_neg[:, 0:J], ALU.pow).then_inc(rstd_done, 1)

            def h_rstds(n):
                alone(pool, h_mv_done, J * n + J, passed)
                pool.tensor_scalar(h_rstd[:], h_mv[:, :, 1], LN_EPS, None, ALU.add).then_inc(h_var_eps, 1)
                pool.wait_ge(h_var_eps, n + 1)
                pool.tensor_tensor(h_rstd[:], h_rstd[:], half_neg[:, 0:J], ALU.pow).then_inc(h_rstd_done, 1)

            def update_x(n):
                pool.wait_ge(hz_done, J * n + J)
                pool.wait_ge(ready, 2)
                for j in range(J):
                    pool.tensor_tensor(hz[:, j, :], hz[:, j, :], ln_s[:], ALU.mult).then_inc(scaled, 1)
                for j in range(J):
                    pool.wait_ge(scaled, J * n + j + 1)
                    xs = x_all[:, J * n + j, :]
                    pool.tensor_tensor(xs, xs, hz[:, j, :], ALU.add).then_inc(x_done, 1)

            rstds(0)
            values(0, 0, 1)

            def body(n, u, loads):
                if not last(n):
                    rstds(n + 1)
                if not first(n):
                    h_rstds(n - 1)
                if not last(n):
                    values(n + 1, 1 - u, loads)
                if not first(n):
                    update_x(n - 1)

            body(0, 0, 1)
            with pool.Fori(0, (B - 2) // 2) as i:
                for u in range(2):
                    body(2 * i + (1 + u), (1 + u) % 2, i + 2)
            body(B - 1, (B - 1) % 2, 0)
            h_rstds(B - 1)
            update_x(B - 1)
            pool.wait_ge(x_done, B * J)

        @block.scalar
        def _(act):
            def queries(n, u):
                act.wait_ge(tz_done, n + 1)
                after(act, cv_done, (n - 1) * H)
                act.activation(qt[u][:], tz[:], ACT.Copy).then_inc(qt_done, 1)

            def softplus(n):
                act.wait_ge(fabs_done, n + 1)
                act.activation(lnt[:], fabs[:], ACT.Exp, scale=-1.0).then_inc(exp_done, 1)
                act.wait_ge(exp_done, n + 1)
                act.activation(lnt[:], lnt[:], ACT.Ln, bias=1.0).then_inc(ln_done, 1)

            def rows(n):
                act.wait_ge(cum_done, n + 1)
                act.activation(a_row[:], row_ps, ACT.Copy).then_inc(a_row_done, 1)

            def thresholds(n, u):
                act.wait_ge(nm_done, n + 1)
                act.activation(thr[u][:], nm_ps, ACT.Exp).then_inc(thr_done, 1)

            def decays(n, u, h):
                act.wait_ge(qk_done, n * H + h + 1)
                after(act, c_done, n * H + h + 1 - R)
                act.activation(decay[h % R][:, 0:S], ex[h % R][:, 0:S], ACT.Exp,
                               bias=a_tok[u][:, 0, h:h + 1]).then_inc(decay_done, 1)
                act.activation(decay[h % R][:, S:W], ex[h % R][:, S:W], ACT.Exp,
                               bias=a_tok[u][:, 1, h:h + 1]).then_inc(decay_done, 1)

            queries(0, 0)
            softplus(0)
            rows(0)
            act.wait_ge(a_tok_done, 1)
            thresholds(0, 0)

            def body(n, u):
                act.wait_ge(a_tok_done, n + 1)
                for h in range(H):
                    decays(n, u, h)
                    if not last(n):
                        if h == 2:
                            queries(n + 1, 1 - u)
                        if h == 4:
                            softplus(n + 1)
                        if h == 6:
                            rows(n + 1)
                        if h == 7:
                            thresholds(n + 1, 1 - u)

            all_batches(act, body)

        @block.vector
        def _(dve):
            post_step = Chain(dve, post, 4)
            dve.wait_ge(const_loaded, 48)
            dve.tensor_copy(wg[:, 0:2, :], wg_raw[:, 0:2, :])
            dve.tensor_tensor(wg[:, 2:4, :], wg_raw[:, 2:4, :], wg_raw[:, 4:6, :], ALU.add).then_inc(ready, 1)
            dve.tensor_scalar(ln_s[:], ln_s[:], tanh_g[:, 0:1], None, ALU.mult).then_inc(ready, 1)
            dve.wait_ge(built, 14)
            dve.tensor_copy(sel[:], sel_raw[:]).then_inc(ready, 1)

            def stat(n):
                for j in range(J):
                    dve.bn_stats(stats[:, j, :], x_all[:, J * n + j, :]).then_inc(stats_done, 1)
                for j in range(J):
                    alone(dve, stats_done, J * n + j + 1, passed)
                    dve.bn_aggr(mean_var[:, j, :], stats[:, j, :]).then_inc(mv_done, 1)

            def norm(n):
                dve.wait_ge(rstd_done, n + 1)
                for j in range(J):
                    dve.tensor_scalar(z[:, j, :], x_all[:, J * n + j, :], mean_var[:, j, 0:1], rstd[:, j:j + 1],
                                      ALU.subtract, ALU.mult).then_inc(z_done, 1)

            def gates(n, u):
                dve.wait_ge(gates_done, n + 1)
                dve.tensor_copy(gsb[u][:], g_ps).then_inc(gates_read, 1)
                dve.wait_ge(gates_read, 2 * n + 1)
                f = gsb[u][:, :, H:2 * H]
                dve.tensor_scalar(fmin[:], f, 0.0, None, ALU.min).then_inc(gates_read, 1)
                dve.scalar_tensor_tensor(out=fabs[:], in0=f, scalar=-1.0, in1=f, op0=ALU.mult, op1=ALU.max).then_inc(fabs_done, 1)

            def soft(n, u):
                dve.wait_ge(ln_done, n + 1)
                dve.wait_ge(gates_read, 2 * n + 2)
                dve.tensor_tensor(gsb[u][:, :, H:2 * H], lnt[:], fmin[:], ALU.subtract).then_inc(soft_done, 1)

            def maxima(n, u):
                dve.wait_ge(cum_done, n + 1)
                dve.wait_ge(a_row_done, n + 1)
                dve.tensor_tensor(a_tok[u][:], tok_ps, gsb[u][:, :, 0:H], ALU.add).then_inc(a_tok_done, 1)
                dve.tensor_tensor_scan(m_row[:], a_row[:], a_row[:], -3e38, ALU.max, ALU.max).then_inc(m_done, 1)
                dve.wait_ge(m_done, n + 1)
                dve.tensor_copy(m_split[u][0:H, :], m_row[:]).then_inc(m_hi_done, 1)
                dve.wait_ge(m_hi_done, n + 1)
                dve.tensor_tensor(m_split[u][LO:LO + H, :], m_row[:], m_split[u][0:H, :], ALU.subtract).then_inc(m_split_done, 1)

            def weigh(n, h):
                dve.wait_ge(decay_done, 2 * (n * H + h) + 2)
                after(dve, cv_done, n * H + h + 1 - R)
                dve.scalar_tensor_tensor(out=c_mat[h % R][:], in0=qk[h % R][:, 0:W], scalar=SCALE, in1=decay[h % R][:],
                                         op0=ALU.mult, op1=ALU.mult).then_inc(c_done, 1)

            def normalise(n, u):
                post_step.begin(n)
                dve.wait_ge(cv_done, n * H + H)
                dve.wait_ge(thr_done, n + 1)
                for sign in (-1.0, 1.0):
                    post_step(dve.scalar_tensor_tensor(out=nrm[:], in0=hv[:, :, :, DH], scalar=sign,
                                                       in1=(thr[u] if sign < 0 else nrm)[:], op0=ALU.mult, op1=ALU.max))
                post_step(dve.tensor_scalar(nrm[:], nrm[:], MLSTM_EPS, None, ALU.add))
                post_step(dve.reciprocal(rn[:], nrm[:]))
                dve.tensor_tensor(hn[:], hv[:, :, :, 0:DH], rn[:].rearrange("p j (h a) -> p j h a", a=1).broadcast_to([P, J, H, DH]),
                                  ALU.mult).then_inc(hp_read, 1)

            def h_stat(n):
                dve.wait_ge(hp_read, n + 1)
                for j in range(J):
                    dve.bn_stats(h_stats[:, j, :], hn[:, j, :, :].rearrange("p h d -> p (h d)")).then_inc(h_stats_done, 1)
                for j in range(J):
                    alone(dve, h_stats_done, J * n + j + 1, passed)
                    dve.bn_aggr(h_mv[:, j, :], h_stats[:, j, :]).then_inc(h_mv_done, 1)

            def h_norm(n):
                dve.wait_ge(h_rstd_done, n + 1)
                after(dve, x_done, J * n)
                for j in range(J):
                    dve.tensor_scalar(hz[:, j, :], hn[:, j, :, :].rearrange("p h d -> p (h d)"), h_mv[:, j, 0:1],
                                      h_rstd[:, j:j + 1], ALU.subtract, ALU.mult).then_inc(hz_done, 1)

            stat(0)
            norm(0)
            gates(0, 0)
            soft(0, 0)
            maxima(0, 0)

            def body(n, u):
                for h in range(H):
                    weigh(n, h)
                    if not first(n):
                        if h == 0:
                            normalise(n - 1, 1 - u)
                        if h == 1:
                            h_stat(n - 1)
                        if h == 3:
                            h_norm(n - 1)
                    if not last(n):
                        if h == 0:
                            stat(n + 1)
                        if h == 2:
                            norm(n + 1)
                        if h == 4:
                            gates(n + 1, 1 - u)
                        if h == 5:
                            soft(n + 1, 1 - u)
                        if h == 7:
                            maxima(n + 1, 1 - u)

            all_batches(dve, body)
            normalise(B - 1, (B - 1) % 2)
            h_stat(B - 1)
            h_norm(B - 1)

        @block.tensor
        def _(pe):
            def transpose_z(n):
                pe.wait_ge(z_done, J * n + J)
                after(pe, qt_done, n)
                for c in range(J):
                    for j in range(J):
                        mm = pe.transpose(tz[:, c, j * P:(j + 1) * P], z[:, j, c * P:(c + 1) * P], ident[:])
                mm.then_inc(tz_done, 1)

            def gate_sums(n, u, loads):
                pe.wait_ge(qt_done, n + 1)
                pe.wait_ge(c_loaded[u], 32 * loads)
                after(pe, thr_done, n)
                for j in range(J):
                    cols = slice(j * P, (j + 1) * P)
                    for c in range(2):
                        pe.matmul(g_ps[:, j, :], qt[u][:, c, cols], wg[:, c, :], start=(c == 0), stop=False)
                    for c in range(2):
                        pe.matmul(g_ps[:, j, :], kt[u][:, c, cols], wg[:, 2 + c, :], start=False, stop=False)
                    mm = pe.matmul(g_ps[:, j, :], tri[0:1, P:S], gb[:], start=False, stop=True)
                mm.then_inc(gates_done, 1)

            def minus_cs(out, u, j, stop):
                soft = gsb[u]
                if j == 0:
                    return pe.matmul(out[:, 0, :], tri[:, 0:P], soft[:, 0, H:2 * H], start=True, stop=stop)
                pe.matmul(out[:, 1, :], tri[:, P:S], soft[:, 0, H:2 * H], start=True, stop=False)
                return pe.matmul(out[:, 1, :], tri[:, 0:P], soft[:, 1, H:2 * H], start=False, stop=stop)

            def cumulate(n, u):
                pe.wait_ge(soft_done, n + 1)
                g = gsb[u]
                pe.matmul(row_ps, g[:, 0, H:2 * H], tri[:], start=True, stop=False)
                pe.matmul(row_ps[:, P:S], g[:, 1, H:2 * H], tri[:, 0:P], start=False, stop=False)
                pe.matmul(row_ps[:, 0:P], g[:, 0, 0:H], ident[:], start=False, stop=False)
                pe.matmul(row_ps[:, P:S], g[:, 1, 0:H], ident[:], start=False, stop=True)
                minus_cs(tok_ps, u, 0, True)
                minus_cs(tok_ps, u, 1, True).then_inc(cum_done, 1)

            def minus_max(n, u):
                pe.wait_ge(m_split_done, n + 1)
                pe.wait_ge(a_tok_done, n + 1)
                for j in range(J):
                    minus_cs(nm_ps, u, j, False)
                    mm = pe.matmul(nm_ps[:, j, :], m_row[:, j * P:(j + 1) * P], minus_i[:], start=False, stop=True)
                mm.then_inc(nm_done, 1)

            def scores(n, u, h):
                after(pe, c_done, n * H + h + 1 - R)
                after(pe, decay_done, 2 * (n * H + h + 1 - R))
                rows, c = slice(DH * (h % 4), DH * (h % 4) + DH), h // 4
                q, k, s, e = qt[u], kt[u], qk[h % R], ex[h % R]
                pe.matmul(s[:, 0:S], k[rows, c, 0:P], q[rows, c, :], start=True, stop=True)
                pe.matmul(s[:, S:W], k[rows, c, P:S], q[rows, c, P:S], start=True, stop=True)
                pe.matmul(e[:, 0:S], sel[:, h, :], m_split[u][:], start=True, stop=True)
                pe.matmul(e[:, 0:P], ident_b[:], mask[:], start=False, stop=True, skip_group_check=True)
                pe.matmul(e[:, S:W], sel[:, h, :], m_split[u][:, P:S], start=False, stop=False, skip_group_check=True)
                pe.matmul(e[:, S:W], ident_b[:], mask[:], start=False, stop=True, skip_group_check=True).then_inc(qk_done, 1)

            def values(n, u, h):
                pe.wait_ge(c_done, n * H + h + 1)
                if h == 0:
                    after(pe, hp_read, n)
                    pe.wait_ge(va_done, n + 1)
                c = c_mat[h % R]
                pe.matmul(hv[:, 0, h, :], c[:, 0:P], va[u][:, 0, h, :], start=True, stop=True)
                pe.matmul(hv[:, 1, h, :], c[:, P:S], va[u][:, 0, h, :], start=True, stop=False)
                pe.matmul(hv[:, 1, h, :], c[:, S:W], va[u][:, 1, h, :], start=False, stop=True).then_inc(cv_done, 1)

            pe.wait_ge(ready, 3)
            pe.wait_ge(built, 14)
            transpose_z(0)
            gate_sums(0, 0, 1)
            cumulate(0, 0)
            minus_max(0, 0)

            def body(n, u, loads):
                for h in range(H + 1):
                    if h < H:
                        scores(n, u, h)
                    if h > 0:
                        values(n, u, h - 1)
                    if not last(n):
                        if h == 3:
                            transpose_z(n + 1)
                        if h == 4:
                            gate_sums(n + 1, 1 - u, loads)
                        if h == 6:
                            cumulate(n + 1, 1 - u)
                if not last(n):
                    minus_max(n + 1, 1 - u)

            body(0, 0, 1)
            with pe.Fori(0, (B - 2) // 2) as i:
                for u in range(2):
                    body(2 * i + (1 + u), (1 + u) % 2, i + 2)
            body(B - 1, (B - 1) % 2, 0)


def phase_lora_ffn(nc, x_all, tanh_g, ident, half_neg, passed, w_fc_t, b_fc, a_fc, b_fc_t, w_pr_t, b_pr, a_pr, b_pr_t):
    D, FF, R = 256, w_fc_t.shape[2], a_fc.shape[0]
    T = 4
    TOK = T * P
    CHUNKS = x_all.shape[1] // T
    KD, KF = D // P, FF // P
    HR = 4
    GR = 2
    EARLY = 6
    PIECE = 512
    with ExitStack() as ctx:
        def sb(name, shape, dt=F32):
            return ctx.enter_context(nc.sbuf_tensor("b_" + name, shape, dt))

        def sem(name):
            return ctx.enter_context(nc.semaphore("b_" + name))

        w1_hi, w1_lo = sb("w1_hi", [P, KD, FF], F32R), sb("w1_lo", [P, KD, FF], F32R)
        w2_hi, w2_lo = sb("w2_hi", [P, KF, D], F32R), sb("w2_lo", [P, KF, D], F32R)
        w1_raw, w2_raw = sb("w1_raw", [P, KD, FF]), sb("w2_raw", [P, KF, D])
        b1, b2 = sb("b1", [P, KF]), sb("b2", [P, D])
        a1, a2 = sb("a1", [R, D]), sb("a2", [R, FF])
        b1t, b2t = sb("b1t", [R, FF]), sb("b2t", [R, D])
        amax, amax_rows = sb("amax", [P, 2]), sb("amax_rows", [P, 2])
        scale, inv = sb("scale", [P, 2]), sb("inv", [P, 2])
        stats, mean_var = sb("stats", [P, T, 6]), sb("mean_var", [P, T, 2])
        rstd = sb("rstd", [P, T])
        z = sb("z", [P, T, D])
        zt_hi, zt_lo = sb("zt_hi", [P, KD, TOK], F32R), sb("zt_lo", [P, KD, TOK], F32R)
        g_full = sb("g_full", [P, GR, TOK])
        g_hi, g_lo = sb("g_hi", [P, KF, TOK], F32R), sb("g_lo", [P, KF, TOK], F32R)
        hid = [ctx.enter_context(nc.psum_tensor(f"b_hid{i}", [P, TOK], F32)) for i in range(HR)]
        zt = [ctx.enter_context(nc.psum_tensor(f"b_zt{i}", [P, TOK], F32)) for i in range(KD)]
        y = [ctx.enter_context(nc.psum_tensor(f"b_y{i}", [P, 2, D], F32)) for i in range(T // 2)]

        w_loaded, small_loaded = sem("w_loaded"), sem("small_loaded")
        amax_done, amax_all = sem("amax_done"), sem("amax_all")
        prep, lora_done, lora_used, w_ready = sem("prep"), sem("lora_done"), sem("lora_used"), sem("w_ready")
        stats_done, mv_done = sem("stats_done"), sem("mv_done")
        var_eps, rstd_done = sem("var_eps"), sem("rstd_done")
        z_done, zt_done, zt_hi_done, zt_lo_done = sem("z_done"), sem("zt_done"), sem("zt_hi_done"), sem("zt_lo_done")
        hid_done, gelu_full = sem("hid_done"), sem("gelu_full")
        gelu_hi = sem("gelu_hi")
        gelu_lo = sem("gelu_lo")
        y_done, x_added, x_biased = sem("y_done"), sem("x_added"), sem("x_biased")
        block = ctx.enter_context(nc.Block())

        @block.sync
        def _(sync):
            sync.dma_start(w1_raw[:], w_fc_t).then_inc(w_loaded, 16)
            sync.dma_start(w2_raw[:], w_pr_t).then_inc(w_loaded, 16)

        @block.scalar
        def _(act):
            for dst, src in ((a1, a_fc), (a2, a_pr), (b1t, b_fc_t), (b2t, b_pr_t), (b1, b_fc)):
                act.dma_start(dst[:], src).then_inc(small_loaded, 16)
            act.dma_start(b2[:], b_pr.partition_broadcast(P)).then_inc(small_loaded, 16)
            act.sem_inc(gelu_hi, HR)

            def split_zt(n):
                for c in range(KD):
                    act.wait_ge(zt_done, n * KD + c + 1)
                    act.activation(zt_hi[:, c, :], zt[c][:], ACT.Copy).then_inc(zt_hi_done, 1)

            def gelus(n):
                for m in range(KF):
                    act.wait_ge(hid_done, n * KF + m + 1)
                    act.wait_ge(gelu_lo, n * KF + m + 1)
                    act.activation(g_full[:, m % GR, :], hid[m % HR][:], ACT.Gelu,
                                   bias=b1[:, m:m + 1]).then_inc(gelu_full, 1)
                    act.activation(g_hi[:, m, :], hid[m % HR][:], ACT.Gelu,
                                   bias=b1[:, m:m + 1]).then_inc(gelu_hi, 1)

            split_zt(0)
            act.wait_ge(small_loaded, 96)
            with act.Fori(0, CHUNKS - 1) as n:
                gelus(n)
                split_zt(n + 1)
            gelus(CHUNKS - 1)

        @block.gpsimd
        def _(pool):
            def rstds(n):
                alone(pool, mv_done, n * T + T, passed)
                pool.tensor_scalar(rstd[:], mean_var[:, :, 1], LN_EPS, None, ALU.add).then_inc(var_eps, 1)
                pool.wait_ge(var_eps, n + 1)
                pool.tensor_tensor(rstd[:], rstd[:], half_neg[:, 0:T], ALU.pow).then_inc(rstd_done, 1)

            def bias_x(n):
                pool.wait_ge(z_done, n * T + T)
                for t in range(T):
                    xs = x_all[:, n * T + t, :]
                    pool.tensor_tensor(xs, xs, b2[:], ALU.add).then_inc(x_biased, 1)

            rstds(0)
            pool.wait_ge(amax_done, 2)
            pool.partition_all_reduce(amax[:], amax_rows[:], P, RMAX).then_inc(amax_all, 1)
            pool.wait_ge(w_ready, 1)
            bias_x(0)
            with pool.Fori(0, CHUNKS - 1) as n:
                rstds(n + 1)
                bias_x(n + 1)

        @block.vector
        def _(dve):
            steps = [0]

            def chain(ins):
                steps[0] += 1
                ins.then_inc(prep, 1)
                dve.wait_ge(prep, steps[0])

            def stat(n):
                for t in range(T):
                    dve.bn_stats(stats[:, t, :], x_all[:, n * T + t, :]).then_inc(stats_done, 1)
                for t in range(T):
                    alone(dve, stats_done, n * T + t + 1, passed)
                    dve.bn_aggr(mean_var[:, t, :], stats[:, t, :]).then_inc(mv_done, 1)

            def norm(n):
                dve.wait_ge(rstd_done, n + 1)
                for t in range(T):
                    dve.tensor_scalar(z[:, t, :], x_all[:, n * T + t, :], mean_var[:, t, 0:1], rstd[:, t:t + 1],
                                      ALU.subtract, ALU.mult).then_inc(z_done, 1)

            def split_zt(n):
                for c in range(KD):
                    dve.wait_ge(zt_hi_done, n * KD + c + 1)
                    dve.tensor_tensor(zt_lo[:, c, :], zt[c][:], zt_hi[:, c, :], ALU.subtract).then_inc(zt_lo_done, 1)

            def split_gelu(n):
                for m in range(KF):
                    dve.wait_ge(gelu_hi, HR + n * KF + m + 1)
                    dve.wait_ge(gelu_full, n * KF + m + 1)
                    dve.tensor_tensor(g_lo[:, m, :], g_full[:, m % GR, :], g_hi[:, m, :],
                                      ALU.subtract).then_inc(gelu_lo, 1)

            def add_x(n):
                for h in range(T // 2):
                    dve.wait_ge(y_done, n * (T // 2) + h + 1)
                    dve.wait_ge(x_biased, n * T + T)
                    xs = x_all[:, bass.ds(n * T + 2 * h, 2), :]
                    dve.tensor_tensor(xs, xs, y[h][:], ALU.add).then_inc(x_added, 1)

            dve.sem_inc(gelu_lo, GR)
            stat(0)
            dve.wait_ge(w_loaded, 32)
            for i, w in enumerate((w1_raw, w2_raw)):
                dve.tensor_reduce(amax_rows[:, i:i + 1], w[:].rearrange("p a b -> p (a b)"), AX.X, ALU.max,
                                  apply_absolute_value=True).then_inc(amax_done, 1)
            norm(0)
            dve.wait_ge(amax_all, 1)
            chain(dve.tensor_scalar(scale[:], amax[:], 1.0 / QMAX, None, ALU.mult))
            chain(dve.reciprocal(inv[:], scale[:]))
            dve.wait_ge(small_loaded, 96)
            chain(dve.tensor_scalar(b2[:], b2[:], tanh_g[:, 2:3], None, ALU.mult))
            for i, (w, hi, lo) in enumerate(((w1_raw, w1_hi, w1_lo), (w2_raw, w2_hi, w2_lo))):
                flat = w[:].rearrange("p a b -> p (a b)")
                chain(dve.tensor_scalar(flat, flat, inv[:, i:i + 1], ROUND, ALU.mult, ALU.add))
                chain(dve.tensor_scalar(flat, flat, -ROUND, QMAX, ALU.add, ALU.min))
                chain(dve.tensor_scalar(flat, flat, -QMAX - 1.0, scale[:, i:i + 1], ALU.max, ALU.mult))
                for q in range(4):
                    dve.wait_ge(lora_done, 4 * i + q + 1)
                    dst = flat[:, PIECE * q:PIECE * (q + 1)]
                    dve.scalar_tensor_tensor(out=dst, in0=hid[q][:], scalar=2.0, in1=dst,
                                             op0=ALU.mult, op1=ALU.add).then_inc(lora_used, 1)
                dve.wait_ge(lora_used, 4 * i + 4)
                if i == 1:
                    chain(dve.tensor_scalar(flat, flat, tanh_g[:, 2:3], None, ALU.mult))
                chain(dve.tensor_copy(hi[:], w[:]))
                dve.tensor_tensor(lo[:], w[:], hi[:], ALU.subtract).then_inc(w_ready, 1)
            split_zt(0)
            with dve.Fori(0, CHUNKS - 1) as n:
                stat(n + 1)
                norm(n + 1)
                split_gelu(n)
                split_zt(n + 1)
                add_x(n)
            split_gelu(CHUNKS - 1)
            add_x(CHUNKS - 1)
            dve.wait_ge(x_added, CHUNKS * T // 2)

        @block.tensor
        def _(pe):
            def transpose_z(n):
                pe.wait_ge(z_done, n * T + T)
                for c in range(KD):
                    for t in range(T):
                        mm = pe.transpose(zt[c][:, t * P:(t + 1) * P], z[:, t, c * P:(c + 1) * P], ident[:])
                    mm.then_inc(zt_done, 1)

            def lora_products(i):
                if i == 0:
                    pe.wait_ge(small_loaded, 96)
                for q in range(4):
                    if i == 1:
                        pe.wait_ge(lora_used, q + 1)
                    if i == 0:
                        c, cols = q // 2, slice(PIECE * (q % 2), PIECE * (q % 2 + 1))
                        mm = pe.matmul(hid[q][:], a1[:, c * P:(c + 1) * P], b1t[:, cols], start=True, stop=True)
                    else:
                        for k in range(2):
                            m = 2 * q + k
                            mm = pe.matmul(hid[q][:, D * k:D * (k + 1)], a2[:, m * P:(m + 1) * P], b2t[:],
                                           start=True, stop=True)
                    mm.then_inc(lora_done, 1)

            def hidden(n):
                pe.wait_ge(zt_lo_done, n * KD + KD)
                for m in range(KF):
                    pe.wait_ge(gelu_hi, n * KF + m + 1)
                    cols = slice(m * P, (m + 1) * P)
                    for c in range(KD):
                        mm = three_passes(pe, hid[m % HR][:], (w1_hi[:, c, cols], w1_lo[:, c, cols]),
                                          (zt_hi[:, c, :], zt_lo[:, c, :]), c == 0, c == KD - 1)
                    mm.then_inc(hid_done, 1)

            def outputs(n):
                def product(t, m):
                    cols = slice(t * P, (t + 1) * P)
                    return three_passes(pe, y[t // 2][:, t % 2, :], (g_hi[:, m, cols], g_lo[:, m, cols]),
                                        (w2_hi[:, m, :], w2_lo[:, m, :]), m == 0, m == KF - 1)

                pe.wait_ge(x_added, n * (T // 2))
                pe.wait_ge(gelu_lo, GR + n * KF + EARLY)
                for t in range(0, T, 2):
                    for m in range(EARLY):
                        product(t, m)
                pe.wait_ge(gelu_lo, GR + n * KF + KF)
                for t in range(T):
                    for m in range(0 if t % 2 else EARLY, KF):
                        mm = product(t, m)
                    if t % 2:
                        mm.then_inc(y_done, 1)

            lora_products(0)
            transpose_z(0)
            lora_products(1)
            pe.wait_ge(w_ready, 2)
            with pe.Fori(0, CHUNKS - 1) as n:
                hidden(n)
                transpose_z(n + 1)
                outputs(n)
            hidden(CHUNKS - 1)
            outputs(CHUNKS - 1)


def phase_attention(nc, x_all, tanh_g, ident, half_neg, passed, ctx_t, wq_in, wkv_in, wc_in):
    B, S, D, H = 16, 256, 256, 16
    DH = D // H
    J = S // P
    SLOT = 64
    PAIRS = H * SLOT // P
    K3 = 3 * DH
    SCALE = float(DH) ** -0.5
    OSLOT = 32
    GH = P // OSLOT
    R = 2
    PR, LAG = 4, 2
    FILLS = 2 * PAIRS * J // 4
    MAX_SLOTS = {s: (2 * (s - 4), 2 * (s - 4) + 1) for s in range(4, 10)} | {s: (s + 2,) for s in range(10, 14)}
    with ExitStack() as ctx:
        def sb(name, shape, dt=F32):
            return ctx.enter_context(nc.sbuf_tensor("c_" + name, shape, dt))

        def sem(name):
            return ctx.enter_context(nc.semaphore("c_" + name))

        w_raw = sb("w_raw", [P, 2, 4 * D])
        w_hi, w_lo = sb("w_hi", [P, 2, 4 * D], F32R), sb("w_lo", [P, 2, 4 * D], F32R)
        sel_raw = sb("sel_raw", [2 * H, H, P])
        sel = sb("sel", [2 * H, H, P], F32R)
        c_raw = [sb(f"c_raw{i}", [P, 2, S]) for i in range(R)]
        ct_hi, ct_lo = sb("ct_hi", [P, 2, S], F32R), sb("ct_lo", [P, 2, S], F32R)
        stats, mean_var, rstd = sb("stats", [P, J, 6]), sb("mean_var", [P, J, 2]), sb("rstd", [P, J])
        z = sb("z", [P, J, D])
        zt_hi, zt_lo = sb("zt_hi", [P, 2, S], F32R), sb("zt_lo", [P, 2, S], F32R)
        q3, k3 = sb("q3", [P, J * H, SLOT], F32R), sb("k3", [P, J * H, SLOT], F32R)
        v_tmp = sb("v_tmp", [P, J, D])
        va = [sb(f"va{i}", [P, J, H, OSLOT]) for i in range(R)]
        qt = [sb(f"qt{i}", [P, PAIRS, S], F32R) for i in range(R)]
        kt = [sb(f"kt{i}", [P, PAIRS, S], F32R) for i in range(R)]
        mx = sb("mx", [P, J, H])
        m_tok = sb("m_tok", [P, J, 2 * H], F32R)
        m_row = [sb(f"m_row{i}", [2 * H, S], F32R) for i in range(R)]
        probs = [sb(f"probs{i}", [P, J, S]) for i in range(PR)]
        ot = sb("ot", [P, 2, 2, S])
        rden = sb("rden", [P, J, H])
        yn = sb("yn", [P, J, H, DH])
        yt_hi, yt_lo = sb("yt_hi", [P, 2, S], F32R), sb("yt_lo", [P, 2, S], F32R)

        def pb(name, shape):
            return ctx.enter_context(nc.psum_tensor("c_" + name, shape, F32))

        s_ps = [pb(f"s{i}", [P, J, S]) for i in range(R)]
        t_ps = [pb(f"t{i}", [P, J, S]) for i in range(R)]
        o_ps = [pb(f"o{i}", [P, 2, S]) for i in range(2)]
        even, odd = pb("even", [P, 2, S]), pb("odd", [P, 2, S])

        w_loaded, w_ready, prep, built = sem("w_loaded"), sem("w_ready"), sem("prep"), sem("built")
        c_loaded = [sem(f"c_loaded{i}") for i in range(R)]
        ct_hi_done, ct_lo_done = sem("ct_hi_done"), sem("ct_lo_done")
        stats_done, mv_done, var_eps, rstd_done = sem("stats_done"), sem("mv_done"), sem("var_eps"), sem("rstd_done")
        z_done, zt_done, zt_hi_done, zt_lo_done = sem("z_done"), sem("zt_done"), sem("zt_hi_done"), sem("zt_lo_done")
        q_done, q_hi_done, q_lo_done = sem("q_done"), sem("q_hi_done"), sem("q_lo_done")
        kv_done, k_hi_done, v_done, k_lo_done = sem("kv_done"), sem("k_hi_done"), sem("v_done"), sem("k_lo_done")
        va_done = sem("va_done")
        turned, turned_read = sem("turned"), sem("turned_read")
        s_done, max_done, m_hi_done, m_tok_done = sem("s_done"), sem("max_done"), sem("m_hi_done"), sem("m_tok_done")
        m_turned, m_row_done = sem("m_turned"), sem("m_row_done")
        t_done, exp_done, pv_done = sem("t_done"), sem("exp_done"), sem("pv_done")
        rden_done, y_done, yt_done, yt_hi_done, yt_lo_done = sem("rden_done"), sem("y_done"), sem("yt_done"), sem("yt_hi_done"), sem("yt_lo_done")
        ot_done, o_turned = sem("ot_done"), sem("o_turned")
        out_done, x_done = sem("out_done"), sem("x_done")
        block = ctx.enter_context(nc.Block())

        def all_batches(engine, body):
            body(0, 0)
            with engine.Fori(0, (B - 4) // 2) as i:
                for u in range(2):
                    body(2 * i + (1 + u), (1 + u) % 2)
            for n in range(B - 3, B):
                body(n, n % 2)

        def has(n, least=None, below=None):
            return not isinstance(n, int) or ((least is None or n >= least) and (below is None or n < below))

        @block.sync
        def _(sync):
            sync.dma_start(w_raw[:, :, 0:D], wq_in).then_inc(w_loaded, 16)
            sync.dma_start(w_raw[:, :, D:3 * D], wkv_in).then_inc(w_loaded, 16)
            sync.dma_start(w_raw[:, :, 3 * D:4 * D], wc_in).then_inc(w_loaded, 16)

            def load(n, u):
                if not (isinstance(n, int) and n < R):
                    sync.wait_ge(ct_lo_done, n - 1)
                sync.dma_start(c_raw[u][:], ctx_t[:, :, bass.ds(n * S, S)]).then_inc(c_loaded[u], 16)

            load(0, 0)
            load(1, 1)
            with sync.Fori(0, (B - R) // 2) as i:
                for u in range(2):
                    load(2 * i + (2 + u), u)

        @block.gpsimd
        def _(pool):
            pool.memset(sel_raw[:], 0.0).then_inc(built, 1)
            pool.memset(q3[:].bitcast(F32), 0.0).then_inc(built, 1)
            pool.memset(k3[:].bitcast(F32), 0.0).then_inc(built, 1)
            for i in range(R):
                pool.memset(va[i][:], 0.0).then_inc(built, 1)
            pool.wait_ge(built, 5)
            for i in range(R):
                pool.memset(va[i][:, :, :, DH:DH + 1], 1.0).then_inc(built, 1)
            for k in range(2):
                pool.wait_ge(built, 7 + k)
                pool.affine_select(out=sel_raw[:], in_=sel_raw[:], compare_op=ALU.not_equal, fill=-1.0, base=-H * k,
                                   pattern=[[-1, H], [0, P]], channel_multiplier=1).then_inc(built, 1)

            def split_context(n, u, loads):
                pool.wait_ge(c_loaded[u], 16 * loads)
                alone(pool, kv_done, J * n, passed)
                pool.tensor_copy(ct_hi[:], c_raw[u][:]).then_inc(ct_hi_done, 1)
                pool.wait_ge(ct_hi_done, n + 1)
                pool.tensor_tensor(ct_lo[:], c_raw[u][:], ct_hi[:], ALU.subtract).then_inc(ct_lo_done, 1)

            def rstds(n):
                alone(pool, mv_done, J * n + J, passed)
                pool.tensor_scalar(rstd[:], mean_var[:, :, 1], LN_EPS, None, ALU.add).then_inc(var_eps, 1)
                pool.wait_ge(var_eps, n + 1)
                pool.tensor_tensor(rstd[:], rstd[:], half_neg[:, 0:J], ALU.pow).then_inc(rstd_done, 1)

            def values(n, u):
                pool.wait_ge(v_done, J * n + J)
                alone(pool, pv_done, (n - 1) * H, passed)
                pool.tensor_copy(va[u][:, :, :, 0:DH], v_tmp[:].rearrange("p j (h d) -> p j h d", d=DH)).then_inc(va_done, 1)

            split_context(0, 0, 1)
            rstds(0)
            values(0, 0)
            rstds(1)
            split_context(1, 1, 1)

            def body(n, u, loads):
                if has(n, below=B - 1):
                    values(n + 1, 1 - u)
                if has(n, below=B - 2):
                    rstds(n + 2)
                    split_context(n + 2, u, loads)

            body(0, 0, 2)
            with pool.Fori(0, (B - 4) // 2) as i:
                for u in range(2):
                    body(2 * i + (1 + u), (1 + u) % 2, i + (2 + u))
            for n in range(B - 3, B):
                body(n, n % 2, n // 2 + 2)

        @block.scalar
        def _(act):
            def split_zt(n):
                act.wait_ge(zt_done, n + 1)
                act.activation(zt_hi[:], even[:], ACT.Copy).then_inc(zt_hi_done, 1)

            def three_rows(t3, tiles, at, src, scale):
                out = t3[:, tiles, 0:K3].rearrange("p h (r d) -> p h r d", r=3)[:, :, at, :]
                n = src.shape[1] // DH
                src = src.rearrange("p (h a d) -> p h a d", a=1, d=DH).broadcast_to([P, n, 2, DH])
                return act.activation(out, src, ACT.Copy, scale=scale)

            def split_q(n):
                act.wait_ge(q_done, n + 1)
                three_rows(q3, slice(0, J * H), slice(0, 2), odd[:].rearrange("p j d -> p (j d)"), SCALE).then_inc(q_hi_done, 1)

            def split_kv(n, j):
                act.wait_ge(kv_done, J * n + j + 1)
                after(act, va_done, n)
                bank = (even, odd)[j]
                three_rows(k3, slice(j * H, (j + 1) * H), slice(0, 3, 2), bank[:, 0, :], 1.0).then_inc(k_hi_done, 1)
                act.activation(v_tmp[:, j, :], bank[:, 1, :], ACT.Copy).then_inc(v_done, 1)

            def read_turned(n, u, f):
                act.wait_ge(turned, FILLS * n + f + 1)
                after(act, pv_done, (n - 1) * H)
                g = f // 2
                dst = (qt, kt)[f % 2][u]
                act.activation(dst[:, 2 * g:2 * g + 2, :], (even, odd)[f % 2][:], ACT.Copy).then_inc(turned_read, 1)

            def max_rows(n, u):
                act.wait_ge(m_turned, n + 1)
                act.activation(m_row[u][:], even[0:2 * H, 0, :], ACT.Copy).then_inc(m_row_done, 1)

            def exps(n, u, h):
                act.wait_ge(t_done, n * H + h + 1)
                after(act, pv_done, n * H + h + 1 - PR)
                act.activation(probs[h % PR][:], t_ps[h % R][:], ACT.Exp).then_inc(exp_done, 1)

            def read_outputs(n, f):
                act.wait_ge(pv_done, n * H + (f + 1) * H // 2)
                after(act, o_turned, 2 * (n - 1) + f + 1)
                act.activation(ot[:, f], o_ps[f][:], ACT.Copy).then_inc(ot_done, 1)

            def split_yt(n):
                act.wait_ge(yt_done, n + 1)
                act.activation(yt_hi[:], even[:], ACT.Copy).then_inc(yt_hi_done, 1)

            act.wait_ge(built, 9)
            for n in range(2):
                split_zt(n)
                split_q(n)
                for j in range(J):
                    split_kv(n, j)
                if n == 0:
                    for f in range(FILLS):
                        read_turned(0, 0, f)
            max_rows(0, 0)

            def body(n, u):
                for h in range(H):
                    exps(n, u, h)
                    if has(n, below=B - 1) and h < FILLS // 2:
                        read_turned(n + 1, 1 - u, 2 * h)
                        read_turned(n + 1, 1 - u, 2 * h + 1)
                    if has(n, least=1):
                        if h == 2:
                            read_outputs(n - 1, 1)
                        if h == 7:
                            split_yt(n - 1)
                    if h == 11:
                        read_outputs(n, 0)
                    if has(n, below=B - 2):
                        if h == 9:
                            split_zt(n + 2)
                        if h == 11:
                            split_q(n + 2)
                        if h in (12, 13):
                            split_kv(n + 2, h - 12)
                    if has(n, below=B - 1) and h == 15:
                        max_rows(n + 1, 1 - u)

            all_batches(act, body)
            read_outputs(B - 1, 1)
            split_yt(B - 1)

        @block.vector
        def _(dve):
            dve.wait_ge(w_loaded, 48)
            dve.tensor_scalar(w_raw[:, :, 3 * D:], w_raw[:, :, 3 * D:], tanh_g[:, 1:2], None, ALU.mult).then_inc(prep, 1)
            dve.wait_ge(prep, 1)
            dve.tensor_copy(w_hi[:], w_raw[:]).then_inc(prep, 1)
            dve.wait_ge(prep, 2)
            dve.tensor_tensor(w_lo[:], w_raw[:], w_hi[:], ALU.subtract).then_inc(w_ready, 1)
            dve.wait_ge(built, 9)
            dve.tensor_copy(sel[:], sel_raw[:]).then_inc(w_ready, 1)

            def stat(n):
                for j in range(J):
                    dve.bn_stats(stats[:, j, :], x_all[:, J * n + j, :]).then_inc(stats_done, 1)
                for j in range(J):
                    alone(dve, stats_done, J * n + j + 1, passed)
                    dve.bn_aggr(mean_var[:, j, :], stats[:, j, :]).then_inc(mv_done, 1)

            def norm(n):
                dve.wait_ge(rstd_done, n + 1)
                for j in range(J):
                    dve.tensor_scalar(z[:, j, :], x_all[:, J * n + j, :], mean_var[:, j, 0:1], rstd[:, j:j + 1],
                                      ALU.subtract, ALU.mult).then_inc(z_done, 1)

            def split_zt(n):
                dve.wait_ge(zt_hi_done, n + 1)
                dve.tensor_tensor(zt_lo[:], even[:], zt_hi[:], ALU.subtract).then_inc(zt_lo_done, 1)

            def split_q(n):
                dve.wait_ge(q_hi_done, n + 1)
                dve.scalar_tensor_tensor(out=q3[:, :, 2 * DH:K3], in0=odd[:].rearrange("p j (h d) -> p (j h) d", d=DH),
                                         scalar=SCALE, in1=q3[:, :, 0:DH], op0=ALU.mult, op1=ALU.subtract).then_inc(q_lo_done, 1)

            def split_kv(n, j):
                dve.wait_ge(k_hi_done, J * n + j + 1)
                dve.wait_ge(v_done, J * n + j + 1)
                t = slice(j * H, (j + 1) * H)
                dve.tensor_tensor(k3[:, t, DH:2 * DH], (even, odd)[j][:, 0, :].rearrange("p (h d) -> p h d", d=DH),
                                  k3[:, t, 0:DH], ALU.subtract).then_inc(k_lo_done, 1)

            def maximum(n, h):
                dve.wait_ge(s_done, n * H + h + 1)
                dve.tensor_reduce(mx[:, :, h:h + 1], s_ps[h % R][:], AX.X, ALU.max).then_inc(max_done, 1)

            def split_max(n):
                dve.wait_ge(max_done, n * H + H)
                dve.tensor_copy(m_tok[:, :, 0:H], mx[:]).then_inc(m_hi_done, 1)
                dve.wait_ge(m_hi_done, n + 1)
                dve.tensor_tensor(m_tok[:, :, H:], mx[:], m_tok[:, :, 0:H], ALU.subtract).then_inc(m_tok_done, 1)

            def normalise(n, f):
                dve.wait_ge(o_turned, 2 * n + f + 1)
                bank = (even, odd)[f][:].rearrange("p a (j g d) -> p a j g d", j=J, g=GH)
                for j in range(J):
                    r = rden[:, j, f * H // 2:(f + 1) * H // 2].rearrange("p (a g) -> p a g", a=2)
                    dve.reciprocal(r, bank[:, :, j, :, DH]).then_inc(rden_done, 1)
                for j in range(J):
                    dve.wait_ge(rden_done, (2 * n + f) * J + j + 1)
                    r = rden[:, j, f * H // 2:(f + 1) * H // 2].rearrange("p (a g x) -> p a g x", a=2, x=1)
                    out = yn[:, j, f * H // 2:(f + 1) * H // 2, :].rearrange("p (a g) d -> p a g d", a=2)
                    dve.tensor_tensor(out, bank[:, :, j, :, 0:DH], r.broadcast_to([P, 2, GH, DH]), ALU.mult).then_inc(y_done, 1)

            def split_yt(n):
                dve.wait_ge(yt_hi_done, n + 1)
                dve.tensor_tensor(yt_lo[:], even[:], yt_hi[:], ALU.subtract).then_inc(yt_lo_done, 1)

            def add_x(n):
                dve.wait_ge(out_done, n + 1)
                xs = x_all[:, bass.ds(J * n, J), :]
                dve.tensor_tensor(xs, xs, odd[:], ALU.add).then_inc(x_done, 1)

            stat(0)
            norm(0)
            for n in range(2):
                split_zt(n)
                split_q(n)
                for j in range(J):
                    split_kv(n, j)
                if n == 0:
                    stat(1)
                    norm(1)
            for h in range(H):
                maximum(0, h)
            split_max(0)

            def body(n, u):
                for h in range(H):
                    if has(n, below=B - 2):
                        if h == 0:
                            stat(n + 2)
                        if h == 2:
                            norm(n + 2)
                    if has(n, below=B - 1):
                        for k in MAX_SLOTS.get(h, ()):
                            maximum(n + 1, k)
                        if h == 14:
                            split_max(n + 1)
                    if has(n, least=1):
                        if h == 4:
                            normalise(n - 1, 0)
                            normalise(n - 1, 1)
                        if h == 7:
                            split_yt(n - 1)
                        if h == 8:
                            add_x(n - 1)
                    if has(n, below=B - 2):
                        if h == 9:
                            split_zt(n + 2)
                        if h == 11:
                            split_q(n + 2)
                        if h in (12, 13):
                            split_kv(n + 2, h - 12)

            all_batches(dve, body)
            normalise(B - 1, 0)
            normalise(B - 1, 1)
            split_yt(B - 1)
            add_x(B - 1)
            dve.wait_ge(x_done, B)

        @block.tensor
        def _(pe):
            def banks_free(n, kinds):
                for s, v in kinds:
                    after(pe, s, v)

            def transpose_z(n):
                pe.wait_ge(z_done, J * n + J)
                after(pe, turned_read, FILLS * n)
                after(pe, yt_lo_done, n - 2)
                after(pe, m_row_done, n - 1)
                for c in range(2):
                    for j in range(J):
                        mm = pe.transpose(even[:, c, j * P:(j + 1) * P], z[:, j, c * P:(c + 1) * P], ident[:])
                mm.then_inc(zt_done, 1)

            def project_q(n):
                pe.wait_ge(zt_lo_done, n + 1)
                after(pe, turned_read, FILLS * n)
                after(pe, x_done, n - 2)
                for j in range(J):
                    cols = slice(j * P, (j + 1) * P)
                    for c in range(2):
                        mm = three_passes(pe, odd[:, j, :], (zt_hi[:, c, cols], zt_lo[:, c, cols]),
                                          (w_hi[:, c, 0:D], w_lo[:, c, 0:D]), c == 0, c == 1)
                mm.then_inc(q_done, 1)

            def project_kv(n, j):
                bank = (even, odd)[j]
                pe.wait_ge(ct_lo_done, n + 1)
                if j == 0:
                    pe.wait_ge(zt_lo_done, n + 1)
                else:
                    pe.wait_ge(q_lo_done, n + 1)
                cols = slice(j * P, (j + 1) * P)
                for c in range(2):
                    mm = three_passes(pe, bank[:].rearrange("p j d -> p (j d)"), (ct_hi[:, c, cols], ct_lo[:, c, cols]),
                                      (w_hi[:, c, D:3 * D], w_lo[:, c, D:3 * D]), c == 0, c == 1)
                mm.then_inc(kv_done, 1)

            def turn(n, f):
                if f == 0:
                    pe.wait_ge(q_lo_done, n + 1)
                    pe.wait_ge(k_lo_done, J * n + J)
                    after(pe, m_row_done, n)
                else:
                    after(pe, turned_read, FILLS * n + f - 1)
                g = f // 2
                src, bank = (q3, k3)[f % 2], (even, odd)[f % 2]
                for a in range(2):
                    for j in range(J):
                        h = j * H + 2 * (2 * g + a)
                        mm = pe.transpose(bank[:, a, j * P:(j + 1) * P],
                                          src[:, h:h + 2, :].rearrange("p h r -> p (h r)").bitcast(F32), ident[:])
                mm.then_inc(turned, 1)

            def scores(n, u, h):
                after(pe, max_done, n * H + h + 1 - R)
                pe.wait_ge(turned_read, FILLS * n + 2 * (h // 4) + 2)
                rows, pair = slice(SLOT * (h % 2), SLOT * (h % 2) + K3), h // 2
                for j in range(J):
                    mm = pe.matmul(s_ps[h % R][:, j, :], qt[u][rows, pair, j * P:(j + 1) * P], kt[u][rows, pair, :],
                                   start=True, stop=True)
                mm.then_inc(s_done, 1)

            def turn_max(n):
                pe.wait_ge(m_tok_done, n + 1)
                pe.wait_ge(turned_read, FILLS * n + FILLS)
                after(pe, yt_lo_done, n - 1)
                pe.wait_ge(k_lo_done, min(J * n + 2 * J, J * B) if isinstance(n, int) else J * n + 2 * J)
                for j in range(J):
                    mm = pe.transpose(even[0:2 * H, 0, j * P:(j + 1) * P], m_tok[:, j, :].bitcast(F32), ident[:])
                mm.then_inc(m_turned, 1)

            def shifted_scores(n, u, h):
                after(pe, exp_done, n * H + h + 1 - R)
                if h == 0:
                    pe.wait_ge(m_row_done, n + 1)
                rows, pair = slice(SLOT * (h % 2), SLOT * (h % 2) + K3), h // 2
                for i in range(J):
                    pe.matmul(t_ps[h % R][:, i, :], kt[u][rows, pair, i * P:(i + 1) * P], qt[u][rows, pair, :],
                              start=True, stop=False)
                    mm = pe.matmul(t_ps[h % R][:, i, :], sel[:, h, :], m_row[u][:], start=False, stop=True)
                mm.then_inc(t_done, 1)

            def weigh_values(n, u, h):
                pe.wait_ge(exp_done, n * H + h + 1)
                if h == 0:
                    pe.wait_ge(va_done, n + 1)
                if h % (H // 2) == 0:
                    after(pe, ot_done, 2 * (n - 1) + 2 * h // H + 1)
                out = o_ps[2 * h // H][OSLOT * (h % GH):OSLOT * (h % GH + 1), h // GH % 2, :]
                for i in range(J):
                    mm = pe.matmul(out, va[u][:, i, h, :], probs[h % PR][:, i, :], start=(i == 0), stop=(i == J - 1))
                mm.then_inc(pv_done, 1)

            def turn_outputs(n, f):
                pe.wait_ge(ot_done, 2 * n + f + 1)
                pe.wait_ge(turned_read, min(FILLS * (n + 3), FILLS * B) if isinstance(n, int) else FILLS * (n + 3))
                pe.wait_ge(m_row_done, min(n + 2, B) if isinstance(n, int) else n + 2)
                pe.wait_ge(k_lo_done, min(J * (n + 3), J * B) if isinstance(n, int) else J * (n + 3))
                after(pe, (yt_lo_done, x_done)[f], n)
                for a in range(2):
                    for j in range(J):
                        mm = pe.transpose((even, odd)[f][:, a, j * P:(j + 1) * P], ot[:, f, a, j * P:(j + 1) * P], ident[:])
                mm.then_inc(o_turned, 1)

            def transpose_y(n):
                pe.wait_ge(y_done, 2 * J * n + 2 * J)
                for c in range(2):
                    for j in range(J):
                        mm = pe.transpose(even[:, c, j * P:(j + 1) * P],
                                          yn[:, j].rearrange("p h d -> p (h d)")[:, c * P:(c + 1) * P], ident[:])
                mm.then_inc(yt_done, 1)

            def project_out(n):
                pe.wait_ge(yt_lo_done, n + 1)
                for j in range(J):
                    cols = slice(j * P, (j + 1) * P)
                    for c in range(2):
                        mm = three_passes(pe, odd[:, j, :], (yt_hi[:, c, cols], yt_lo[:, c, cols]),
                                          (w_hi[:, c, 3 * D:], w_lo[:, c, 3 * D:]), c == 0, c == 1)
                mm.then_inc(out_done, 1)

            pe.wait_ge(w_ready, 2)
            for n in range(2):
                transpose_z(n)
                project_q(n)
                for j in range(J):
                    project_kv(n, j)
                if n == 0:
                    for f in range(FILLS):
                        turn(0, f)
            for h in range(H):
                scores(0, 0, h)
            turn_max(0)

            def body(n, u):
                for h in range(H):
                    shifted_scores(n, u, h)
                    if h >= LAG:
                        weigh_values(n, u, h - LAG)
                    elif has(n, least=1):
                        weigh_values(n - 1, 1 - u, H - LAG + h)
                    if has(n, below=B - 1):
                        if h < FILLS // 2:
                            turn(n + 1, 2 * h)
                            turn(n + 1, 2 * h + 1)
                        for k in MAX_SLOTS.get(h, ()):
                            scores(n + 1, 1 - u, k)
                    if has(n, least=1):
                        if h == 4:
                            turn_outputs(n - 1, 0)
                            turn_outputs(n - 1, 1)
                        if h == 6:
                            transpose_y(n - 1)
                        if h == 8:
                            project_out(n - 1)
                    if has(n, below=B - 2):
                        if h == 8:
                            transpose_z(n + 2)
                        if h == 10:
                            project_q(n + 2)
                        if h in (11, 12):
                            project_kv(n + 2, h - 11)
                    if has(n, below=B - 1) and h == 15:
                        turn_max(n + 1)

            all_batches(pe, body)
            for h in range(H - LAG, H):
                weigh_values(B - 1, (B - 1) % R, h)
            turn_outputs(B - 1, 0)
            turn_outputs(B - 1, 1)
            transpose_y(B - 1)
            project_out(B - 1)


def phase_moe(nc, x_all, tanh_g, ident, half_neg, passed, router_w, router_b, w1_in, b1_in, w2_in, b2_in):
    D, E, NE = 256, router_w.shape[2], w1_in.shape[0]
    FF = w1_in.shape[3]
    T = 4
    TOK = T * P
    TILES = x_all.shape[1]
    CHUNKS = TILES // T
    KD, KF = D // P, FF // P
    SHARED = NE - E
    HR, GR = 2, 2
    with ExitStack() as ctx:
        def sb(name, shape, dt=F32):
            return ctx.enter_context(nc.sbuf_tensor("d_" + name, shape, dt))

        def sem(name):
            return ctx.enter_context(nc.semaphore("d_" + name))

        zt_hi, zt_lo = sb("zt_hi", [P, KD, TILES * P], F32R), sb("zt_lo", [P, KD, TILES * P], F32R)
        zs_hi, zs_lo = sb("zs_hi", [P, KD, P], F32R), sb("zs_lo", [P, KD, P], F32R)
        rw_raw = sb("rw_raw", [P, KD, E])
        rw_hi, rw_lo = sb("rw_hi", [P, KD, E], F32R), sb("rw_lo", [P, KD, E], F32R)
        rb = sb("rb", [P, E])
        b1, b2 = sb("b1", [P, NE, KF]), sb("b2", [NE, D])
        expert = sb("expert", [P, E])
        comb = sb("comb", [P, TILES, NE])
        comb_s = sb("comb_s", [P, NE])
        comb_t = sb("comb_t", [NE, P])
        stats, mean_var, rstd = sb("stats", [P, 6]), sb("mean_var", [P, 2]), sb("rstd", [P, 1])
        z = sb("z", [P, D])
        gates, top, top_i = sb("gates", [P, E]), sb("top", [P, 8]), sb("top_i", [P, 8], mybir.dt.uint32)
        top_f, diff, expd, den, prob = sb("top_f", [P, 2]), sb("diff", [P, 1]), sb("expd", [P, 1]), sb("den", [P, 1]), sb("prob", [P, 2])
        pick = sb("pick", [P, 2, E])
        w1_raw, w2_raw = [sb(f"w1_raw{i}", [P, KD, FF]) for i in range(2)], [sb(f"w2_raw{i}", [P, KF, D]) for i in range(2)]
        w1_hi, w1_lo = [sb(f"w1_hi{i}", [P, KD, FF], F32R) for i in range(2)], [sb(f"w1_lo{i}", [P, KD, FF], F32R) for i in range(2)]
        w2_hi, w2_lo = [sb(f"w2_hi{i}", [P, KF, D], F32R) for i in range(2)], [sb(f"w2_lo{i}", [P, KF, D], F32R) for i in range(2)]
        g_full = sb("g_full", [P, GR, TOK])
        g_hi, g_lo = [sb(f"g_hi{i}", [P, KF, TOK], F32R) for i in range(2)], [sb(f"g_lo{i}", [P, KF, TOK], F32R) for i in range(2)]
        hid = [ctx.enter_context(nc.psum_tensor(f"d_hid{i}", [P, TOK], F32)) for i in range(HR)]
        y = [ctx.enter_context(nc.psum_tensor(f"d_y{i}", [P, D], F32)) for i in range(T)]
        zt_ps = ctx.enter_context(nc.psum_tensor("d_zt_ps", [P, KD, P], F32))
        r_ps = ctx.enter_context(nc.psum_tensor("d_r_ps", [P, 512], F32))

        small_loaded, ready, route = sem("small_loaded"), sem("ready"), sem("route")
        w_loaded = [sem(f"w_loaded{i}") for i in range(2)]
        w_hi_done, w_lo_done = sem("w_hi_done"), sem("w_lo_done")
        stats_done, mv_done, var_eps, rstd_done = sem("stats_done"), sem("mv_done"), sem("var_eps"), sem("rstd_done")
        z_done, zt_done, zs_hi_done, zs_lo_done = sem("z_done"), sem("zt_done"), sem("zs_hi_done"), sem("zs_lo_done")
        zt_copied, comb_kept = sem("zt_copied"), sem("comb_kept")
        gates_done, diff_done, exp_done, comb_done = sem("gates_done"), sem("diff_done"), sem("exp_done"), sem("comb_done")
        comb_turned, comb_t_done, bias_done, bias_added = sem("comb_turned"), sem("comb_t_done"), sem("bias_done"), sem("bias_added")
        hid_done, gelu_full = sem("hid_done"), sem("gelu_full")
        gelu_hi = sem("gelu_hi")
        gelu_lo = sem("gelu_lo")
        y_done = sem("y_done")
        x_added = sem("x_added")
        block = ctx.enter_context(nc.Block())

        def all_steps(engine, hidden, outputs, start=None):
            def expert_steps(e, u):
                if start:
                    start(e, u)
                hidden(e, 0, u, 0)
                if not (isinstance(e, int) and e == 0):
                    outputs(e - 1, CHUNKS - 1, 1 - u, 1)
                with engine.Fori(0, (CHUNKS - 2) // 2) as j:
                    for v in (1, 0):
                        hidden(e, 2 * j + (2 - v), u, v)
                        outputs(e, 2 * j + (1 - v), u, 1 - v)
                hidden(e, CHUNKS - 1, u, 1)
                outputs(e, CHUNKS - 2, u, 0)

            expert_steps(0, 0)
            with engine.Fori(0, (NE - 2) // 2) as i:
                for u in (1, 0):
                    expert_steps(2 * i + (2 - u), u)
            expert_steps(NE - 1, 1)
            outputs(NE - 1, CHUNKS - 1, 1, 1)

        @block.sync
        def _(sync):
            for dst, src in ((rw_raw, router_w), (b1, b1_in), (b2, b2_in)):
                sync.dma_start(dst[:], src).then_inc(small_loaded, 16)
            sync.dma_start(rb[:], router_b.partition_broadcast(P)).then_inc(small_loaded, 16)

            def load(e, u):
                if not (isinstance(e, int) and e < 2):
                    sync.wait_ge(w_lo_done, 2 * (e - 1))
                sync.dma_start(w1_raw[u][:], w1_in[bass.ds(e, 1)].rearrange("e p k f -> p (e k) f")).then_inc(w_loaded[u], 16)
                sync.dma_start(w2_raw[u][:], w2_in[bass.ds(e, 1)].rearrange("e p k f -> p (e k) f")).then_inc(w_loaded[u], 16)

            load(0, 0)
            load(1, 1)
            with sync.Fori(0, (NE - 2) // 2) as i:
                for u in range(2):
                    load(2 * i + (2 + u), u)

        @block.gpsimd
        def _(pool):
            pool.iota(expert[:], pattern=[[1, E]], base=0, channel_multiplier=0, allow_small_or_imprecise_dtypes=True).then_inc(ready, 1)
            with pool.Fori(0, TILES) as t:
                alone(pool, mv_done, t + 1, passed)
                pool.tensor_scalar(rstd[:], mean_var[:, 1:2], LN_EPS, None, ALU.add).then_inc(var_eps, 1)
                pool.wait_ge(var_eps, t + 1)
                pool.tensor_tensor(rstd[:], rstd[:], half_neg[:, 0:1], ALU.pow).then_inc(rstd_done, 1)

            def split(e, u, loads):
                pool.wait_ge(w_loaded[u], 32 * loads)
                alone(pool, y_done, (e - 1) * TILES, passed)
                for raw, hi, lo in ((w1_raw, w1_hi, w1_lo), (w2_raw, w2_hi, w2_lo)):
                    pool.tensor_copy(hi[u][:], raw[u][:]).then_inc(w_hi_done, 1)
                for k, (raw, hi, lo) in enumerate(((w1_raw, w1_hi, w1_lo), (w2_raw, w2_hi, w2_lo))):
                    pool.wait_ge(w_hi_done, 2 * e + k + 1)
                    pool.tensor_tensor(lo[u][:], raw[u][:], hi[u][:], ALU.subtract).then_inc(w_lo_done, 1)

            split(0, 0, 1)
            split(1, 1, 1)
            with pool.Fori(0, (NE - 2) // 2) as i:
                for u in range(2):
                    split(2 * i + (2 + u), u, i + 2)

        @block.scalar
        def _(act):
            act.sem_inc(gelu_hi, HR)
            with act.Fori(0, TILES) as t:
                act.wait_ge(zt_done, t + 1)
                act.activation(zs_hi[:], zt_ps[:], ACT.Copy).then_inc(zs_hi_done, 1)
                act.wait_ge(diff_done, t + 1)
                act.activation(expd[:], diff[:], ACT.Exp).then_inc(exp_done, 1)
                act.wait_ge(comb_turned, t + 1)
                act.activation(comb_t[:], r_ps[0:NE, 64:64 + P], ACT.Copy).then_inc(comb_t_done, 1)
            act.wait_ge(small_loaded, 64)

            def hidden(e, n, u, v):
                for m in range(KF):
                    step = (e * CHUNKS + n) * KF + m + 1
                    act.wait_ge(hid_done, step)
                    alone(act, gelu_lo, step, passed)
                    bias = b1[:, bass.ds(e, 1), m:m + 1].rearrange("p e m -> p (e m)")
                    act.activation(g_full[:, m % GR, :], hid[m % HR][:], ACT.Gelu, bias=bias).then_inc(gelu_full, 1)
                    act.activation(g_hi[v][:, m, :], hid[m % HR][:], ACT.Gelu, bias=bias).then_inc(gelu_hi, 1)

            all_steps(act, hidden, lambda e, n, u, v: None)

        @block.vector
        def _(dve):
            dve.sem_inc(gelu_lo, GR)
            dve.sem_inc(x_added, T)
            dve.wait_ge(small_loaded, 64)
            dve.tensor_copy(rw_hi[:], rw_raw[:]).then_inc(ready, 1)
            dve.memset(comb_s[:, E:NE], 1.0 / SHARED).then_inc(ready, 1)
            dve.wait_ge(ready, 3)
            dve.tensor_tensor(rw_lo[:], rw_raw[:], rw_hi[:], ALU.subtract).then_inc(ready, 1)
            dve.tensor_scalar(comb_s[:, E:NE], comb_s[:, E:NE], tanh_g[:, 3:4], None, ALU.mult).then_inc(ready, 1)
            dve.wait_ge(ready, 5)
            step = Chain(dve, route, 9, passed)

            with dve.Fori(0, TILES) as t:
                step.begin(t)
                dve.bn_stats(stats[:], x_all[:, t, :]).then_inc(stats_done, 1)
                alone(dve, stats_done, t + 1, passed)
                dve.bn_aggr(mean_var[:], stats[:]).then_inc(mv_done, 1)
                dve.wait_ge(rstd_done, t + 1)
                dve.tensor_scalar(z[:], x_all[:, t, :], mean_var[:, 0:1], rstd[:, 0:1], ALU.subtract, ALU.mult).then_inc(z_done, 1)
                dve.wait_ge(zs_hi_done, t + 1)
                dve.tensor_tensor(zs_lo[:], zt_ps[:], zs_hi[:], ALU.subtract).then_inc(zs_lo_done, 1)
                dve.tensor_copy(zt_hi[:, :, bass.ds(t * P, P)], zs_hi[:]).then_inc(zt_copied, 1)
                dve.wait_ge(zs_lo_done, t + 1)
                dve.tensor_copy(zt_lo[:, :, bass.ds(t * P, P)], zs_lo[:]).then_inc(zt_copied, 1)
                dve.wait_ge(gates_done, t + 1)
                step(dve.tensor_tensor(gates[:], r_ps[:, 0:E], rb[:], ALU.add))
                step(dve.max(top[:], gates[:]))
                step(dve.max_index(top_i[:], top[:], gates[:]))
                dve.tensor_tensor(diff[:], top[:, 1:2], top[:, 0:1], ALU.subtract).then_inc(diff_done, 1)
                step(dve.tensor_copy(top_f[:], top_i[:, 0:2]))
                for k in range(2):
                    ins = dve.tensor_scalar(pick[:, k, :], expert[:], top_f[:, k:k + 1], tanh_g[:, 3:4], ALU.is_equal, ALU.mult)
                step(ins)
                dve.wait_ge(exp_done, t + 1)
                step(dve.tensor_scalar(den[:], expd[:], 1.0, None, ALU.add))
                step(dve.reciprocal(prob[:, 0:1], den[:]))
                step(dve.tensor_tensor(prob[:, 1:2], prob[:, 0:1], expd[:], ALU.mult))
                step(dve.tensor_scalar(pick[:, 0, :], pick[:, 0, :], prob[:, 0:1], None, ALU.mult))
                dve.scalar_tensor_tensor(out=comb_s[:, 0:E], in0=pick[:, 1, :], scalar=prob[:, 1:2], in1=pick[:, 0, :],
                                         op0=ALU.mult, op1=ALU.add).then_inc(comb_done, 1)
                dve.wait_ge(comb_done, t + 1)
                dve.tensor_copy(comb[:, bass.ds(t, 1), :].rearrange("p t e -> p (t e)"), comb_s[:]).then_inc(comb_kept, 1)
                dve.wait_ge(bias_done, t + 1)
                dve.tensor_tensor(x_all[:, t, :], x_all[:, t, :], r_ps[:, 256:512], ALU.add).then_inc(bias_added, 1)
            dve.wait_ge(bias_added, TILES)
            dve.wait_ge(comb_kept, TILES)

            def hidden(e, n, u, v):
                for m in range(KF):
                    step = (e * CHUNKS + n) * KF + m + 1
                    dve.wait_ge(gelu_hi, HR + step)
                    dve.wait_ge(gelu_full, step)
                    dve.tensor_tensor(g_lo[v][:, m, :], g_full[:, m % GR, :], g_hi[v][:, m, :], ALU.subtract).then_inc(gelu_lo, 1)

            def outputs(e, n, u, v):
                for t in range(T):
                    dve.wait_ge(y_done, (e * CHUNKS + n) * T + t + 1)
                    xs = x_all[:, n * T + t, :]
                    w = comb[:, n * T + t, bass.ds(e, 1)]
                    dve.scalar_tensor_tensor(out=xs, in0=y[t][:], scalar=w, in1=xs, op0=ALU.mult, op1=ALU.add).then_inc(x_added, 1)

            all_steps(dve, hidden, outputs)
            dve.wait_ge(x_added, T + NE * TILES)

        @block.tensor
        def _(pe):
            pe.wait_ge(ready, 5)
            with pe.Fori(0, TILES) as t:
                pe.wait_ge(z_done, t + 1)
                for c in range(KD):
                    mm = pe.transpose(zt_ps[:, c, :], z[:, c * P:(c + 1) * P], ident[:])
                mm.then_inc(zt_done, 1)
                pe.wait_ge(zs_lo_done, t + 1)
                for c in range(KD):
                    mm = three_passes(pe, r_ps[:, 0:E], (zs_hi[:, c, :], zs_lo[:, c, :]), (rw_hi[:, c, :], rw_lo[:, c, :]),
                                      c == 0, c == KD - 1)
                mm.then_inc(gates_done, 1)
                pe.wait_ge(comb_done, t + 1)
                pe.transpose(r_ps[0:NE, 64:64 + P], comb_s[:], ident[:]).then_inc(comb_turned, 1)
                pe.wait_ge(comb_t_done, t + 1)
                pe.matmul(r_ps[:, 256:512], comb_t[:], b2[:], start=True, stop=True).then_inc(bias_done, 1)

            pe.wait_ge(zt_copied, 2 * TILES)

            def start(e, u):
                pe.wait_ge(w_lo_done, 2 * e + 2)

            def hidden(e, n, u, v):
                for m in range(KF):
                    pe.wait_ge(gelu_hi, (e * CHUNKS + n) * KF + m + 1)
                    cols = slice(m * P, (m + 1) * P)
                    toks = bass.ds(n * TOK, TOK)
                    for c in range(KD):
                        mm = three_passes(pe, hid[m % HR][:], (w1_hi[u][:, c, cols], w1_lo[u][:, c, cols]),
                                          (zt_hi[:, c, toks], zt_lo[:, c, toks]), c == 0, c == KD - 1)
                    mm.then_inc(hid_done, 1)

            def outputs(e, n, u, v):
                pe.wait_ge(gelu_lo, GR + (e * CHUNKS + n + 1) * KF)
                for t in range(T):
                    pe.wait_ge(x_added, (e * CHUNKS + n) * T + t + 1)
                    cols = slice(t * P, (t + 1) * P)
                    for m in range(KF):
                        mm = three_passes(pe, y[t][:], (g_hi[v][:, m, cols], g_lo[v][:, m, cols]),
                                          (w2_hi[u][:, m, :], w2_lo[u][:, m, :]), m == 0, m == KF - 1)
                    mm.then_inc(y_done, 1)

            all_steps(pe, hidden, outputs, start)


def phase_store(nc, x_all, out):
    with ExitStack() as ctx:
        stored = ctx.enter_context(nc.semaphore("stored"))
        block = ctx.enter_context(nc.Block())
        ov = out.rearrange("b (j p) d -> p (b j) d", p=P)

        @block.sync
        def _(sync):
            for c in range(4):
                sync.dma_start(ov[:, 8 * c:8 * c + 8, :], x_all[:, 8 * c:8 * c + 8, :]).then_inc(stored, 16)
            sync.wait_ge(stored, 64)


def flamingo_kernel(nc, t, out, phases="ABCD"):
    with ExitStack() as ctx:
        x_all = ctx.enter_context(nc.sbuf_tensor("x_all", [P, 32, 256], F32))
        tanh_g = ctx.enter_context(nc.sbuf_tensor("tanh_g", [P, 4], F32))
        ident = ctx.enter_context(nc.sbuf_tensor("ident", [P, P], F32))
        half_neg = ctx.enter_context(nc.sbuf_tensor("half_neg", [P, 8], F32))
        passed = ctx.enter_context(nc.semaphore("passed"))
        common = (nc, x_all, tanh_g, ident, half_neg, passed)
        phase_setup(nc, t["x"], t["gates"], x_all, tanh_g, ident, half_neg)
        if "A" in phases:
            phase_mlstm(*common, t["ctx"], t["ctx_t"], t["gate_w"], t["gate_b"], t["ln_scale"])
        if "B" in phases:
            phase_lora_ffn(*common, t["w_fc_t"], t["b_fc"], t["a_fc"], t["b_fc_t"], t["w_pr_t"], t["b_pr"], t["a_pr"],
                           t["b_pr_t"])
        if "C" in phases:
            phase_attention(*common, t["ctx_t"], t["wq"], t["wkv"], t["wc"])
        if "D" in phases:
            phase_moe(*common, t["router_w"], t["router_b"], t["w1"], t["b1"], t["w2"], t["b2"])
        phase_store(nc, x_all, out)


def blocks_first(a):
    return a.reshape(-1, P, a.shape[-1]).transpose(1, 0, 2)


def lay_out(v):
    a = {k: np.asarray(i) for k, i in v.items()}
    ctx = a["ctx_1024"]
    t = {
        "x": a["x"],
        "gates": np.concatenate([a["g_xattn"], a["g_ffn"]]),
        "ctx": ctx,
        "ctx_t": ctx.reshape(-1, 2, P).transpose(2, 1, 0),
        "gate_w": blocks_first(np.concatenate([a["L0_xattn_igate_w"], a["L0_xattn_fgate_w"]]).T),
        "gate_b": np.concatenate([a["L0_xattn_igate_b"], a["L0_xattn_fgate_b"]]),
        "ln_scale": a["L0_xattn_ln_scale"],
        "w_fc_t": blocks_first(a["L0_ffn_W_fc"].T),
        "b_fc": a["L0_ffn_b_fc"].reshape(-1, P).T,
        "a_fc": a["L0_ffn_A_fc"],
        "b_fc_t": a["L0_ffn_B_fc"].T,
        "w_pr_t": blocks_first(a["L0_ffn_W_proj"].T),
        "b_pr": a["L0_ffn_b_proj"],
        "a_pr": a["L0_ffn_A_proj"],
        "b_pr_t": a["L0_ffn_B_proj"].T,
        "wq": blocks_first(a["L1_xattn_Wq"]),
        "wkv": blocks_first(a["L1_xattn_Wkv"]),
        "wc": blocks_first(a["L1_xattn_Wc"]),
        "router_w": blocks_first(a["L1_ffn_router_w"]),
        "router_b": a["L1_ffn_router_b"],
        "w1": np.concatenate([a["L1_ffn_w1"], a["L1_ffn_sw1"]]).reshape(10, 2, P, 512).transpose(0, 2, 1, 3),
        "b1": np.concatenate([a["L1_ffn_b1"], a["L1_ffn_sb1"]]).reshape(10, 4, P).transpose(2, 0, 1),
        "w2": np.concatenate([a["L1_ffn_w2"], a["L1_ffn_sw2"]]).reshape(10, 4, P, 256).transpose(0, 2, 1, 3),
        "b2": np.concatenate([a["L1_ffn_b2"], a["L1_ffn_sb2"]]),
    }
    return {k: np.ascontiguousarray(i) for k, i in t.items()}


def build(nc, t, phases="ABCD"):
    aps = {k: nc.dram_tensor(f"in_{k}", i.shape, F32, kind="ExternalInput").ap() for k, i in t.items()}
    out = nc.dram_tensor("out_x", t["x"].shape, F32, kind="ExternalOutput").ap()
    flamingo_kernel(nc, aps, out, phases)


def kernel(**inputs):
    import concourse.bacc as bacc
    from concourse.bass_utils import run_bass_kernel_spmd

    nc = bacc.Bacc("TRN2", target_bir_lowering=False, num_devices=1)
    t = lay_out(inputs)
    build(nc, t)
    result = run_bass_kernel_spmd(nc, [{f"in_{k}": i for k, i in t.items()}], core_ids=[0])
    return result.results[0]["out_x"]
```

```python
from contextlib import ExitStack

import numpy as np
import concourse.bass as bass
from concourse import mybir
from concourse.alu_op_type import AluOpType as ALU

F32 = mybir.dt.float32
F32R = mybir.dt.float32r
BF16 = mybir.dt.bfloat16
ACT = mybir.ActivationFunctionType
AX = mybir.AxisListType
RMAX = bass.bass_isa.ReduceOp.max
P = 128
LN_EPS = 1e-5
MLSTM_EPS = 1e-6
ROUND = 1.5 * 2.0 ** 23
QMAX = 127.0


def three_passes(tensor, out, lhs, rhs, start, stop):
    (lhs_hi, lhs_lo), (rhs_hi, rhs_lo) = lhs, rhs
    tensor.matmul(out, lhs_hi, rhs_hi, start=start, stop=False)
    tensor.matmul(out, lhs_hi, rhs_lo, start=False, stop=False)
    return tensor.matmul(out, lhs_lo, rhs_hi, start=False, stop=stop)


def after(engine, semaphore, value):
    if not isinstance(value, int) or value > 0:
        engine.wait_ge(semaphore, value)


def alone(engine, semaphore, value, passed):
    if not isinstance(value, int) or value > 0:
        engine.wait_ge(semaphore, value)
        engine.sem_inc(passed, 1)


def cleared_semaphores(nc, ctx, prefix):
    used = []
    ctx.callback(nc.all_engine_barrier)
    ctx.callback(nc.clear_and_free_semaphores, used)

    def semaphore(name):
        used.append(nc.alloc_semaphore(prefix + name))
        return used[-1]

    return semaphore


class Chain:

    def __init__(self, engine, semaphore, per, passed=None):
        self.engine, self.semaphore, self.per, self.passed = engine, semaphore, per, passed

    def begin(self, n):
        self.base, self.step = n * self.per, 0

    def __call__(self, instruction):
        self.step += 1
        assert self.step <= self.per
        instruction.then_inc(self.semaphore, 1)
        if self.passed is None:
            self.engine.wait_ge(self.semaphore, self.base + self.step)
        else:
            alone(self.engine, self.semaphore, self.base + self.step, self.passed)


def phase_setup(nc, x, gates, x_all, tanh_g, ident, half_neg):
    with ExitStack() as ctx:
        sem = cleared_semaphores(nc, ctx, "setup_")
        gate_raw = ctx.enter_context(nc.sbuf_tensor("gate_raw", [P, 4], F32))
        x_loaded = sem("x_loaded")
        gates_loaded = sem("gates_loaded")
        filled = sem("filled")
        tanh_done = sem("tanh_done")
        block = ctx.enter_context(nc.Block())
        xv = x.rearrange("b (j p) d -> p (b j) d", p=P)

        @block.sync
        def _(sync):
            for c in range(4):
                sync.dma_start(x_all[:, 8 * c:8 * c + 8, :], xv[:, 8 * c:8 * c + 8, :]).then_inc(x_loaded, 16)
            sync.wait_ge(x_loaded, 64)

        @block.scalar
        def _(act):
            act.dma_start(gate_raw[:], gates.partition_broadcast(P)).then_inc(gates_loaded, 16)
            act.wait_ge(gates_loaded, 16)
            act.activation(tanh_g[:], gate_raw[:], ACT.Tanh).then_inc(tanh_done, 1)
            act.wait_ge(tanh_done, 1)

        @block.gpsimd
        def _(pool):
            pool.memset(half_neg[:], -0.5).then_inc(filled, 1)
            pool.memset(ident[:], 0.0).then_inc(filled, 1)
            pool.wait_ge(filled, 2)
            pool.affine_select(out=ident[:], in_=ident[:], compare_op=ALU.not_equal, fill=1.0, base=0,
                               pattern=[[-1, P]], channel_multiplier=1).then_inc(filled, 1)
            pool.wait_ge(filled, 3)


def phase_mlstm(nc, x_all, tanh_g, ident, half_neg, passed, ctx_in, ctx_t, gate_w, gate_b, ln_scale):
    B, S, D, H = 16, 256, 256, 8
    DH = D // H
    J = S // P
    LO = 32
    SCALE = float(DH) ** -0.5
    W = S + P
    R = 2
    SLOT = 2 * DH
    GROUPS = H * SLOT // P
    GH = H // GROUPS
    ROWS = LO + H
    with ExitStack() as ctx:
        def sb(name, shape, dt=F32):
            return ctx.enter_context(nc.sbuf_tensor("a_" + name, shape, dt))

        sem = cleared_semaphores(nc, ctx, "a_")

        wg_raw, wg = sb("wg_raw", [P, 6, 2 * H]), sb("wg", [P, 4, ROWS])
        gb = sb("gb", [ROWS, 1])
        ln_s = sb("ln_s", [P, D])
        mask = sb("mask", [P, P], BF16)
        ident_b = sb("ident_b", [P, P], BF16)
        zero_row = sb("zero_row", [H, S])
        sel_raw = sb("sel_raw", [LO + H, H, P])
        sel = sb("sel", [LO + H, H, P], F32R)
        c_raw = [sb(f"c_raw{i}", [P, J, D]) for i in range(R)]
        kt = [sb(f"kt{i}", [P, J, S]) for i in range(R)]
        va = [sb(f"va{i}", [P, J, H, SLOT]) for i in range(R)]
        qt = [sb(f"qt{i}", [P, J, S]) for i in range(R)]
        z = sb("z", [P, J, D])
        stats, mean_var, rstd = sb("stats", [P, J, 6]), sb("mean_var", [P, J, 2]), sb("rstd", [P, J])
        f_row, fabs, lnt, log_f = sb("f_row", [H, S]), sb("fabs", [H, S]), sb("lnt", [H, S]), sb("log_f", [H, S])
        i_row, cs_row, m_row, minus_max = sb("i_row", [H, S]), sb("cs_row", [H, S]), sb("m_row", [H, S]), sb("minus_max", [H, S])
        tok_rows = sb("tok_rows", [ROWS, S])
        m_split = [sb(f"m_split{i}", [LO + H, S], F32R) for i in range(R)]
        tok = [sb(f"tok{i}", [P, J, ROWS]) for i in range(R)]
        decay = [sb(f"decay{i}", [P, W]) for i in range(R)]
        c_mat = [sb(f"c_mat{i}", [P, W]) for i in range(R)]
        ot = [sb(f"ot{i}", [P, GROUPS, S]) for i in range(R)]
        nrm, rn = sb("nrm", [P, J, H]), sb("rn", [P, J, H])
        hn = sb("hn", [P, J, H, DH])
        h_stats, h_mv, h_rstd = sb("h_stats", [P, J, 6]), sb("h_mv", [P, J, 2]), sb("h_rstd", [P, J])
        hz = sb("hz", [P, J, D])
        qk = [ctx.enter_context(nc.psum_tensor(f"a_qk{i}", [P, 512], F32)) for i in range(R)]
        ex = [ctx.enter_context(nc.psum_tensor(f"a_ex{i}", [P, 512], F32)) for i in range(R)]
        hp = ctx.enter_context(nc.psum_tensor("a_hp", [P, J, 512], F32))
        hvt = [ctx.enter_context(nc.psum_tensor(f"a_hvt{i}", [P, 512], F32)) for i in range(2)]
        tz = hp[:, 0, :].rearrange("p (c s) -> p c s", c=J)
        g_ps = hp[0:ROWS, 1, 0:S]
        tok_ps = hp[:, 1, S:S + J * ROWS].rearrange("p (j g) -> p j g", j=J)
        hv = hp[:].rearrange("p j (h d) -> p j h d", d=SLOT)

        const_loaded, built, ready = sem("const_loaded"), sem("built"), sem("ready")
        c_loaded = [sem(f"c_loaded{i}") for i in range(R)]
        va_done = sem("va_done")
        stats_done, mv_done, var_eps, rstd_done = sem("stats_done"), sem("mv_done"), sem("var_eps"), sem("rstd_done")
        z_done, tz_done, qt_done = sem("z_done"), sem("tz_done"), sem("qt_done")
        gates_done, f_done, fabs_done, i_done = sem("gates_done"), sem("f_done"), sem("fabs_done"), sem("i_done")
        exp_done, ln_done, log_f_done, cs_done = sem("exp_done"), sem("ln_done"), sem("log_f_done"), sem("cs_done")
        a_done, m_done, m_hi_done, m_split_done = sem("a_done"), sem("m_done"), sem("m_hi_done"), sem("m_split_done")
        max_done, thr_done, tok_turned, tok_done = sem("max_done"), sem("thr_done"), sem("tok_turned"), sem("tok_done")
        ot_done, turned = sem("ot_done"), sem("turned")
        qk_done, decay_done, c_done, cv_done = sem("qk_done"), sem("decay_done"), sem("c_done"), sem("cv_done")
        post, hp_read, h_stats_done, h_mv_done = sem("post"), sem("hp_read"), sem("h_stats_done"), sem("h_mv_done")
        h_var_eps, h_rstd_done, hz_done = sem("h_var_eps"), sem("h_rstd_done"), sem("hz_done")
        scaled, x_done = sem("scaled"), sem("x_done")
        block = ctx.enter_context(nc.Block())
        cv = ctx_in.rearrange("b (j p) d -> b p j d", p=P)

        def all_batches(engine, body):
            body(0, 0)
            with engine.Fori(0, (B - 4) // 2) as i:
                for u in range(2):
                    body(2 * i + (1 + u), (1 + u) % 2)
            for n in range(B - 3, B):
                body(n, n % 2)

        def first(n):
            return isinstance(n, int) and n == 0

        def below(n, bound):
            return not isinstance(n, int) or n < bound

        @block.sync
        def _(sync):
            sync.dma_start(wg_raw[:], gate_w).then_inc(const_loaded, 16)
            gate_cols = gate_b.rearrange("(n a) -> n a", a=1)
            sync.dma_start(gb[0:H, :], gate_cols[H:2 * H, :]).then_inc(const_loaded, 16)
            sync.dma_start(gb[LO:ROWS, :], gate_cols[0:H, :]).then_inc(const_loaded, 16)
            sync.dma_start(ln_s[:], ln_scale.partition_broadcast(P)).then_inc(const_loaded, 16)

            def load(n, u):
                if not (isinstance(n, int) and n < R):
                    sync.wait_ge(cv_done, (n - 1) * H)
                    sync.wait_ge(va_done, n - 1)
                sync.dma_start(kt[u][:], ctx_t[:, :, bass.ds(n * S, S)]).then_inc(c_loaded[u], 16)
                sync.dma_start(c_raw[u][:], cv[bass.ds(n, 1)].rearrange("b p j d -> p (b j) d")).then_inc(c_loaded[u], 16)

            load(0, 0)
            load(1, 1)
            with sync.Fori(0, (B - R) // 2) as i:
                for u in range(2):
                    load(2 * i + (2 + u), u)

        FILLS = 5 + 2 * R + 1
        BUILT = FILLS + R + 3

        @block.gpsimd
        def _(pool):
            pool.memset(zero_row[:], 0.0).then_inc(built, 1)
            pool.memset(mask[:], 0.0).then_inc(built, 1)
            pool.memset(tok_rows[:], 0.0).then_inc(built, 1)
            pool.memset(wg[:], 0.0).then_inc(built, 1)
            pool.memset(sel_raw[:], 0.0).then_inc(built, 1)
            for i in range(R):
                pool.memset(va[i][:], 0.0).then_inc(built, 1)
                pool.memset(m_split[i][:].bitcast(F32), 0.0).then_inc(built, 1)
            pool.tensor_copy(ident_b[:], ident[:]).then_inc(built, 1)
            pool.wait_ge(built, FILLS)
            for i in range(R):
                pool.memset(va[i][:, :, :, DH:DH + 1], 1.0).then_inc(built, 1)
            pool.affine_select(out=mask[:], in_=mask[:], compare_op=ALU.is_ge, fill=-1e30, base=0,
                               pattern=[[1, P]], channel_multiplier=-1).then_inc(built, 1)
            for k in range(2):
                pool.affine_select(out=sel_raw[:], in_=sel_raw[:], compare_op=ALU.not_equal, fill=-1.0, base=-LO * k,
                                   pattern=[[-1, H], [0, P]], channel_multiplier=1).then_inc(built, 1)
                pool.wait_ge(built, FILLS + R + 2 + k)

            def values(n, u, loads):
                pool.wait_ge(c_loaded[u], 32 * loads)
                alone(pool, cv_done, (n - 1) * H, passed)
                pool.tensor_copy(va[u][:, :, :, 0:DH], c_raw[u][:].rearrange("p j (h d) -> p j h d", d=DH)).then_inc(va_done, 1)

            def rstds(n):
                alone(pool, mv_done, J * n + J, passed)
                pool.tensor_scalar(rstd[:], mean_var[:, :, 1], LN_EPS, None, ALU.add).then_inc(var_eps, 1)
                pool.wait_ge(var_eps, n + 1)
                pool.tensor_tensor(rstd[:], rstd[:], half_neg[:, 0:J], ALU.pow).then_inc(rstd_done, 1)

            def h_rstds(n):
                alone(pool, h_mv_done, J * n + J, passed)
                pool.tensor_scalar(h_rstd[:], h_mv[:, :, 1], LN_EPS, None, ALU.add).then_inc(h_var_eps, 1)
                pool.wait_ge(h_var_eps, n + 1)
                pool.tensor_tensor(h_rstd[:], h_rstd[:], half_neg[:, 0:J], ALU.pow).then_inc(h_rstd_done, 1)

            def update_x(n):
                pool.wait_ge(hz_done, J * n + J)
                pool.wait_ge(ready, 2)
                for j in range(J):
                    pool.tensor_tensor(hz[:, j, :], hz[:, j, :], ln_s[:], ALU.mult).then_inc(scaled, 1)
                for j in range(J):
                    pool.wait_ge(scaled, J * n + j + 1)
                    xs = x_all[:, J * n + j, :]
                    pool.tensor_tensor(xs, xs, hz[:, j, :], ALU.add).then_inc(x_done, 1)

            rstds(0)
            values(0, 0, 1)
            rstds(1)

            def body(n, u, loads):
                if below(n, B - 1):
                    values(n + 1, 1 - u, loads)
                if below(n, B - 2):
                    rstds(n + 2)
                if not first(n):
                    h_rstds(n - 1)
                    update_x(n - 1)

            body(0, 0, 1)
            with pool.Fori(0, (B - 4) // 2) as i:
                for u in range(2):
                    body(2 * i + (1 + u), (1 + u) % 2, i + 2)
            for n in range(B - 3, B):
                body(n, n % 2, (n + 1) // 2 + 1)
            h_rstds(B - 1)
            update_x(B - 1)
            pool.wait_ge(x_done, B * J)

        @block.scalar
        def _(act):
            def queries(n, u):
                act.wait_ge(tz_done, n + 1)
                after(act, cv_done, (n - 1) * H)
                act.activation(qt[u][:], tz[:], ACT.Copy).then_inc(qt_done, 1)

            def input_gates(n):
                act.wait_ge(gates_done, n + 1)
                act.wait_ge(fabs_done, n + 1)
                after(act, a_done, n)
                act.activation(i_row[:], g_ps[LO:ROWS, :], ACT.Identity, bias=gb[LO:ROWS, :]).then_inc(i_done, 1)

            def softplus(n):
                act.activation(lnt[:], fabs[:], ACT.Exp, scale=-1.0).then_inc(exp_done, 1)
                act.wait_ge(exp_done, n + 1)
                act.activation(lnt[:], lnt[:], ACT.Ln, bias=1.0).then_inc(ln_done, 1)

            def thresholds(n):
                act.wait_ge(max_done, n + 1)
                after(act, tok_turned, n)
                act.activation(tok_rows[LO:ROWS, :], minus_max[:], ACT.Exp).then_inc(thr_done, 1)

            def keep_outputs(n, u, g):
                act.wait_ge(cv_done, n * H + GH * (g + 1))
                act.wait_ge(turned, n + 1)
                act.activation(ot[u][:, g, :], hvt[g % 2][:, 0:S], ACT.Copy).then_inc(ot_done, 1)

            def decays(n, u, h):
                act.wait_ge(qk_done, n * H + h + 1)
                after(act, c_done, n * H + h + 1 - R)
                act.activation(decay[h % R][:, 0:S], ex[h % R][:, 0:S], ACT.Exp,
                               bias=tok[u][:, 0, h:h + 1]).then_inc(decay_done, 1)
                act.activation(decay[h % R][:, S:W], ex[h % R][:, S:W], ACT.Exp,
                               bias=tok[u][:, 1, h:h + 1]).then_inc(decay_done, 1)

            queries(0, 0)
            input_gates(0)
            softplus(0)
            thresholds(0)

            def body(n, u):
                act.wait_ge(tok_done, n + 1)
                for h in range(H):
                    decays(n, u, h)
                    if h == 0:
                        if not first(n):
                            keep_outputs(n - 1, 1 - u, GROUPS - 1)
                        if below(n, B - 1):
                            queries(n + 1, 1 - u)
                    if h > 0 and h % GH == 0:
                        keep_outputs(n, u, h // GH - 1)
                    if below(n, B - 1):
                        if h == 2:
                            input_gates(n + 1)
                            softplus(n + 1)
                        if h == 6:
                            thresholds(n + 1)

            all_batches(act, body)
            keep_outputs(B - 1, (B - 1) % 2, GROUPS - 1)

        @block.vector
        def _(dve):
            post_step = Chain(dve, post, 4)
            dve.sem_inc(hp_read, 1)
            dve.wait_ge(const_loaded, 64)
            dve.wait_ge(built, BUILT)
            for at, g in ((0, H), (LO, 0)):
                dve.tensor_copy(wg[:, 0:2, at:at + H], wg_raw[:, 0:2, g:g + H])
                ins = dve.tensor_tensor(wg[:, 2:4, at:at + H], wg_raw[:, 2:4, g:g + H], wg_raw[:, 4:6, g:g + H], ALU.add)
            ins.then_inc(ready, 1)
            dve.tensor_scalar(ln_s[:], ln_s[:], tanh_g[:, 0:1], None, ALU.mult).then_inc(ready, 1)
            dve.tensor_copy(sel[:], sel_raw[:]).then_inc(ready, 1)

            def stat(n):
                for j in range(J):
                    dve.bn_stats(stats[:, j, :], x_all[:, J * n + j, :]).then_inc(stats_done, 1)
                for j in range(J):
                    alone(dve, stats_done, J * n + j + 1, passed)
                    dve.bn_aggr(mean_var[:, j, :], stats[:, j, :]).then_inc(mv_done, 1)

            def norm(n):
                dve.wait_ge(rstd_done, n + 1)
                after(dve, tz_done, n)
                for j in range(J):
                    dve.tensor_scalar(z[:, j, :], x_all[:, J * n + j, :], mean_var[:, j, 0:1], rstd[:, j:j + 1],
                                      ALU.subtract, ALU.mult).then_inc(z_done, 1)

            def forget_gates(n):
                dve.wait_ge(gates_done, n + 1)
                after(dve, log_f_done, n)
                dve.tensor_scalar(f_row[:], g_ps[0:H, :], gb[0:H, 0:1], None, ALU.add).then_inc(f_done, 1)
                dve.wait_ge(f_done, n + 1)
                dve.scalar_tensor_tensor(out=fabs[:], in0=f_row[:], scalar=-1.0, in1=f_row[:], op0=ALU.mult, op1=ALU.max).then_inc(fabs_done, 1)

            def decay_sums(n):
                dve.wait_ge(ln_done, n + 1)
                dve.scalar_tensor_tensor(out=log_f[:], in0=f_row[:], scalar=0.0, in1=lnt[:], op0=ALU.min, op1=ALU.subtract).then_inc(log_f_done, 1)
                dve.wait_ge(log_f_done, n + 1)
                dve.tensor_tensor_scan(cs_row[:], log_f[:], zero_row[:], 0.0, ALU.add, ALU.add).then_inc(cs_done, 1)

            def maxima(n, u):
                dve.wait_ge(cs_done, n + 1)
                dve.wait_ge(i_done, n + 1)
                dve.wait_ge(tok_turned, n) if not first(n) else None
                dve.tensor_tensor(tok_rows[0:H, :], i_row[:], cs_row[:], ALU.subtract).then_inc(a_done, 1)
                dve.wait_ge(a_done, n + 1)
                dve.tensor_tensor_scan(m_row[:], tok_rows[0:H, :], tok_rows[0:H, :], -3e38, ALU.max, ALU.max).then_inc(m_done, 1)

            def split_maxima(n, u):
                dve.wait_ge(m_done, n + 1)
                dve.scalar_tensor_tensor(out=minus_max[:], in0=cs_row[:], scalar=-1.0, in1=m_row[:], op0=ALU.mult, op1=ALU.subtract).then_inc(max_done, 1)
                dve.tensor_copy(m_split[u][0:H, :], m_row[:]).then_inc(m_hi_done, 1)
                dve.wait_ge(m_hi_done, n + 1)
                dve.tensor_tensor(m_split[u][LO:LO + H, :], m_row[:], m_split[u][0:H, :], ALU.subtract).then_inc(m_split_done, 1)

            def by_tokens(n, u):
                dve.wait_ge(tok_turned, n + 1)
                dve.tensor_copy(tok[u][:], tok_ps).then_inc(tok_done, 1)

            def weigh(n, h):
                dve.wait_ge(decay_done, 2 * (n * H + h) + 2)
                after(dve, cv_done, n * H + h + 1 - R)
                dve.scalar_tensor_tensor(out=c_mat[h % R][:], in0=qk[h % R][:, 0:W], scalar=SCALE, in1=decay[h % R][:],
                                         op0=ALU.mult, op1=ALU.mult).then_inc(c_done, 1)

            def normalise(n, u):
                post_step.begin(n)
                dve.wait_ge(turned, n + 3)
                for sign in (-1.0, 1.0):
                    post_step(dve.scalar_tensor_tensor(out=nrm[:], in0=hv[:, :, :, DH], scalar=sign,
                                                       in1=tok[u][:, :, LO:ROWS] if sign < 0 else nrm[:], op0=ALU.mult, op1=ALU.max))
                post_step(dve.tensor_scalar(nrm[:], nrm[:], MLSTM_EPS, None, ALU.add))
                post_step(dve.reciprocal(rn[:], nrm[:]))
                dve.tensor_tensor(hn[:], hv[:, :, :, 0:DH], rn[:].rearrange("p j (h a) -> p j h a", a=1).broadcast_to([P, J, H, DH]),
                                  ALU.mult).then_inc(hp_read, 1)

            def h_stat(n):
                dve.wait_ge(hp_read, n + 2)
                for j in range(J):
                    dve.bn_stats(h_stats[:, j, :], hn[:, j, :, :].rearrange("p h d -> p (h d)")).then_inc(h_stats_done, 1)
                for j in range(J):
                    alone(dve, h_stats_done, J * n + j + 1, passed)
                    dve.bn_aggr(h_mv[:, j, :], h_stats[:, j, :]).then_inc(h_mv_done, 1)

            def h_norm(n):
                dve.wait_ge(h_rstd_done, n + 1)
                after(dve, x_done, J * n)
                for j in range(J):
                    dve.tensor_scalar(hz[:, j, :], hn[:, j, :, :].rearrange("p h d -> p (h d)"), h_mv[:, j, 0:1],
                                      h_rstd[:, j:j + 1], ALU.subtract, ALU.mult).then_inc(hz_done, 1)

            stat(0)
            norm(0)
            forget_gates(0)
            decay_sums(0)
            maxima(0, 0)
            split_maxima(0, 0)
            stat(1)
            norm(1)
            by_tokens(0, 0)

            def body(n, u):
                for h in range(H):
                    weigh(n, h)
                    if below(n, B - 1):
                        if h == 1:
                            forget_gates(n + 1)
                        if h == 3:
                            decay_sums(n + 1)
                        if h == 4:
                            maxima(n + 1, 1 - u)
                        if h == 5:
                            split_maxima(n + 1, 1 - u)
                        if h == 7:
                            by_tokens(n + 1, 1 - u)
                    if not first(n):
                        if h == 5:
                            normalise(n - 1, 1 - u)
                        if h == 6:
                            h_stat(n - 1)
                        if h == 7:
                            h_norm(n - 1)
                    if below(n, B - 2):
                        if h == 2:
                            stat(n + 2)
                        if h == 4:
                            norm(n + 2)

            all_batches(dve, body)
            normalise(B - 1, (B - 1) % 2)
            h_stat(B - 1)
            h_norm(B - 1)

        @block.tensor
        def _(pe):
            def transpose_z(n):
                pe.wait_ge(z_done, J * n + J)
                after(pe, hp_read, n - 1)
                for c in range(J):
                    for j in range(J):
                        mm = pe.transpose(tz[:, c, j * P:(j + 1) * P], z[:, j, c * P:(c + 1) * P], ident[:])
                mm.then_inc(tz_done, 1)

            def gate_sums(n, u, loads):
                pe.wait_ge(c_loaded[u], 32 * loads)
                after(pe, tok_done, n)
                for c in range(2):
                    pe.matmul(g_ps, wg[:, 2 + c, :], kt[u][:, c, :], start=(c == 0), stop=False)
                pe.wait_ge(qt_done, n + 1)
                for c in range(2):
                    mm = pe.matmul(g_ps, wg[:, c, :], qt[u][:, c, :], start=False, stop=(c == 1))
                mm.then_inc(gates_done, 1)

            def turn_rows(n):
                pe.wait_ge(thr_done, n + 1)
                pe.wait_ge(a_done, n + 1)
                alone(pe, hp_read, n, passed)
                for j in range(J):
                    mm = pe.transpose(tok_ps[:, j, :], tok_rows[:, j * P:(j + 1) * P], ident[0:ROWS, 0:ROWS])
                mm.then_inc(tok_turned, 1)

            def turn_outputs(n, u):
                pe.wait_ge(ot_done, GROUPS * (n + 1))
                pe.wait_ge(qt_done, min(n + 3, B) if isinstance(n, int) else n + 3)
                pe.wait_ge(i_done, min(n + 3, B) if isinstance(n, int) else n + 3)
                for g in range(GROUPS):
                    for j in range(J):
                        mm = pe.transpose(hp[:, j, g * P:(g + 1) * P], ot[u][:, g, j * P:(j + 1) * P], ident[:])
                mm.then_inc(turned, 1)

            def scores(n, u, h):
                after(pe, c_done, n * H + h + 1 - R)
                after(pe, decay_done, 2 * (n * H + h + 1 - R))
                rows, c = slice(DH * (h % 4), DH * (h % 4) + DH), h // 4
                q, k, s, e = qt[u], kt[u], qk[h % R], ex[h % R]
                pe.matmul(s[:, 0:S], k[rows, c, 0:P], q[rows, c, :], start=True, stop=True)
                pe.matmul(s[:, S:W], k[rows, c, P:S], q[rows, c, P:S], start=True, stop=True)
                pe.matmul(e[:, 0:S], sel[:, h, :], m_split[u][:], start=True, stop=True)
                pe.matmul(e[:, 0:P], ident_b[:], mask[:], start=False, stop=True, skip_group_check=True)
                pe.matmul(e[:, S:W], sel[:, h, :], m_split[u][:, P:S], start=False, stop=False, skip_group_check=True)
                pe.matmul(e[:, S:W], ident_b[:], mask[:], start=False, stop=True, skip_group_check=True).then_inc(qk_done, 1)

            def values(n, u, h):
                pe.wait_ge(c_done, n * H + h + 1)
                if h == 0:
                    pe.wait_ge(va_done, n + 1)
                g = h // GH
                if h % GH == 0:
                    after(pe, ot_done, GROUPS * n + g - 1)
                c = c_mat[h % R]
                out = hvt[g % 2][SLOT * (h % GH):SLOT * (h % GH + 1), :]
                pe.matmul(out[:, 0:S], va[u][:, 0, h, :], c[:, 0:S], start=True, stop=True)
                pe.matmul(out[:, P:S], va[u][:, 1, h, :], c[:, S:W], start=False, stop=True, skip_group_check=True).then_inc(cv_done, 1)

            pe.wait_ge(ready, 3)
            pe.wait_ge(built, BUILT)
            pe.sem_inc(turned, 2)
            transpose_z(0)
            gate_sums(0, 0, 1)
            turn_rows(0)

            def body(n, u, loads):
                pe.wait_ge(m_split_done, n + 1)
                for h in range(H):
                    scores(n, u, h)
                    if h > 0:
                        values(n, u, h - 1)
                    elif not first(n):
                        values(n - 1, 1 - u, H - 1)
                    if below(n, B - 1):
                        if h == 0:
                            transpose_z(n + 1)
                        if h == 1:
                            gate_sums(n + 1, 1 - u, loads)
                        if h == 7:
                            turn_rows(n + 1)
                    if h == 3 and not first(n):
                        turn_outputs(n - 1, 1 - u)

            body(0, 0, 1)
            with pe.Fori(0, (B - 4) // 2) as i:
                for u in range(2):
                    body(2 * i + (1 + u), (1 + u) % 2, i + 2)
            for n in range(B - 3, B):
                body(n, n % 2, (n + 1) // 2 + 1)
            values(B - 1, (B - 1) % 2, H - 1)
            turn_outputs(B - 1, (B - 1) % 2)


def phase_lora_ffn(nc, x_all, tanh_g, ident, half_neg, passed, w_fc_t, b_fc, a_fc, b_fc_t, w_pr_t, b_pr, a_pr, b_pr_t):
    D, FF, R = 256, w_fc_t.shape[2], a_fc.shape[0]
    T = 4
    TOK = T * P
    CHUNKS = x_all.shape[1] // T
    KD, KF = D // P, FF // P
    HR = 4
    GR = 2
    EARLY = 6
    PIECE = 512
    with ExitStack() as ctx:
        def sb(name, shape, dt=F32):
            return ctx.enter_context(nc.sbuf_tensor("b_" + name, shape, dt))

        sem = cleared_semaphores(nc, ctx, "b_")

        w1_hi, w1_lo = sb("w1_hi", [P, KD, FF], F32R), sb("w1_lo", [P, KD, FF], F32R)
        w2_hi, w2_lo = sb("w2_hi", [P, KF, D], F32R), sb("w2_lo", [P, KF, D], F32R)
        w1_raw, w2_raw = sb("w1_raw", [P, KD, FF]), sb("w2_raw", [P, KF, D])
        b1, b2 = sb("b1", [P, KF]), sb("b2", [P, D])
        a1, a2 = sb("a1", [R, D]), sb("a2", [R, FF])
        b1t, b2t = sb("b1t", [R, FF]), sb("b2t", [R, D])
        amax, amax_rows = sb("amax", [P, 2]), sb("amax_rows", [P, 2])
        scale, inv = sb("scale", [P, 2]), sb("inv", [P, 2])
        stats, mean_var = sb("stats", [P, T, 6]), sb("mean_var", [P, T, 2])
        rstd = sb("rstd", [P, T])
        z = sb("z", [P, T, D])
        zt_hi, zt_lo = sb("zt_hi", [P, KD, TOK], F32R), sb("zt_lo", [P, KD, TOK], F32R)
        g_full = sb("g_full", [P, GR, TOK])
        g_hi, g_lo = sb("g_hi", [P, KF, TOK], F32R), sb("g_lo", [P, KF, TOK], F32R)
        hid = [ctx.enter_context(nc.psum_tensor(f"b_hid{i}", [P, TOK], F32)) for i in range(HR)]
        zt = [ctx.enter_context(nc.psum_tensor(f"b_zt{i}", [P, TOK], F32)) for i in range(KD)]
        y = [ctx.enter_context(nc.psum_tensor(f"b_y{i}", [P, 2, D], F32)) for i in range(T // 2)]

        w_loaded, small_loaded = sem("w_loaded"), sem("small_loaded")
        amax_done, amax_all = sem("amax_done"), sem("amax_all")
        prep, lora_done, lora_used, w_ready = sem("prep"), sem("lora_done"), sem("lora_used"), sem("w_ready")
        stats_done, mv_done = sem("stats_done"), sem("mv_done")
        var_eps, rstd_done = sem("var_eps"), sem("rstd_done")
        z_done, zt_done, zt_hi_done, zt_lo_done = sem("z_done"), sem("zt_done"), sem("zt_hi_done"), sem("zt_lo_done")
        hid_done, gelu_full = sem("hid_done"), sem("gelu_full")
        gelu_hi = sem("gelu_hi")
        gelu_lo = sem("gelu_lo")
        y_done, x_added, x_biased = sem("y_done"), sem("x_added"), sem("x_biased")
        block = ctx.enter_context(nc.Block())

        @block.sync
        def _(sync):
            sync.dma_start(w1_raw[:], w_fc_t).then_inc(w_loaded, 16)
            sync.dma_start(w2_raw[:], w_pr_t).then_inc(w_loaded, 16)

        @block.scalar
        def _(act):
            for dst, src in ((a1, a_fc), (a2, a_pr), (b1t, b_fc_t), (b2t, b_pr_t), (b1, b_fc)):
                act.dma_start(dst[:], src).then_inc(small_loaded, 16)
            act.dma_start(b2[:], b_pr.partition_broadcast(P)).then_inc(small_loaded, 16)
            act.sem_inc(gelu_hi, HR)

            def split_zt(n):
                for c in range(KD):
                    act.wait_ge(zt_done, n * KD + c + 1)
                    act.activation(zt_hi[:, c, :], zt[c][:], ACT.Copy).then_inc(zt_hi_done, 1)

            def gelus(n):
                for m in range(KF):
                    act.wait_ge(hid_done, n * KF + m + 1)
                    act.wait_ge(gelu_lo, n * KF + m + 1)
                    act.activation(g_full[:, m % GR, :], hid[m % HR][:], ACT.Gelu,
                                   bias=b1[:, m:m + 1]).then_inc(gelu_full, 1)
                    act.activation(g_hi[:, m, :], hid[m % HR][:], ACT.Gelu,
                                   bias=b1[:, m:m + 1]).then_inc(gelu_hi, 1)

            split_zt(0)
            act.wait_ge(small_loaded, 96)
            with act.Fori(0, CHUNKS - 1) as n:
                gelus(n)
                split_zt(n + 1)
            gelus(CHUNKS - 1)

        @block.gpsimd
        def _(pool):
            def rstds(n):
                alone(pool, mv_done, n * T + T, passed)
                pool.tensor_scalar(rstd[:], mean_var[:, :, 1], LN_EPS, None, ALU.add).then_inc(var_eps, 1)
                pool.wait_ge(var_eps, n + 1)
                pool.tensor_tensor(rstd[:], rstd[:], half_neg[:, 0:T], ALU.pow).then_inc(rstd_done, 1)

            def bias_x(n):
                pool.wait_ge(z_done, n * T + T)
                for t in range(T):
                    xs = x_all[:, n * T + t, :]
                    pool.tensor_tensor(xs, xs, b2[:], ALU.add).then_inc(x_biased, 1)

            rstds(0)
            pool.wait_ge(amax_done, 2)
            pool.partition_all_reduce(amax[:], amax_rows[:], P, RMAX).then_inc(amax_all, 1)
            pool.wait_ge(w_ready, 1)
            bias_x(0)
            with pool.Fori(0, CHUNKS - 1) as n:
                rstds(n + 1)
                bias_x(n + 1)

        @block.vector
        def _(dve):
            steps = [0]

            def chain(ins):
                steps[0] += 1
                ins.then_inc(prep, 1)
                dve.wait_ge(prep, steps[0])

            def stat(n):
                for t in range(T):
                    dve.bn_stats(stats[:, t, :], x_all[:, n * T + t, :]).then_inc(stats_done, 1)
                for t in range(T):
                    alone(dve, stats_done, n * T + t + 1, passed)
                    dve.bn_aggr(mean_var[:, t, :], stats[:, t, :]).then_inc(mv_done, 1)

            def norm(n):
                dve.wait_ge(rstd_done, n + 1)
                for t in range(T):
                    dve.tensor_scalar(z[:, t, :], x_all[:, n * T + t, :], mean_var[:, t, 0:1], rstd[:, t:t + 1],
                                      ALU.subtract, ALU.mult).then_inc(z_done, 1)

            def split_zt(n):
                for c in range(KD):
                    dve.wait_ge(zt_hi_done, n * KD + c + 1)
                    dve.tensor_tensor(zt_lo[:, c, :], zt[c][:], zt_hi[:, c, :], ALU.subtract).then_inc(zt_lo_done, 1)

            def split_gelu(n):
                for m in range(KF):
                    dve.wait_ge(gelu_hi, HR + n * KF + m + 1)
                    dve.wait_ge(gelu_full, n * KF + m + 1)
                    dve.tensor_tensor(g_lo[:, m, :], g_full[:, m % GR, :], g_hi[:, m, :],
                                      ALU.subtract).then_inc(gelu_lo, 1)

            def add_x(n):
                for h in range(T // 2):
                    dve.wait_ge(y_done, n * (T // 2) + h + 1)
                    dve.wait_ge(x_biased, n * T + T)
                    xs = x_all[:, bass.ds(n * T + 2 * h, 2), :]
                    dve.tensor_tensor(xs, xs, y[h][:], ALU.add).then_inc(x_added, 1)

            dve.sem_inc(gelu_lo, GR)
            stat(0)
            dve.wait_ge(w_loaded, 32)
            for i, w in enumerate((w1_raw, w2_raw)):
                dve.tensor_reduce(amax_rows[:, i:i + 1], w[:].rearrange("p a b -> p (a b)"), AX.X, ALU.max,
                                  apply_absolute_value=True).then_inc(amax_done, 1)
            norm(0)
            dve.wait_ge(amax_all, 1)
            chain(dve.tensor_scalar(scale[:], amax[:], 1.0 / QMAX, None, ALU.mult))
            chain(dve.reciprocal(inv[:], scale[:]))
            dve.wait_ge(small_loaded, 96)
            chain(dve.tensor_scalar(b2[:], b2[:], tanh_g[:, 2:3], None, ALU.mult))
            for i, (w, hi, lo) in enumerate(((w1_raw, w1_hi, w1_lo), (w2_raw, w2_hi, w2_lo))):
                flat = w[:].rearrange("p a b -> p (a b)")
                chain(dve.tensor_scalar(flat, flat, inv[:, i:i + 1], ROUND, ALU.mult, ALU.add))
                chain(dve.tensor_scalar(flat, flat, -ROUND, QMAX, ALU.add, ALU.min))
                chain(dve.tensor_scalar(flat, flat, -QMAX - 1.0, scale[:, i:i + 1], ALU.max, ALU.mult))
                for q in range(4):
                    dve.wait_ge(lora_done, 4 * i + q + 1)
                    dst = flat[:, PIECE * q:PIECE * (q + 1)]
                    dve.scalar_tensor_tensor(out=dst, in0=hid[q][:], scalar=2.0, in1=dst,
                                             op0=ALU.mult, op1=ALU.add).then_inc(lora_used, 1)
                dve.wait_ge(lora_used, 4 * i + 4)
                if i == 1:
                    chain(dve.tensor_scalar(flat, flat, tanh_g[:, 2:3], None, ALU.mult))
                chain(dve.tensor_copy(hi[:], w[:]))
                dve.tensor_tensor(lo[:], w[:], hi[:], ALU.subtract).then_inc(w_ready, 1)
            split_zt(0)
            with dve.Fori(0, CHUNKS - 1) as n:
                stat(n + 1)
                norm(n + 1)
                split_gelu(n)
                split_zt(n + 1)
                add_x(n)
            split_gelu(CHUNKS - 1)
            add_x(CHUNKS - 1)
            dve.wait_ge(x_added, CHUNKS * T // 2)

        @block.tensor
        def _(pe):
            def transpose_z(n):
                pe.wait_ge(z_done, n * T + T)
                for c in range(KD):
                    for t in range(T):
                        mm = pe.transpose(zt[c][:, t * P:(t + 1) * P], z[:, t, c * P:(c + 1) * P], ident[:])
                    mm.then_inc(zt_done, 1)

            def lora_products(i):
                if i == 0:
                    pe.wait_ge(small_loaded, 96)
                for q in range(4):
                    if i == 1:
                        pe.wait_ge(lora_used, q + 1)
                    if i == 0:
                        c, cols = q // 2, slice(PIECE * (q % 2), PIECE * (q % 2 + 1))
                        mm = pe.matmul(hid[q][:], a1[:, c * P:(c + 1) * P], b1t[:, cols], start=True, stop=True)
                    else:
                        for k in range(2):
                            m = 2 * q + k
                            mm = pe.matmul(hid[q][:, D * k:D * (k + 1)], a2[:, m * P:(m + 1) * P], b2t[:],
                                           start=True, stop=True)
                    mm.then_inc(lora_done, 1)

            def hidden(n):
                pe.wait_ge(zt_lo_done, n * KD + KD)
                for m in range(KF):
                    pe.wait_ge(gelu_hi, n * KF + m + 1)
                    cols = slice(m * P, (m + 1) * P)
                    for c in range(KD):
                        mm = three_passes(pe, hid[m % HR][:], (w1_hi[:, c, cols], w1_lo[:, c, cols]),
                                          (zt_hi[:, c, :], zt_lo[:, c, :]), c == 0, c == KD - 1)
                    mm.then_inc(hid_done, 1)

            def outputs(n):
                def product(t, m):
                    cols = slice(t * P, (t + 1) * P)
                    return three_passes(pe, y[t // 2][:, t % 2, :], (g_hi[:, m, cols], g_lo[:, m, cols]),
                                        (w2_hi[:, m, :], w2_lo[:, m, :]), m == 0, m == KF - 1)

                pe.wait_ge(x_added, n * (T // 2))
                pe.wait_ge(gelu_lo, GR + n * KF + EARLY)
                for t in range(0, T, 2):
                    for m in range(EARLY):
                        product(t, m)
                pe.wait_ge(gelu_lo, GR + n * KF + KF)
                for t in range(T):
                    for m in range(0 if t % 2 else EARLY, KF):
                        mm = product(t, m)
                    if t % 2:
                        mm.then_inc(y_done, 1)

            lora_products(0)
            transpose_z(0)
            lora_products(1)
            pe.wait_ge(w_ready, 2)
            with pe.Fori(0, CHUNKS - 1) as n:
                hidden(n)
                transpose_z(n + 1)
                outputs(n)
            hidden(CHUNKS - 1)
            outputs(CHUNKS - 1)


def phase_attention(nc, x_all, tanh_g, ident, half_neg, passed, ctx_t, wq_in, wkv_in, wc_in):
    B, S, D, H = 16, 256, 256, 16
    DH = D // H
    J = S // P
    SLOT = 64
    PAIRS = H * SLOT // P
    K3 = 3 * DH
    SCALE = float(DH) ** -0.5
    OSLOT = 32
    GH = P // OSLOT
    R = 2
    PR, LAG = 4, 2
    FILLS = 2 * PAIRS * J // 4
    MAX_SLOTS = {s: (2 * (s - 4), 2 * (s - 4) + 1) for s in range(4, 10)} | {s: (s + 2,) for s in range(10, 14)}
    with ExitStack() as ctx:
        def sb(name, shape, dt=F32):
            return ctx.enter_context(nc.sbuf_tensor("c_" + name, shape, dt))

        sem = cleared_semaphores(nc, ctx, "c_")

        w_raw = sb("w_raw", [P, 2, 4 * D])
        w_hi, w_lo = sb("w_hi", [P, 2, 4 * D], F32R), sb("w_lo", [P, 2, 4 * D], F32R)
        sel_raw = sb("sel_raw", [2 * H, H, P])
        sel = sb("sel", [2 * H, H, P], F32R)
        c_raw = [sb(f"c_raw{i}", [P, 2, S]) for i in range(R)]
        ct_hi, ct_lo = sb("ct_hi", [P, 2, S], F32R), sb("ct_lo", [P, 2, S], F32R)
        stats, mean_var, rstd = sb("stats", [P, J, 6]), sb("mean_var", [P, J, 2]), sb("rstd", [P, J])
        z = sb("z", [P, J, D])
        zt_hi, zt_lo = sb("zt_hi", [P, 2, S], F32R), sb("zt_lo", [P, 2, S], F32R)
        q3, k3 = sb("q3", [P, J * H, SLOT], F32R), sb("k3", [P, J * H, SLOT], F32R)
        v_tmp = sb("v_tmp", [P, J, D])
        va = [sb(f"va{i}", [P, J, H, OSLOT]) for i in range(R)]
        qt = [sb(f"qt{i}", [P, PAIRS, S], F32R) for i in range(R)]
        kt = [sb(f"kt{i}", [P, PAIRS, S], F32R) for i in range(R)]
        mx = sb("mx", [P, J, H])
        m_tok = sb("m_tok", [P, J, 2 * H], F32R)
        m_row = [sb(f"m_row{i}", [2 * H, S], F32R) for i in range(R)]
        probs = [sb(f"probs{i}", [P, J, S]) for i in range(PR)]
        ot = sb("ot", [P, 2, 2, S])
        rden = sb("rden", [P, J, H])
        yn = sb("yn", [P, J, H, DH])
        yt_hi, yt_lo = sb("yt_hi", [P, 2, S], F32R), sb("yt_lo", [P, 2, S], F32R)

        def pb(name, shape):
            return ctx.enter_context(nc.psum_tensor("c_" + name, shape, F32))

        s_ps = [pb(f"s{i}", [P, J, S]) for i in range(R)]
        t_ps = [pb(f"t{i}", [P, J, S]) for i in range(R)]
        o_ps = [pb(f"o{i}", [P, 2, S]) for i in range(2)]
        even, odd = pb("even", [P, 2, S]), pb("odd", [P, 2, S])

        w_loaded, w_ready, prep, built = sem("w_loaded"), sem("w_ready"), sem("prep"), sem("built")
        c_loaded = [sem(f"c_loaded{i}") for i in range(R)]
        ct_hi_done, ct_lo_done = sem("ct_hi_done"), sem("ct_lo_done")
        stats_done, mv_done, var_eps, rstd_done = sem("stats_done"), sem("mv_done"), sem("var_eps"), sem("rstd_done")
        z_done, zt_done, zt_hi_done, zt_lo_done = sem("z_done"), sem("zt_done"), sem("zt_hi_done"), sem("zt_lo_done")
        q_done, q_hi_done, q_lo_done = sem("q_done"), sem("q_hi_done"), sem("q_lo_done")
        kv_done, k_hi_done, v_done, k_lo_done = sem("kv_done"), sem("k_hi_done"), sem("v_done"), sem("k_lo_done")
        va_done = sem("va_done")
        turned, turned_read = sem("turned"), sem("turned_read")
        s_done, max_done, m_hi_done, m_tok_done = sem("s_done"), sem("max_done"), sem("m_hi_done"), sem("m_tok_done")
        m_turned, m_row_done = sem("m_turned"), sem("m_row_done")
        t_done, exp_done, pv_done = sem("t_done"), sem("exp_done"), sem("pv_done")
        rden_done, y_done, yt_done, yt_hi_done, yt_lo_done = sem("rden_done"), sem("y_done"), sem("yt_done"), sem("yt_hi_done"), sem("yt_lo_done")
        ot_done, o_turned = sem("ot_done"), sem("o_turned")
        out_done, x_done = sem("out_done"), sem("x_done")
        block = ctx.enter_context(nc.Block())

        def all_batches(engine, body):
            body(0, 0)
            with engine.Fori(0, (B - 4) // 2) as i:
                for u in range(2):
                    body(2 * i + (1 + u), (1 + u) % 2)
            for n in range(B - 3, B):
                body(n, n % 2)

        def has(n, least=None, below=None):
            return not isinstance(n, int) or ((least is None or n >= least) and (below is None or n < below))

        @block.sync
        def _(sync):
            sync.dma_start(w_raw[:, :, 0:D], wq_in).then_inc(w_loaded, 16)
            sync.dma_start(w_raw[:, :, D:3 * D], wkv_in).then_inc(w_loaded, 16)
            sync.dma_start(w_raw[:, :, 3 * D:4 * D], wc_in).then_inc(w_loaded, 16)

            def load(n, u):
                if not (isinstance(n, int) and n < R):
                    sync.wait_ge(ct_lo_done, n - 1)
                sync.dma_start(c_raw[u][:], ctx_t[:, :, bass.ds(n * S, S)]).then_inc(c_loaded[u], 16)

            load(0, 0)
            load(1, 1)
            with sync.Fori(0, (B - R) // 2) as i:
                for u in range(2):
                    load(2 * i + (2 + u), u)

        @block.gpsimd
        def _(pool):
            pool.memset(sel_raw[:], 0.0).then_inc(built, 1)
            pool.memset(q3[:].bitcast(F32), 0.0).then_inc(built, 1)
            pool.memset(k3[:].bitcast(F32), 0.0).then_inc(built, 1)
            for i in range(R):
                pool.memset(va[i][:], 0.0).then_inc(built, 1)
            pool.wait_ge(built, 5)
            for i in range(R):
                pool.memset(va[i][:, :, :, DH:DH + 1], 1.0).then_inc(built, 1)
            for k in range(2):
                pool.wait_ge(built, 7 + k)
                pool.affine_select(out=sel_raw[:], in_=sel_raw[:], compare_op=ALU.not_equal, fill=-1.0, base=-H * k,
                                   pattern=[[-1, H], [0, P]], channel_multiplier=1).then_inc(built, 1)

            def split_context(n, u, loads):
                pool.wait_ge(c_loaded[u], 16 * loads)
                alone(pool, kv_done, J * n, passed)
                pool.tensor_copy(ct_hi[:], c_raw[u][:]).then_inc(ct_hi_done, 1)
                pool.wait_ge(ct_hi_done, n + 1)
                pool.tensor_tensor(ct_lo[:], c_raw[u][:], ct_hi[:], ALU.subtract).then_inc(ct_lo_done, 1)

            def rstds(n):
                alone(pool, mv_done, J * n + J, passed)
                pool.tensor_scalar(rstd[:], mean_var[:, :, 1], LN_EPS, None, ALU.add).then_inc(var_eps, 1)
                pool.wait_ge(var_eps, n + 1)
                pool.tensor_tensor(rstd[:], rstd[:], half_neg[:, 0:J], ALU.pow).then_inc(rstd_done, 1)

            def values(n, u):
                pool.wait_ge(v_done, J * n + J)
                alone(pool, pv_done, (n - 1) * H, passed)
                pool.tensor_copy(va[u][:, :, :, 0:DH], v_tmp[:].rearrange("p j (h d) -> p j h d", d=DH)).then_inc(va_done, 1)

            split_context(0, 0, 1)
            rstds(0)
            values(0, 0)
            rstds(1)
            split_context(1, 1, 1)

            def body(n, u, loads):
                if has(n, below=B - 1):
                    values(n + 1, 1 - u)
                if has(n, below=B - 2):
                    rstds(n + 2)
                    split_context(n + 2, u, loads)

            body(0, 0, 2)
            with pool.Fori(0, (B - 4) // 2) as i:
                for u in range(2):
                    body(2 * i + (1 + u), (1 + u) % 2, i + (2 + u))
            for n in range(B - 3, B):
                body(n, n % 2, n // 2 + 2)

        @block.scalar
        def _(act):
            def split_zt(n):
                act.wait_ge(zt_done, n + 1)
                act.activation(zt_hi[:], even[:], ACT.Copy).then_inc(zt_hi_done, 1)

            def three_rows(t3, tiles, at, src, scale):
                out = t3[:, tiles, 0:K3].rearrange("p h (r d) -> p h r d", r=3)[:, :, at, :]
                n = src.shape[1] // DH
                src = src.rearrange("p (h a d) -> p h a d", a=1, d=DH).broadcast_to([P, n, 2, DH])
                return act.activation(out, src, ACT.Copy, scale=scale)

            def split_q(n):
                act.wait_ge(q_done, n + 1)
                three_rows(q3, slice(0, J * H), slice(0, 2), odd[:].rearrange("p j d -> p (j d)"), SCALE).then_inc(q_hi_done, 1)

            def split_kv(n, j):
                act.wait_ge(kv_done, J * n + j + 1)
                after(act, va_done, n)
                bank = (even, odd)[j]
                three_rows(k3, slice(j * H, (j + 1) * H), slice(0, 3, 2), bank[:, 0, :], 1.0).then_inc(k_hi_done, 1)
                act.activation(v_tmp[:, j, :], bank[:, 1, :], ACT.Copy).then_inc(v_done, 1)

            def read_turned(n, u, f):
                act.wait_ge(turned, FILLS * n + f + 1)
                after(act, pv_done, (n - 1) * H)
                g = f // 2
                dst = (qt, kt)[f % 2][u]
                act.activation(dst[:, 2 * g:2 * g + 2, :], (even, odd)[f % 2][:], ACT.Copy).then_inc(turned_read, 1)

            def max_rows(n, u):
                act.wait_ge(m_turned, n + 1)
                act.activation(m_row[u][:], even[0:2 * H, 0, :], ACT.Copy).then_inc(m_row_done, 1)

            def exps(n, u, h):
                act.wait_ge(t_done, n * H + h + 1)
                after(act, pv_done, n * H + h + 1 - PR)
                act.activation(probs[h % PR][:], t_ps[h % R][:], ACT.Exp).then_inc(exp_done, 1)

            def read_outputs(n, f):
                act.wait_ge(pv_done, n * H + (f + 1) * H // 2)
                after(act, o_turned, 2 * (n - 1) + f + 1)
                act.activation(ot[:, f], o_ps[f][:], ACT.Copy).then_inc(ot_done, 1)

            def split_yt(n):
                act.wait_ge(yt_done, n + 1)
                act.activation(yt_hi[:], even[:], ACT.Copy).then_inc(yt_hi_done, 1)

            act.wait_ge(built, 9)
            for n in range(2):
                split_zt(n)
                split_q(n)
                for j in range(J):
                    split_kv(n, j)
                if n == 0:
                    for f in range(FILLS):
                        read_turned(0, 0, f)
            max_rows(0, 0)

            def body(n, u):
                for h in range(H):
                    exps(n, u, h)
                    if has(n, below=B - 1) and h < FILLS // 2:
                        read_turned(n + 1, 1 - u, 2 * h)
                        read_turned(n + 1, 1 - u, 2 * h + 1)
                    if has(n, least=1):
                        if h == 2:
                            read_outputs(n - 1, 1)
                        if h == 7:
                            split_yt(n - 1)
                    if h == 11:
                        read_outputs(n, 0)
                    if has(n, below=B - 2):
                        if h == 9:
                            split_zt(n + 2)
                        if h == 11:
                            split_q(n + 2)
                        if h in (12, 13):
                            split_kv(n + 2, h - 12)
                    if has(n, below=B - 1) and h == 15:
                        max_rows(n + 1, 1 - u)

            all_batches(act, body)
            read_outputs(B - 1, 1)
            split_yt(B - 1)

        @block.vector
        def _(dve):
            dve.wait_ge(w_loaded, 48)
            dve.tensor_scalar(w_raw[:, :, 3 * D:], w_raw[:, :, 3 * D:], tanh_g[:, 1:2], None, ALU.mult).then_inc(prep, 1)
            dve.wait_ge(prep, 1)
            dve.tensor_copy(w_hi[:], w_raw[:]).then_inc(prep, 1)
            dve.wait_ge(prep, 2)
            dve.tensor_tensor(w_lo[:], w_raw[:], w_hi[:], ALU.subtract).then_inc(w_ready, 1)
            dve.wait_ge(built, 9)
            dve.tensor_copy(sel[:], sel_raw[:]).then_inc(w_ready, 1)

            def stat(n):
                for j in range(J):
                    dve.bn_stats(stats[:, j, :], x_all[:, J * n + j, :]).then_inc(stats_done, 1)
                for j in range(J):
                    alone(dve, stats_done, J * n + j + 1, passed)
                    dve.bn_aggr(mean_var[:, j, :], stats[:, j, :]).then_inc(mv_done, 1)

            def norm(n):
                dve.wait_ge(rstd_done, n + 1)
                for j in range(J):
                    dve.tensor_scalar(z[:, j, :], x_all[:, J * n + j, :], mean_var[:, j, 0:1], rstd[:, j:j + 1],
                                      ALU.subtract, ALU.mult).then_inc(z_done, 1)

            def split_zt(n):
                dve.wait_ge(zt_hi_done, n + 1)
                dve.tensor_tensor(zt_lo[:], even[:], zt_hi[:], ALU.subtract).then_inc(zt_lo_done, 1)

            def split_q(n):
                dve.wait_ge(q_hi_done, n + 1)
                dve.scalar_tensor_tensor(out=q3[:, :, 2 * DH:K3], in0=odd[:].rearrange("p j (h d) -> p (j h) d", d=DH),
                                         scalar=SCALE, in1=q3[:, :, 0:DH], op0=ALU.mult, op1=ALU.subtract).then_inc(q_lo_done, 1)

            def split_kv(n, j):
                dve.wait_ge(k_hi_done, J * n + j + 1)
                dve.wait_ge(v_done, J * n + j + 1)
                t = slice(j * H, (j + 1) * H)
                dve.tensor_tensor(k3[:, t, DH:2 * DH], (even, odd)[j][:, 0, :].rearrange("p (h d) -> p h d", d=DH),
                                  k3[:, t, 0:DH], ALU.subtract).then_inc(k_lo_done, 1)

            def maximum(n, h):
                dve.wait_ge(s_done, n * H + h + 1)
                dve.tensor_reduce(mx[:, :, h:h + 1], s_ps[h % R][:], AX.X, ALU.max).then_inc(max_done, 1)

            def split_max(n):
                dve.wait_ge(max_done, n * H + H)
                dve.tensor_copy(m_tok[:, :, 0:H], mx[:]).then_inc(m_hi_done, 1)
                dve.wait_ge(m_hi_done, n + 1)
                dve.tensor_tensor(m_tok[:, :, H:], mx[:], m_tok[:, :, 0:H], ALU.subtract).then_inc(m_tok_done, 1)

            def normalise(n, f):
                dve.wait_ge(o_turned, 2 * n + f + 1)
                bank = (even, odd)[f][:].rearrange("p a (j g d) -> p a j g d", j=J, g=GH)
                for j in range(J):
                    r = rden[:, j, f * H // 2:(f + 1) * H // 2].rearrange("p (a g) -> p a g", a=2)
                    dve.reciprocal(r, bank[:, :, j, :, DH]).then_inc(rden_done, 1)
                for j in range(J):
                    dve.wait_ge(rden_done, (2 * n + f) * J + j + 1)
                    r = rden[:, j, f * H // 2:(f + 1) * H // 2].rearrange("p (a g x) -> p a g x", a=2, x=1)
                    out = yn[:, j, f * H // 2:(f + 1) * H // 2, :].rearrange("p (a g) d -> p a g d", a=2)
                    dve.tensor_tensor(out, bank[:, :, j, :, 0:DH], r.broadcast_to([P, 2, GH, DH]), ALU.mult).then_inc(y_done, 1)

            def split_yt(n):
                dve.wait_ge(yt_hi_done, n + 1)
                dve.tensor_tensor(yt_lo[:], even[:], yt_hi[:], ALU.subtract).then_inc(yt_lo_done, 1)

            def add_x(n):
                dve.wait_ge(out_done, n + 1)
                xs = x_all[:, bass.ds(J * n, J), :]
                dve.tensor_tensor(xs, xs, odd[:], ALU.add).then_inc(x_done, 1)

            stat(0)
            norm(0)
            for n in range(2):
                split_zt(n)
                split_q(n)
                for j in range(J):
                    split_kv(n, j)
                if n == 0:
                    stat(1)
                    norm(1)
            for h in range(H):
                maximum(0, h)
            split_max(0)

            def body(n, u):
                for h in range(H):
                    if has(n, below=B - 2):
                        if h == 0:
                            stat(n + 2)
                        if h == 2:
                            norm(n + 2)
                    if has(n, below=B - 1):
                        for k in MAX_SLOTS.get(h, ()):
                            maximum(n + 1, k)
                        if h == 14:
                            split_max(n + 1)
                    if has(n, least=1):
                        if h == 4:
                            normalise(n - 1, 0)
                            normalise(n - 1, 1)
                        if h == 7:
                            split_yt(n - 1)
                        if h == 8:
                            add_x(n - 1)
                    if has(n, below=B - 2):
                        if h == 9:
                            split_zt(n + 2)
                        if h == 11:
                            split_q(n + 2)
                        if h in (12, 13):
                            split_kv(n + 2, h - 12)

            all_batches(dve, body)
            normalise(B - 1, 0)
            normalise(B - 1, 1)
            split_yt(B - 1)
            add_x(B - 1)
            dve.wait_ge(x_done, B)

        @block.tensor
        def _(pe):
            def banks_free(n, kinds):
                for s, v in kinds:
                    after(pe, s, v)

            def transpose_z(n):
                pe.wait_ge(z_done, J * n + J)
                after(pe, turned_read, FILLS * n)
                after(pe, yt_lo_done, n - 2)
                after(pe, m_row_done, n - 1)
                for c in range(2):
                    for j in range(J):
                        mm = pe.transpose(even[:, c, j * P:(j + 1) * P], z[:, j, c * P:(c + 1) * P], ident[:])
                mm.then_inc(zt_done, 1)

            def project_q(n):
                pe.wait_ge(zt_lo_done, n + 1)
                after(pe, turned_read, FILLS * n)
                after(pe, x_done, n - 2)
                for j in range(J):
                    cols = slice(j * P, (j + 1) * P)
                    for c in range(2):
                        mm = three_passes(pe, odd[:, j, :], (zt_hi[:, c, cols], zt_lo[:, c, cols]),
                                          (w_hi[:, c, 0:D], w_lo[:, c, 0:D]), c == 0, c == 1)
                mm.then_inc(q_done, 1)

            def project_kv(n, j):
                bank = (even, odd)[j]
                pe.wait_ge(ct_lo_done, n + 1)
                if j == 0:
                    pe.wait_ge(zt_lo_done, n + 1)
                else:
                    pe.wait_ge(q_lo_done, n + 1)
                cols = slice(j * P, (j + 1) * P)
                for c in range(2):
                    mm = three_passes(pe, bank[:].rearrange("p j d -> p (j d)"), (ct_hi[:, c, cols], ct_lo[:, c, cols]),
                                      (w_hi[:, c, D:3 * D], w_lo[:, c, D:3 * D]), c == 0, c == 1)
                mm.then_inc(kv_done, 1)

            def turn(n, f):
                if f == 0:
                    pe.wait_ge(q_lo_done, n + 1)
                    pe.wait_ge(k_lo_done, J * n + J)
                    after(pe, m_row_done, n)
                else:
                    after(pe, turned_read, FILLS * n + f - 1)
                g = f // 2
                src, bank = (q3, k3)[f % 2], (even, odd)[f % 2]
                for a in range(2):
                    for j in range(J):
                        h = j * H + 2 * (2 * g + a)
                        mm = pe.transpose(bank[:, a, j * P:(j + 1) * P],
                                          src[:, h:h + 2, :].rearrange("p h r -> p (h r)").bitcast(F32), ident[:])
                mm.then_inc(turned, 1)

            def scores(n, u, h):
                after(pe, max_done, n * H + h + 1 - R)
                pe.wait_ge(turned_read, FILLS * n + 2 * (h // 4) + 2)
                rows, pair = slice(SLOT * (h % 2), SLOT * (h % 2) + K3), h // 2
                for j in range(J):
                    mm = pe.matmul(s_ps[h % R][:, j, :], qt[u][rows, pair, j * P:(j + 1) * P], kt[u][rows, pair, :],
                                   start=True, stop=True)
                mm.then_inc(s_done, 1)

            def turn_max(n):
                pe.wait_ge(m_tok_done, n + 1)
                pe.wait_ge(turned_read, FILLS * n + FILLS)
                after(pe, yt_lo_done, n - 1)
                pe.wait_ge(k_lo_done, min(J * n + 2 * J, J * B) if isinstance(n, int) else J * n + 2 * J)
                for j in range(J):
                    mm = pe.transpose(even[0:2 * H, 0, j * P:(j + 1) * P], m_tok[:, j, :].bitcast(F32), ident[:])
                mm.then_inc(m_turned, 1)

            def shifted_scores(n, u, h):
                after(pe, exp_done, n * H + h + 1 - R)
                if h == 0:
                    pe.wait_ge(m_row_done, n + 1)
                rows, pair = slice(SLOT * (h % 2), SLOT * (h % 2) + K3), h // 2
                for i in range(J):
                    pe.matmul(t_ps[h % R][:, i, :], kt[u][rows, pair, i * P:(i + 1) * P], qt[u][rows, pair, :],
                              start=True, stop=False)
                    mm = pe.matmul(t_ps[h % R][:, i, :], sel[:, h, :], m_row[u][:], start=False, stop=True)
                mm.then_inc(t_done, 1)

            def weigh_values(n, u, h):
                pe.wait_ge(exp_done, n * H + h + 1)
                if h == 0:
                    pe.wait_ge(va_done, n + 1)
                if h % (H // 2) == 0:
                    after(pe, ot_done, 2 * (n - 1) + 2 * h // H + 1)
                out = o_ps[2 * h // H][OSLOT * (h % GH):OSLOT * (h % GH + 1), h // GH % 2, :]
                for i in range(J):
                    mm = pe.matmul(out, va[u][:, i, h, :], probs[h % PR][:, i, :], start=(i == 0), stop=(i == J - 1))
                mm.then_inc(pv_done, 1)

            def turn_outputs(n, f):
                pe.wait_ge(ot_done, 2 * n + f + 1)
                pe.wait_ge(turned_read, min(FILLS * (n + 3), FILLS * B) if isinstance(n, int) else FILLS * (n + 3))
                pe.wait_ge(m_row_done, min(n + 2, B) if isinstance(n, int) else n + 2)
                pe.wait_ge(k_lo_done, min(J * (n + 3), J * B) if isinstance(n, int) else J * (n + 3))
                after(pe, (yt_lo_done, x_done)[f], n)
                for a in range(2):
                    for j in range(J):
                        mm = pe.transpose((even, odd)[f][:, a, j * P:(j + 1) * P], ot[:, f, a, j * P:(j + 1) * P], ident[:])
                mm.then_inc(o_turned, 1)

            def transpose_y(n):
                pe.wait_ge(y_done, 2 * J * n + 2 * J)
                for c in range(2):
                    for j in range(J):
                        mm = pe.transpose(even[:, c, j * P:(j + 1) * P],
                                          yn[:, j].rearrange("p h d -> p (h d)")[:, c * P:(c + 1) * P], ident[:])
                mm.then_inc(yt_done, 1)

            def project_out(n):
                pe.wait_ge(yt_lo_done, n + 1)
                for j in range(J):
                    cols = slice(j * P, (j + 1) * P)
                    for c in range(2):
                        mm = three_passes(pe, odd[:, j, :], (yt_hi[:, c, cols], yt_lo[:, c, cols]),
                                          (w_hi[:, c, 3 * D:], w_lo[:, c, 3 * D:]), c == 0, c == 1)
                mm.then_inc(out_done, 1)

            pe.wait_ge(w_ready, 2)
            for n in range(2):
                transpose_z(n)
                project_q(n)
                for j in range(J):
                    project_kv(n, j)
                if n == 0:
                    for f in range(FILLS):
                        turn(0, f)
            for h in range(H):
                scores(0, 0, h)
            turn_max(0)

            def body(n, u):
                for h in range(H):
                    shifted_scores(n, u, h)
                    if h >= LAG:
                        weigh_values(n, u, h - LAG)
                    elif has(n, least=1):
                        weigh_values(n - 1, 1 - u, H - LAG + h)
                    if has(n, below=B - 1):
                        if h < FILLS // 2:
                            turn(n + 1, 2 * h)
                            turn(n + 1, 2 * h + 1)
                        for k in MAX_SLOTS.get(h, ()):
                            scores(n + 1, 1 - u, k)
                    if has(n, least=1):
                        if h == 4:
                            turn_outputs(n - 1, 0)
                            turn_outputs(n - 1, 1)
                        if h == 6:
                            transpose_y(n - 1)
                        if h == 8:
                            project_out(n - 1)
                    if has(n, below=B - 2):
                        if h == 8:
                            transpose_z(n + 2)
                        if h == 10:
                            project_q(n + 2)
                        if h in (11, 12):
                            project_kv(n + 2, h - 11)
                    if has(n, below=B - 1) and h == 15:
                        turn_max(n + 1)

            all_batches(pe, body)
            for h in range(H - LAG, H):
                weigh_values(B - 1, (B - 1) % R, h)
            turn_outputs(B - 1, 0)
            turn_outputs(B - 1, 1)
            transpose_y(B - 1)
            project_out(B - 1)


def moe_sizes(x_all, router_w, w1_in):
    class S:
        D, E, NE, FF = 256, router_w.shape[2], w1_in.shape[0], w1_in.shape[3]
        TILES = x_all.shape[1]
        T = 2
        TOK = T * P
        CHUNKS = TILES // T
        KD, KF = D // P, FF // P
        TOP = 2
        ROWS = (TILES + 1) * P
        PAIR_TILES = TOP * TILES + E - 1
        BIAS_LO = 32
        BIAS_ROWS = BIAS_LO + NE
    return S


def pipeline(engine, count, order, parts, head=3):
    offsets = [offset for _, offset in order]
    loops = (count - max(offsets) - head) // 2

    def step(n, u):
        for name, offset in order:
            if name in parts and not (isinstance(n, int) and not 0 <= n + offset < count):
                parts[name](n + offset, (u + offset) % 2)

    for n in range(-max(offsets), head):
        step(n, n % 2)
    with engine.Fori(0, loops) as i:
        for k in range(2):
            step(2 * i + (head + k), (head + k) % 2)
    for n in range(head + 2 * loops, count - min(offsets)):
        step(n, n % 2)


def phase_moe(nc, x_all, tanh_g, ident, half_neg, passed, router_w, router_b, w1_in, b1_in, b1_rows, w2_in, b2_in, out):
    S = moe_sizes(x_all, router_w, w1_in)
    z_rows = nc.dram_tensor("d_z_rows", [(S.E + 1) * S.ROWS, S.D], F32, kind="Internal").ap()
    y_rows = nc.dram_tensor("d_y_rows", [S.PAIR_TILES * P, S.D], F32, kind="Internal").ap()
    zt_kept = nc.dram_tensor("d_zt_kept", [S.CHUNKS, P, 2, S.KD * S.TOK], F32, kind="Internal").ap()
    with ExitStack() as ctx:
        def sb(name, shape, dt=F32):
            return ctx.enter_context(nc.sbuf_tensor("d_" + name, shape, dt))

        class M:
            prob = sb("prob", [P, S.TILES, S.TOP])
            pos = sb("pos", [P, S.TILES, S.TOP], mybir.dt.int32)
            count = sb("count", [P, S.E])
            tiles_at = sb("tiles_at", [1, 2, S.PAIR_TILES], mybir.dt.int32)
            own = sb("own", [S.BIAS_ROWS, S.PAIR_TILES])
            bias1, bias2 = sb("bias1", [S.BIAS_ROWS, S.FF], F32R), sb("bias2", [S.BIAS_ROWS, S.D], F32R)
            ones = sb("ones", [S.BIAS_ROWS, P])
            shared_row = sb("shared_row", [S.BIAS_ROWS, S.NE - S.E, P], F32R)
            rows_of = sb("rows_of", [S.BIAS_ROWS, S.NE])
            half_tanh = sb("half_tanh", [P, 1])
            w1_lo, w2_lo = sb("w1_lo", [P, S.E, S.KD, S.FF], F32R), sb("w2_lo", [P, S.E, S.KF, S.D], F32R)
            experts_loaded = ctx.enter_context(nc.semaphore("d_experts_loaded"))

        moe_route(nc, S, M, x_all, tanh_g, ident, half_neg, passed, router_w, router_b, w1_in, b1_in, b1_rows, w2_in, b2_in,
                  z_rows, zt_kept)
        moe_experts(nc, S, M, ident, passed, z_rows, y_rows)
        moe_combine(nc, S, M, x_all, passed, w1_in, b1_in, w2_in, zt_kept, y_rows, out)


def moe_route(nc, S, M, x_all, tanh_g, ident, half_neg, passed, router_w, router_b, w1_in, b1_in, b1_rows, w2_in, b2_in,
              z_rows, zt_kept):
    E, NE, KD, KF, FF, D, T, TOK, TOP = S.E, S.NE, S.KD, S.KF, S.FF, S.D, S.T, S.TOK, S.TOP
    HR, GR = 4, 4
    I32 = mybir.dt.int32
    ORDER = (("hidden", 0), ("turn", 1), ("rank", 0), ("output0", -1), ("output1", -1), ("gates", 1), ("stats", 2), ("norm", 2))
    with ExitStack() as ctx:
        def sb(name, shape, dt=F32):
            return ctx.enter_context(nc.sbuf_tensor("dr_" + name, shape, dt))

        sem = cleared_semaphores(nc, ctx, "dr_")

        def ps(name, shape):
            return ctx.enter_context(nc.psum_tensor("dr_" + name, shape, F32))

        zt_hi, zt_lo = [sb(f"zt_hi{u}", [P, KD, TOK], F32R) for u in range(2)], [sb(f"zt_lo{u}", [P, KD, TOK], F32R) for u in range(2)]
        rw_raw = sb("rw_raw", [P, KD, E])
        rw_hi, rw_lo = sb("rw_hi", [P, KD, E], F32R), sb("rw_lo", [P, KD, E], F32R)
        rb = sb("rb", [P, E])
        b1 = sb("b1", [P, NE, KF])
        b_raw1, b_raw2 = sb("b_raw1", [S.BIAS_ROWS, FF]), sb("b_raw2", [S.BIAS_ROWS, D])
        expert = sb("expert", [P, E])
        above = sb("above", [P, 2, P], BF16)
        stats, mean_var, rstd = sb("stats", [P, T, 6]), sb("mean_var", [P, T, 2]), sb("rstd", [P, T])
        z = [sb(f"z{u}", [P, T, D]) for u in range(2)]
        gates, top = sb("gates", [P, T, E]), sb("top", [P, T, 8])
        top_i, top_f = sb("top_i", [P, T, 8], mybir.dt.uint32), sb("top_f", [P, T, TOP])
        pick = sb("pick", [P, T, TOP, E])
        both = sb("both", [P, T, E], BF16)
        row, row_k = sb("row", [P, T, E]), sb("row_k", [P, T, TOP, E])
        pos_f = sb("pos_f", [P, T, TOP])
        pos_all, past_region = sb("pos_all", [P, S.TILES, TOP]), sb("past_region", [P, E, S.TILES, TOP])
        pos_u = [[sb(f"pos_u{u}_{k}", [P, 1], I32) for k in range(T * TOP)] for u in range(2)]
        diff, den = sb("diff", [P, S.TILES]), sb("den", [P, S.TILES])
        w1_raw, w2_raw = sb("w1_raw", [P, KD, FF]), sb("w2_raw", [P, KF, D])
        w1_hi, w1_lo = sb("w1_hi", [P, KD, FF], F32R), sb("w1_lo", [P, KD, FF], F32R)
        w2_hi, w2_lo = sb("w2_hi", [P, KF, D], F32R), sb("w2_lo", [P, KF, D], F32R)
        g_full = sb("g_full", [P, GR, TOK])
        g_hi, g_lo = [sb(f"g_hi{u}", [P, KF, TOK], F32R) for u in range(2)], [sb(f"g_lo{u}", [P, KF, TOK], F32R) for u in range(2)]
        zeros = sb("zeros", [P, D])
        tile_no = sb("tile_no", [S.BIAS_ROWS, S.PAIR_TILES])
        cnt, tiles, ends = sb("cnt", [P, E]), sb("tiles", [P, E]), sb("ends", [P, E + 1])
        base, base_step = sb("base", [P, E + 1]), sb("base_step", [P, E])
        mine, bounds = sb("mine", [S.BIAS_ROWS, 2, E]), sb("bounds", [S.BIAS_ROWS, 2])
        past = sb("past", [1, E, S.PAIR_TILES])
        tab = sb("tab", [1, 2, S.PAIR_TILES])
        own_b = sb("own_b", [S.BIAS_ROWS, S.PAIR_TILES])
        zero1 = sb("zero1", [P, E])
        pad_f, pad_i = sb("pad_f", [P, E + 1]), [sb(f"pad_i{e}", [P, 1], I32) for e in range(E + 1)]
        lane = sb("lane", [P, 1])

        hid = [ps(f"hid{i}", [P, 512]) for i in range(HR)]
        y = [ps(f"y{i}", [P, 512]) for i in range(T)]
        zt_ps = ps("zt_ps", [P, KD, TOK])
        r_ps = ps("r_ps", [P, 512])
        rank_ps = r_ps[:, 256:512]

        small_loaded, shared_loaded, ready = sem("small_loaded"), sem("shared_loaded"), sem("ready")
        pool_ready, act_ready, setup_chain = sem("pool_ready"), sem("act_ready"), sem("setup_chain")
        stats_done, mv_done, var_eps, rstd_done = sem("stats_done"), sem("mv_done"), sem("var_eps"), sem("rstd_done")
        z_done, zt_done, zt_hi_done, zt_lo_done = sem("z_done"), sem("zt_done"), sem("zt_hi_done"), sem("zt_lo_done")
        gates_done, both_done, rank_done, pos_done, pos_kept = sem("gates_done"), sem("both_done"), sem("rank_done"), sem("pos_done"), sem("pos_kept")
        route, ranked = sem("route"), sem("ranked")
        hid_done, gelu_hi, gelu_full, gelu_lo = sem("hid_done"), sem("gelu_hi"), sem("gelu_full"), sem("gelu_lo")
        y_done, x_added = sem("y_done"), sem("x_added")
        scattered = [sem(f"scattered{u}") for u in range(2)]
        zt_stored = [sem(f"zt_stored{u}") for u in range(2)]
        padded = sem("padded")
        diff_done, exp_done, last, pads_done = sem("diff_done"), sem("exp_done"), sem("last"), sem("pads_done")
        block = ctx.enter_context(nc.Block())

        def before(n, u, per):
            return per * (n // 2) if isinstance(n, int) else per // 2 * (n - u)

        @block.sync
        def _(sync):
            for dst, src in ((rw_raw[:], router_w), (b1[:], b1_in), (rb[:], router_b.partition_broadcast(P))):
                sync.dma_start(dst, src).then_inc(small_loaded, 16)
            sync.dma_start(w1_raw[:], w1_in[E]).then_inc(shared_loaded, 16)
            sync.dma_start(w2_raw[:], w2_in[E]).then_inc(shared_loaded, 16)
            sync.wait_ge(pool_ready, 1)
            for at in (0, S.BIAS_LO):
                sync.dma_start(b_raw1[at:at + NE, :], b1_rows).then_inc(small_loaded, 16)
                sync.dma_start(b_raw2[at:at + NE, :], b2_in).then_inc(small_loaded, 16)
            for e in range(E):
                sync.dma_start(M.w1_lo[:, e].bitcast(F32), w1_in[e]).then_inc(M.experts_loaded, 16)
                sync.dma_start(M.w2_lo[:, e].bitcast(F32), w2_in[e]).then_inc(M.experts_loaded, 16)

            def keep(n, u):
                sync.wait_ge(zt_lo_done, n + 1)
                for k, part in enumerate((zt_hi, zt_lo)):
                    dst = zt_kept[bass.ds(n, 1), :, k].rearrange("n p f -> p (n f)")
                    sync.dma_start(dst, part[u][:].rearrange("p c t -> p (c t)").bitcast(F32)).then_inc(zt_stored[u], 16)

            with sync.Fori(0, S.CHUNKS // 2) as i:
                for u in range(2):
                    keep(2 * i + u, u)
            for u in range(2):
                sync.wait_ge(zt_stored[u], 32 * S.CHUNKS // 2)

        @block.gpsimd
        def _(pool):
            pool.memset(b_raw1[:], 0.0)
            pool.memset(b_raw2[:], 0.0).then_inc(pool_ready, 1)
            pool.memset(above[:], 1.0).then_inc(pool_ready, 1)
            pool.memset(zeros[:], 0.0)
            pool.memset(M.ones[:], 1.0)
            pool.iota(expert[:], pattern=[[1, E]], base=0, channel_multiplier=0, allow_small_or_imprecise_dtypes=True)
            pool.iota(M.count[:], pattern=[[S.ROWS, E]], base=0, channel_multiplier=0, allow_small_or_imprecise_dtypes=True)
            pool.iota(base[:], pattern=[[S.ROWS, E + 1]], base=0, channel_multiplier=0, allow_small_or_imprecise_dtypes=True)
            pool.iota(tile_no[:], pattern=[[1, S.PAIR_TILES]], base=0, channel_multiplier=0, allow_small_or_imprecise_dtypes=True)
            pool.iota(lane[:], pattern=[[0, 1]], base=0, channel_multiplier=1, allow_small_or_imprecise_dtypes=True)
            pool.wait_ge(pool_ready, 2)
            pool.affine_select(out=above[:, 0, :], in_=above[:, 0, :], compare_op=ALU.is_gt, fill=0.0, base=0,
                               pattern=[[1, P]], channel_multiplier=-1).then_inc(pool_ready, 1)

            def stats_part(n, u):
                alone(pool, mv_done, T * (n + 1), passed)
                pool.tensor_scalar(rstd[:], mean_var[:, :, 1:2].rearrange("p t a -> p (t a)"), LN_EPS, None, ALU.add).then_inc(var_eps, 1)
                pool.wait_ge(var_eps, n + 1)
                pool.tensor_tensor(rstd[:], rstd[:], half_neg[:, 0:T], ALU.pow).then_inc(rstd_done, 1)

            def scatter(n, u):
                alone(pool, pos_done, n + 1, passed)
                for k in range(T * TOP):
                    pool.indirect_dma_start(z_rows, bass.IndirectOffsetOnAxis(ap=pos_u[u][k][:], axis=0),
                                            z[u][:, k // TOP, :], None).then_inc(scattered[u], 16)

            pipeline(pool, S.CHUNKS, ORDER, {"stats": stats_part, "rank": scatter})
            pool.wait_ge(pads_done, E + 1)
            for e in range(E + 1):
                pool.indirect_dma_start(z_rows, bass.IndirectOffsetOnAxis(ap=pad_i[e][:], axis=0), zeros[:],
                                        None).then_inc(padded, 16)
            pool.wait_ge(padded, 16 * (E + 1))
            for u in range(2):
                pool.wait_ge(scattered[u], 16 * T * TOP * S.CHUNKS // 2)

        @block.scalar
        def _(act):
            act.wait_ge(small_loaded, 112)
            act.activation(M.bias1[:], b_raw1[:], ACT.Copy).then_inc(act_ready, 1)
            act.activation(M.bias2[:], b_raw2[:], ACT.Copy).then_inc(act_ready, 1)
            act.wait_ge(shared_loaded, 32)
            act.activation(w1_hi[:], w1_raw[:], ACT.Copy).then_inc(act_ready, 1)
            act.activation(w2_hi[:], w2_raw[:], ACT.Copy).then_inc(act_ready, 1)

            def hidden(n, u):
                for m in range(KF):
                    act.wait_ge(hid_done, n * KF + m + 1)
                    alone(act, gelu_lo, n * KF + m + 1 - GR, passed)
                    if m == 0:
                        after(act, y_done, T * (n - 1))
                    act.activation(g_full[:, m % GR, :], hid[m % HR][:, 0:TOK], ACT.Gelu, bias=b1[:, E, m:m + 1]).then_inc(gelu_full, 1)
                    act.activation(g_hi[u][:, m, :], hid[m % HR][:, 0:TOK], ACT.Gelu, bias=b1[:, E, m:m + 1]).then_inc(gelu_hi, 1)

            def turn(n, u):
                act.wait_ge(zt_done, n + 1)
                after(act, zt_stored[u], before(n, u, 32))
                after(act, hid_done, KF * (n - 1))
                act.activation(zt_hi[u][:], zt_ps[:], ACT.Copy).then_inc(zt_hi_done, 1)

            pipeline(act, S.CHUNKS, ORDER, {"hidden": hidden, "turn": turn})
            act.wait_ge(diff_done, S.CHUNKS)
            act.activation(den[:], diff[:], ACT.Exp).then_inc(exp_done, 1)

        @block.vector
        def _(dve):
            dve.wait_ge(small_loaded, 112)
            dve.tensor_copy(rw_hi[:], rw_raw[:]).then_inc(ready, 1)
            dve.wait_ge(ready, 1)
            dve.tensor_tensor(rw_lo[:], rw_raw[:], rw_hi[:], ALU.subtract).then_inc(ready, 1)
            dve.wait_ge(act_ready, 4)
            lo = slice(S.BIAS_LO, S.BIAS_ROWS)
            dve.tensor_tensor(M.bias1[lo, :], b_raw1[lo, :], M.bias1[lo, :], ALU.subtract).then_inc(ready, 1)
            dve.tensor_tensor(M.bias2[lo, :], b_raw2[lo, :], M.bias2[lo, :], ALU.subtract).then_inc(ready, 1)
            dve.tensor_tensor(w1_lo[:], w1_raw[:], w1_hi[:], ALU.subtract).then_inc(ready, 1)
            dve.tensor_tensor(w2_lo[:], w2_raw[:], w2_hi[:], ALU.subtract).then_inc(ready, 1)
            dve.tensor_scalar(M.half_tanh[:], tanh_g[:, 3:4], 1.0 / (NE - E), None, ALU.mult).then_inc(ready, 1)
            dve.memset(zero1[:], 0.0).then_inc(ready, 1)
            n_rows = S.BIAS_ROWS
            dve.tensor_tensor(M.rows_of[:], ident[0:n_rows, 0:NE], ident[0:n_rows, S.BIAS_LO:S.BIAS_LO + NE], ALU.add).then_inc(ready, 1)
            dve.wait_ge(ready, 9)
            dve.wait_ge(pool_ready, 3)
            for k in range(NE - E):
                dve.tensor_scalar(M.shared_row[:, k, :], M.ones[:], M.rows_of[:, E + k:E + k + 1], None, ALU.mult).then_inc(ready, 1)
            dve.wait_ge(ready, 9 + NE - E)
            step, after_pick = Chain(dve, route, 5, passed), Chain(dve, ranked, 2 + 2 * T, passed)

            def hidden(n, u):
                for m in range(KF):
                    dve.wait_ge(gelu_hi, n * KF + m + 1)
                    dve.wait_ge(gelu_full, n * KF + m + 1)
                    dve.tensor_tensor(g_lo[u][:, m, :], g_full[:, m % GR, :], g_hi[u][:, m, :], ALU.subtract).then_inc(gelu_lo, 1)

            def stats_part(n, u):
                for t in range(T):
                    dve.bn_stats(stats[:, t, :], x_all[:, T * n + t, :]).then_inc(stats_done, 1)
                alone(dve, stats_done, T * (n + 1), passed)
                for t in range(T):
                    dve.bn_aggr(mean_var[:, t, :], stats[:, t, :]).then_inc(mv_done, 1)

            def norm(n, u):
                alone(dve, scattered[u], before(n, u, 16 * T * TOP), passed)
                dve.wait_ge(rstd_done, n + 1)
                for t in range(T):
                    dve.tensor_scalar(z[u][:, t, :], x_all[:, T * n + t, :], mean_var[:, t, 0:1], rstd[:, t:t + 1],
                                      ALU.subtract, ALU.mult).then_inc(z_done, 1)

            def turn(n, u):
                dve.wait_ge(zt_hi_done, n + 1)
                dve.tensor_tensor(zt_lo[u][:], zt_ps[:], zt_hi[u][:], ALU.subtract).then_inc(zt_lo_done, 1)

            def gates_part(n, u):
                step.begin(n)
                dve.wait_ge(gates_done, n + 1)
                step(dve.tensor_tensor(gates[:], r_ps[:, 0:T * E].rearrange("p (t e) -> p t e", t=T),
                                       rb[:].rearrange("p (a e) -> p a e", a=1).broadcast_to([P, T, E]), ALU.add))
                for t in range(T):
                    ins = dve.max(top[:, t, :], gates[:, t, :])
                step(ins)
                for t in range(T):
                    ins = dve.max_index(top_i[:, t, :], top[:, t, :], gates[:, t, :])
                step(ins)
                step(dve.tensor_copy(top_f[:], top_i[:, :, 0:TOP]))
                dve.tensor_tensor(diff[:, bass.ds(T * n, T)], top[:, :, 1:2].rearrange("p t a -> p (t a)"),
                                  top[:, :, 0:1].rearrange("p t a -> p (t a)"), ALU.subtract).then_inc(diff_done, 1)
                step(dve.tensor_tensor(pick[:], expert[:].rearrange("p (a b e) -> p a b e", a=1, b=1).broadcast_to([P, T, TOP, E]),
                                       top_f[:].rearrange("p t (k a) -> p t k a", a=1).broadcast_to([P, T, TOP, E]), ALU.is_equal))
                dve.tensor_tensor(both[:], pick[:, :, 0, :], pick[:, :, 1, :], ALU.add).then_inc(both_done, 1)

            def rank(n, u):
                after_pick.begin(n)
                dve.wait_ge(rank_done, n + 1)
                for t in range(T):
                    after_pick(dve.tensor_tensor(row[:, t, :], rank_ps[:, t * E:(t + 1) * E], M.count[:], ALU.add))
                    after_pick(dve.tensor_tensor(M.count[:], M.count[:], rank_ps[:, (T + t) * E:(T + t + 1) * E], ALU.add))
                after_pick(dve.tensor_tensor(row_k[:], pick[:], row[:].rearrange("p t (a e) -> p t a e", a=1).broadcast_to([P, T, TOP, E]), ALU.mult))
                after_pick(dve.tensor_reduce(pos_f[:], row_k[:], AX.X, ALU.add))
                for k in range(T * TOP):
                    ins = dve.tensor_copy(pos_u[u][k][:], pos_f[:, k // TOP, k % TOP:k % TOP + 1])
                ins.then_inc(pos_done, 1)
                dve.tensor_copy(pos_all[:, bass.ds(T * n, T), :], pos_f[:]).then_inc(pos_kept, 1)

            def output(t, n):
                dve.wait_ge(y_done, T * n + t + 1)
                xs = x_all[:, T * n + t, :]
                dve.scalar_tensor_tensor(out=xs, in0=y[t][:, 0:D], scalar=M.half_tanh[:, 0:1], in1=xs, op0=ALU.mult, op1=ALU.add).then_inc(x_added, 1)

            pipeline(dve, S.CHUNKS, ORDER, {
                "stats": stats_part, "norm": norm, "turn": turn, "gates": gates_part, "rank": rank, "hidden": hidden,
                "output0": lambda n, u: output(0, n), "output1": lambda n, u: output(1, n)})
            dve.wait_ge(pos_kept, S.CHUNKS)
            dve.wait_ge(x_added, S.TILES)
            dve.wait_ge(exp_done, 1)

            chain = Chain(dve, last, 40)
            chain.begin(0)
            second = M.prob[:, :, 1:2].rearrange("p t a -> p (t a)")
            first = M.prob[:, :, 0:1].rearrange("p t a -> p (t a)")
            chain(dve.tensor_scalar(diff[:], den[:], 1.0, None, ALU.add))
            chain(dve.reciprocal(diff[:], diff[:]))
            chain(dve.tensor_scalar(first, diff[:], tanh_g[:, 3:4], None, ALU.mult))
            chain(dve.tensor_tensor(second, first, den[:], ALU.mult))
            chain(dve.tensor_scalar(pad_f[:, 0:E], M.count[:], lane[:, 0:1], None, ALU.add))
            dve.tensor_scalar(pad_f[:, E:E + 1], lane[:], float(E * S.ROWS), None, ALU.add)
            chain(dve.tensor_scalar(cnt[:], expert[:], float(S.ROWS), None, ALU.mult))
            for e in range(E + 1):
                dve.tensor_copy(pad_i[e][:], pad_f[:, e:e + 1]).then_inc(pads_done, 1)
            chain(dve.tensor_tensor(cnt[:], M.count[:], cnt[:], ALU.subtract))
            chain(dve.tensor_scalar(tiles[:], cnt[:], 1.0 / P, (P - 1.0) / P - 0.5 + 0.5 / P, ALU.mult, ALU.add))
            chain(dve.tensor_scalar(tiles[:], tiles[:], ROUND, ROUND, ALU.add, ALU.subtract))
            chain(dve.tensor_copy(ends[:, 0:1], zero1[:, 0:1]))
            chain(dve.tensor_tensor_scan(ends[:, 1:E + 1], tiles[:], zero1[:], 0.0, ALU.add, ALU.add))
            for e in range(E):
                ins = dve.tensor_scalar(past[:, e, :], tile_no[0:1, :], ends[0:1, e + 1:e + 2], None, ALU.is_ge)
            chain(ins)
            chain(dve.scalar_tensor_tensor(out=base[:, 0:E], in0=ends[:, 0:E], scalar=-float(P), in1=base[:, 0:E], op0=ALU.mult, op1=ALU.add))
            chain(dve.tensor_tensor(base_step[:], base[:, 1:E + 1], base[:, 0:E], ALU.subtract))
            dve.tensor_scalar(tab[:, 1, :], tile_no[0:1, :], float(P), None, ALU.mult)
            for e in range(1, E):
                dve.tensor_scalar(past_region[:, e], pos_all[:], float(e * S.ROWS), base_step[:, e - 1:e], ALU.is_ge, ALU.mult)
            chain(dve.tensor_copy(tab[:, 0, :], past[:, 0, :]))
            for e in range(E):
                if e > 0:
                    dve.tensor_tensor(tab[:, 0, :], tab[:, 0, :], past[:, e, :], ALU.add)
                    dve.tensor_tensor(pos_all[:], pos_all[:], past_region[:, e], ALU.subtract)
                chain(dve.scalar_tensor_tensor(out=tab[:, 1, :], in0=past[:, e, :], scalar=base_step[0:1, e:e + 1], in1=tab[:, 1, :],
                                               op0=ALU.mult, op1=ALU.add))
            dve.tensor_copy(M.pos[:], pos_all[:])
            chain(dve.scalar_tensor_tensor(out=past[:, 0, :], in0=tile_no[0:1, :], scalar=-float(P), in1=past[:, E - 1, :], op0=ALU.mult, op1=ALU.mult))
            chain(dve.tensor_tensor(tab[:, 1, :], tab[:, 1, :], past[:, 0, :], ALU.add))
            chain(dve.tensor_scalar(tab[:, 0, :], tab[:, 0, :], float(E - 1), None, ALU.min))
            chain(dve.tensor_copy(M.tiles_at[:], tab[:]))
            for k in range(2):
                ins = dve.tensor_tensor(mine[:, k, :], M.rows_of[:, 0:E], ends[0:n_rows, k:k + E], ALU.mult)
            chain(ins)
            chain(dve.tensor_reduce(bounds[:], mine[:], AX.X, ALU.add))
            dve.tensor_scalar(own_b[:], tile_no[:], bounds[:, 1:2], None, ALU.is_ge)
            chain(dve.tensor_scalar(M.own[:], tile_no[:], bounds[:, 0:1], None, ALU.is_ge))
            chain(dve.tensor_tensor(M.own[:], M.own[:], own_b[:], ALU.subtract))

        @block.tensor
        def _(pe):
            pe.wait_ge(ready, 9 + NE - E)

            def hidden(n, u):
                for m in range(KF):
                    after(pe, gelu_hi, n * KF + m + 1 - HR)
                    cols = slice(m * P, (m + 1) * P)
                    for c in range(KD):
                        mm = three_passes(pe, hid[m % HR][:, 0:TOK], (w1_hi[:, c, cols], w1_lo[:, c, cols]),
                                          (zt_hi[u][:, c, :], zt_lo[u][:, c, :]), c == 0, c == KD - 1)
                    mm.then_inc(hid_done, 1)

            def turn(n, u):
                pe.wait_ge(z_done, T * (n + 1))
                after(pe, zt_lo_done, n)
                for t in range(T):
                    for c in range(KD):
                        mm = pe.transpose(zt_ps[:, c, t * P:(t + 1) * P], z[u][:, t, c * P:(c + 1) * P], ident[:])
                mm.then_inc(zt_done, 1)

            def gates_part(n, u):
                pe.wait_ge(zt_lo_done, n + 1)
                after(pe, pos_done, n)
                for t in range(T):
                    cols = slice(t * P, (t + 1) * P)
                    for c in range(KD):
                        mm = three_passes(pe, r_ps[:, t * E:(t + 1) * E], (zt_hi[u][:, c, cols], zt_lo[u][:, c, cols]),
                                          (rw_hi[:, c, :], rw_lo[:, c, :]), c == 0, c == KD - 1)
                mm.then_inc(gates_done, 1)

            def rank(n, u):
                pe.wait_ge(both_done, n + 1)
                for k in range(2):
                    mm = pe.matmul(rank_ps[:, k * T * E:(k + 1) * T * E], above[:, k, :], both[:].rearrange("p t e -> p (t e)"),
                                   start=True, stop=True)
                mm.then_inc(rank_done, 1)

            def output(t, n, u):
                if t == 0:
                    pe.wait_ge(gelu_lo, (n + 1) * KF)
                after(pe, x_added, T * (n - 1) + t + 1)
                cols = slice(t * P, (t + 1) * P)
                for m in range(KF):
                    three_passes(pe, y[t][:, 0:D], (g_hi[u][:, m, cols], g_lo[u][:, m, cols]),
                                 (w2_hi[:, m, :], w2_lo[:, m, :]), m == 0, False)
                pe.matmul(y[t][:, 0:D], M.shared_row[:, 0, :], M.bias2[:], start=False, stop=True).then_inc(y_done, 1)

            pipeline(pe, S.CHUNKS, ORDER, {"turn": turn, "gates": gates_part, "rank": rank, "hidden": hidden,
                                           "output0": lambda n, u: output(0, n, u), "output1": lambda n, u: output(1, n, u)})


def moe_experts(nc, S, M, ident, passed, z_rows, y_rows):
    E, KD, KF, FF, D = S.E, S.KD, S.KF, S.FF, S.D
    ORDER = (("turn", 0), ("first", 1), ("turn_in", 2), ("second", 0))
    with ExitStack() as ctx:
        def sb(name, shape, dt=F32):
            return [ctx.enter_context(nc.sbuf_tensor(f"de_{name}{u}", shape, dt)) for u in range(2)]

        def ps(name, shape):
            return [ctx.enter_context(nc.psum_tensor(f"de_{name}{u}", shape, F32)) for u in range(2)]

        sem = cleared_semaphores(nc, ctx, "de_")

        w1_hi = ctx.enter_context(nc.sbuf_tensor("de_w1_hi", [P, E, KD, FF], F32R))
        w2_hi = ctx.enter_context(nc.sbuf_tensor("de_w2_hi", [P, E, KF, D], F32R))
        z = sb("z", [P, D])
        own = sb("own", [S.BIAS_ROWS, P], F32R)
        zt_hi, zt_lo = sb("zt_hi", [P, KD, P], F32R), sb("zt_lo", [P, KD, P], F32R)
        g = sb("g", [P, FF])
        gt_hi, gt_lo = sb("gt_hi", [P, KF, P], F32R), sb("gt_lo", [P, KF, P], F32R)
        ys = sb("ys", [P, D])
        h_ps, gt_ps, zt_ps, y_ps = ps("h_ps", [P, FF]), ps("gt_ps", [P, KF, P]), ps("zt_ps", [P, 512]), ps("y_ps", [P, 512])
        z_loaded, stored = [sem(f"z_loaded{u}") for u in range(2)], [sem(f"stored{u}") for u in range(2)]
        hi_done, lo_done = sem("hi_done"), sem("lo_done")
        zt_done, zt_hi_done, zt_lo_done = sem("zt_done"), sem("zt_hi_done"), sem("zt_lo_done")
        own_done, h_done, g_done = sem("own_done"), sem("h_done"), sem("g_done")
        gt_done, gt_hi_done, gt_lo_done = sem("gt_done"), sem("gt_hi_done"), sem("gt_lo_done")
        y_done, y_copied = sem("y_done"), sem("y_copied")
        block = ctx.enter_context(nc.Block())

        def before_last(i, u):
            return 16 * (i // 2) if isinstance(i, int) else 8 * (i - u)

        @block.sync
        def _(sync):
            def store(i, u):
                sync.wait_ge(y_copied, i + 1)
                sync.dma_start(y_rows[bass.ds(i * P, P), :], ys[u][:]).then_inc(stored[u], 16)

            pipeline(sync, S.PAIR_TILES, ORDER, {"second": store})
            for u in range(2):
                sync.wait_ge(stored[u], 16 * ((S.PAIR_TILES + 1 - u) // 2))

        @block.gpsimd
        def _(pool):
            def load(i, u):
                alone(pool, zt_done, i - 1, passed)
                row = pool.value_load(M.tiles_at[:, 1, bass.ds(i, 1)], min_val=0, max_val=(E + 1) * S.ROWS - P)
                pool.dma_start(z[u][:], z_rows[bass.ds(row, P), :]).then_inc(z_loaded[u], 16)

            pipeline(pool, S.PAIR_TILES, ORDER, {"turn_in": load})

        @block.scalar
        def _(act):
            act.wait_ge(M.experts_loaded, 32 * E)
            for e in range(E):
                act.activation(w1_hi[:, e], M.w1_lo[:, e].bitcast(F32), ACT.Copy).then_inc(hi_done, 1)
                act.activation(w2_hi[:, e], M.w2_lo[:, e].bitcast(F32), ACT.Copy).then_inc(hi_done, 1)

            def turn_in(i, u):
                act.wait_ge(zt_done, i + 1)
                after(act, h_done, i - 1)
                act.activation(zt_hi[u][:].rearrange("p c t -> p (c t)"), zt_ps[u][:, 0:D], ACT.Copy).then_inc(zt_hi_done, 1)

            def first(i, u):
                act.wait_ge(h_done, i + 1)
                after(act, gt_done, i - 1)
                act.activation(g[u][:], h_ps[u][:], ACT.Gelu).then_inc(g_done, 1)

            def turn(i, u):
                act.wait_ge(gt_done, i + 1)
                after(act, y_done, i - 1)
                act.activation(gt_hi[u][:], gt_ps[u][:], ACT.Copy).then_inc(gt_hi_done, 1)

            pipeline(act, S.PAIR_TILES, ORDER, {"turn": turn, "first": first, "turn_in": turn_in})

        @block.vector
        def _(dve):
            for e in range(E):
                dve.wait_ge(hi_done, 2 * e + 2)
                for hi, lo in ((w1_hi, M.w1_lo), (w2_hi, M.w2_lo)):
                    dve.tensor_tensor(lo[:, e], lo[:, e].bitcast(F32), hi[:, e], ALU.subtract).then_inc(lo_done, 1)

            def turn_in(i, u):
                dve.wait_ge(zt_hi_done, i + 1)
                dve.tensor_tensor(zt_lo[u][:].rearrange("p c t -> p (c t)"), zt_ps[u][:, 0:D],
                                  zt_hi[u][:].rearrange("p c t -> p (c t)"), ALU.subtract).then_inc(zt_lo_done, 1)

            def turn(i, u):
                dve.wait_ge(gt_hi_done, i + 1)
                dve.tensor_tensor(gt_lo[u][:], gt_ps[u][:], gt_hi[u][:], ALU.subtract).then_inc(gt_lo_done, 1)

            def second(i, u):
                dve.wait_ge(y_done, i + 1)
                after(dve, stored[u], before_last(i, u))
                dve.tensor_copy(ys[u][:], y_ps[u][:, 0:D]).then_inc(y_copied, 1)
                if not (isinstance(i, int) and i + 2 >= S.PAIR_TILES):
                    pick_biases(i + 2, u)

            def pick_biases(i, u):
                after(dve, y_done, i - 1)
                dve.tensor_scalar(own[u][:], M.ones[:], M.own[:, bass.ds(i, 1)], None, ALU.mult).then_inc(own_done, 1)

            for i in range(2):
                pick_biases(i, i)
            pipeline(dve, S.PAIR_TILES, ORDER, {"turn": turn, "turn_in": turn_in, "second": second})

        @block.tensor
        def _(pe):
            def turn_in(i, u):
                after(pe, zt_lo_done, i - 1)
                pe.wait_ge(z_loaded[u], before_last(i, u) + 16)
                for c in range(KD):
                    mm = pe.transpose(zt_ps[u][:, c * P:(c + 1) * P], z[u][:, c * P:(c + 1) * P], ident[:])
                mm.then_inc(zt_done, 1)

            def expert(i):
                return pe.value_load(M.tiles_at[:, 0, bass.ds(i, 1)], min_val=0, max_val=E - 1)

            def first(i, u):
                if isinstance(i, int) and i == 0:
                    pe.wait_ge(lo_done, 2 * E)
                e = expert(i)
                after(pe, g_done, i - 1)
                pe.wait_ge(zt_lo_done, i + 1)
                for c in range(KD):
                    hi, lo = [w[:, bass.ds(e, 1), c, :].rearrange("p e f -> p (e f)") for w in (w1_hi, M.w1_lo)]
                    three_passes(pe, h_ps[u][:], (zt_hi[u][:, c, :], zt_lo[u][:, c, :]), (hi, lo), c == 0, False)
                pe.wait_ge(own_done, i + 1)
                pe.matmul(h_ps[u][:], own[u][:], M.bias1[:], start=False, stop=True).then_inc(h_done, 1)

            def turn(i, u):
                after(pe, gt_lo_done, i - 1)
                pe.wait_ge(g_done, i + 1)
                for m in range(KF):
                    mm = pe.transpose(gt_ps[u][:, m, :], g[u][:, m * P:(m + 1) * P], ident[:])
                mm.then_inc(gt_done, 1)

            def second(i, u):
                e = expert(i)
                after(pe, y_copied, i - 1)
                pe.matmul(y_ps[u][:, 0:D], own[u][:], M.bias2[:], start=True, stop=False)
                pe.wait_ge(gt_lo_done, i + 1)
                for m in range(KF):
                    hi, lo = [w[:, bass.ds(e, 1), m, :].rearrange("p e f -> p (e f)") for w in (w2_hi, M.w2_lo)]
                    mm = three_passes(pe, y_ps[u][:, 0:D], (gt_hi[u][:, m, :], gt_lo[u][:, m, :]), (hi, lo), False, m == KF - 1)
                mm.then_inc(y_done, 1)

            pipeline(pe, S.PAIR_TILES, ORDER, {"turn": turn, "first": first, "turn_in": turn_in, "second": second})


def moe_combine(nc, S, M, x_all, passed, w1_in, b1_in, w2_in, zt_kept, y_rows, out):
    E, NE, KD, KF, FF, D, T, TOK, TOP = S.E, S.NE, S.KD, S.KF, S.FF, S.D, S.T, S.TOK, S.TOP
    HR, GR = 4, 4
    ORDER = (("load", 1), ("hidden", 0), ("outputs", -1))
    with ExitStack() as ctx:
        def sb(name, shape, dt=F32):
            return ctx.enter_context(nc.sbuf_tensor("dc_" + name, shape, dt))

        sem = cleared_semaphores(nc, ctx, "dc_")

        zt = [sb(f"zt{u}", [P, 2, KD, TOK], F32R) for u in range(2)]
        b1 = sb("b1", [P, NE, KF])
        w1_raw, w2_raw = sb("w1_raw", [P, KD, FF]), sb("w2_raw", [P, KF, D])
        w1_hi, w1_lo = sb("w1_hi", [P, KD, FF], F32R), sb("w1_lo", [P, KD, FF], F32R)
        w2_hi, w2_lo = sb("w2_hi", [P, KF, D], F32R), sb("w2_lo", [P, KF, D], F32R)
        g_full = sb("g_full", [P, GR, TOK])
        g_hi, g_lo = [sb(f"g_hi{u}", [P, KF, TOK], F32R) for u in range(2)], [sb(f"g_lo{u}", [P, KF, TOK], F32R) for u in range(2)]
        pos_u = [[sb(f"pos_u{u}_{k}", [P, 1], mybir.dt.int32) for k in range(T * TOP)] for u in range(2)]
        rows = [sb(f"rows{u}", [P, T * TOP, D]) for u in range(2)]
        hid = [ctx.enter_context(nc.psum_tensor(f"dc_hid{i}", [P, 512], F32)) for i in range(HR)]
        y = [ctx.enter_context(nc.psum_tensor(f"dc_y{i}", [P, 512], F32)) for i in range(T)]
        b1_loaded, w_loaded, hi_done, lo_done = sem("b1_loaded"), sem("w_loaded"), sem("hi_done"), sem("lo_done")
        zt_loaded, gathered = [sem(f"zt_loaded{u}") for u in range(2)], [sem(f"gathered{u}") for u in range(2)]
        pos_done, x_stored = sem("pos_done"), sem("x_stored")
        hid_done, gelu_hi, gelu_full, gelu_lo = sem("hid_done"), sem("gelu_hi"), sem("gelu_full"), sem("gelu_lo")
        y_done, weighed, y_added, x_added = sem("y_done"), sem("weighed"), sem("y_added"), sem("x_added")
        block = ctx.enter_context(nc.Block())
        out_tiles = out.rearrange("b (j p) d -> p (b j) d", p=P)

        def before(n, u, per):
            return per * (n // 2) if isinstance(n, int) else per // 2 * (n - u)

        @block.sync
        def _(sync):
            sync.dma_start(w1_raw[:], w1_in[NE - 1]).then_inc(w_loaded, 16)
            sync.dma_start(w2_raw[:], w2_in[NE - 1]).then_inc(w_loaded, 16)
            sync.dma_start(b1[:], b1_in).then_inc(b1_loaded, 16)

            def load(n, u):
                after(sync, hid_done, KF * (n - 1))
                src = zt_kept[bass.ds(n, 1)].rearrange("n p k f -> p (n k f)")
                sync.dma_start(zt[u][:].rearrange("p k c t -> p (k c t)").bitcast(F32), src).then_inc(zt_loaded[u], 16)

            def store(n, u):
                sync.wait_ge(x_added, T * (n + 1))
                sync.dma_start(out_tiles[:, bass.ds(T * n, T), :], x_all[:, bass.ds(T * n, T), :]).then_inc(x_stored, 16)

            pipeline(sync, S.CHUNKS, ORDER, {"load": load, "outputs": store})
            sync.wait_ge(x_stored, 16 * S.CHUNKS)

        @block.gpsimd
        def _(pool):
            def gather(n, u):
                after(pool, x_added, T * (n - 1))
                if not (isinstance(n, int) and n < 2):
                    alone(pool, gathered[u], before(n, u, 16 * T * TOP), passed)
                for k in range(T * TOP):
                    pool.tensor_copy(pos_u[u][k][:], M.pos[:, bass.ds(T * n + k // TOP, 1), k % TOP:k % TOP + 1].rearrange("p t k -> p (t k)")).then_inc(pos_done, 1)
                alone(pool, pos_done, T * TOP * (n + 1), passed)
                for k in range(T * TOP):
                    pool.indirect_dma_start(rows[u][:, k, :], None, y_rows, bass.IndirectOffsetOnAxis(ap=pos_u[u][k][:], axis=0)).then_inc(gathered[u], 16)

            pipeline(pool, S.CHUNKS, ORDER, {"load": gather})

        @block.scalar
        def _(act):
            act.wait_ge(w_loaded, 32)
            act.activation(w1_hi[:], w1_raw[:], ACT.Copy).then_inc(hi_done, 1)
            act.activation(w2_hi[:], w2_raw[:], ACT.Copy).then_inc(hi_done, 1)
            act.wait_ge(b1_loaded, 16)

            def hidden(n, u):
                for m in range(KF):
                    act.wait_ge(hid_done, n * KF + m + 1)
                    alone(act, gelu_lo, n * KF + m + 1 - GR, passed)
                    if m == 0:
                        after(act, y_done, T * (n - 1))
                    act.activation(g_full[:, m % GR, :], hid[m % HR][:, 0:TOK], ACT.Gelu, bias=b1[:, NE - 1, m:m + 1]).then_inc(gelu_full, 1)
                    act.activation(g_hi[u][:, m, :], hid[m % HR][:, 0:TOK], ACT.Gelu, bias=b1[:, NE - 1, m:m + 1]).then_inc(gelu_hi, 1)

            pipeline(act, S.CHUNKS, ORDER, {"hidden": hidden})

        @block.vector
        def _(dve):
            for k, (raw, hi, lo) in enumerate(((w1_raw, w1_hi, w1_lo), (w2_raw, w2_hi, w2_lo))):
                dve.wait_ge(hi_done, k + 1)
                dve.tensor_tensor(lo[:], raw[:], hi[:], ALU.subtract).then_inc(lo_done, 1)

            def hidden(n, u):
                for m in range(KF):
                    dve.wait_ge(gelu_hi, n * KF + m + 1)
                    dve.wait_ge(gelu_full, n * KF + m + 1)
                    dve.tensor_tensor(g_lo[u][:, m, :], g_full[:, m % GR, :], g_hi[u][:, m, :], ALU.subtract).then_inc(gelu_lo, 1)

            def outputs(n, u):
                dve.wait_ge(gathered[u], before(n, u, 16 * T * TOP) + 16 * T * TOP)
                for k in range(TOP):
                    if k > 0:
                        dve.wait_ge(weighed, T * (TOP * n + k))
                    for t in range(T):
                        xs = x_all[:, T * n + t, :]
                        w = M.prob[:, bass.ds(T * n + t, 1), k:k + 1].rearrange("p t k -> p (t k)")
                        dve.scalar_tensor_tensor(out=xs, in0=rows[u][:, t * TOP + k, :], scalar=w, in1=xs, op0=ALU.mult, op1=ALU.add).then_inc(weighed, 1)
                dve.wait_ge(weighed, T * TOP * (n + 1))
                for t in range(T):
                    dve.wait_ge(y_done, T * n + t + 1)
                    xs = x_all[:, T * n + t, :]
                    dve.scalar_tensor_tensor(out=xs, in0=y[t][:, 0:D], scalar=M.half_tanh[:, 0:1], in1=xs, op0=ALU.mult, op1=ALU.add).then_inc(x_added, 1)

            pipeline(dve, S.CHUNKS, ORDER, {"hidden": hidden, "outputs": outputs})

        @block.tensor
        def _(pe):
            pe.wait_ge(lo_done, 2)

            def hidden(n, u):
                pe.wait_ge(zt_loaded[u], before(n, u, 16) + 16)
                for m in range(KF):
                    after(pe, gelu_hi, n * KF + m + 1 - HR)
                    cols = slice(m * P, (m + 1) * P)
                    for c in range(KD):
                        mm = three_passes(pe, hid[m % HR][:, 0:TOK], (w1_hi[:, c, cols], w1_lo[:, c, cols]),
                                          (zt[u][:, 0, c, :], zt[u][:, 1, c, :]), c == 0, c == KD - 1)
                    mm.then_inc(hid_done, 1)

            def outputs(n, u):
                pe.wait_ge(gelu_lo, (n + 1) * KF)
                for t in range(T):
                    after(pe, x_added, T * (n - 1) + t + 1)
                    cols = slice(t * P, (t + 1) * P)
                    for m in range(KF):
                        three_passes(pe, y[t][:, 0:D], (g_hi[u][:, m, cols], g_lo[u][:, m, cols]),
                                     (w2_hi[:, m, :], w2_lo[:, m, :]), m == 0, False)
                    pe.matmul(y[t][:, 0:D], M.shared_row[:, 1, :], M.bias2[:], start=False, stop=True).then_inc(y_done, 1)

            pipeline(pe, S.CHUNKS, ORDER, {"hidden": hidden, "outputs": outputs})


def phase_store(nc, x_all, out):
    with ExitStack() as ctx:
        stored = ctx.enter_context(nc.semaphore("stored"))
        block = ctx.enter_context(nc.Block())
        ov = out.rearrange("b (j p) d -> p (b j) d", p=P)

        @block.sync
        def _(sync):
            for c in range(4):
                sync.dma_start(ov[:, 8 * c:8 * c + 8, :], x_all[:, 8 * c:8 * c + 8, :]).then_inc(stored, 16)
            sync.wait_ge(stored, 64)


def flamingo_kernel(nc, t, out, phases="ABCD"):
    with ExitStack() as ctx:
        x_all = ctx.enter_context(nc.sbuf_tensor("x_all", [P, 32, 256], F32))
        tanh_g = ctx.enter_context(nc.sbuf_tensor("tanh_g", [P, 4], F32))
        ident = ctx.enter_context(nc.sbuf_tensor("ident", [P, P], F32))
        half_neg = ctx.enter_context(nc.sbuf_tensor("half_neg", [P, 8], F32))
        passed = ctx.enter_context(nc.semaphore("passed"))
        common = (nc, x_all, tanh_g, ident, half_neg, passed)
        phase_setup(nc, t["x"], t["gates"], x_all, tanh_g, ident, half_neg)
        if "A" in phases:
            phase_mlstm(*common, t["ctx"], t["ctx_t"], t["gate_w"], t["gate_b"], t["ln_scale"])
        if "B" in phases:
            phase_lora_ffn(*common, t["w_fc_t"], t["b_fc"], t["a_fc"], t["b_fc_t"], t["w_pr_t"], t["b_pr"], t["a_pr"],
                           t["b_pr_t"])
        if "C" in phases:
            phase_attention(*common, t["ctx_t"], t["wq"], t["wkv"], t["wc"])
        if "D" in phases:
            phase_moe(*common, t["router_w"], t["router_b"], t["w1"], t["b1"], t["b1_rows"], t["w2"], t["b2"], out)
        else:
            phase_store(nc, x_all, out)


def blocks_first(a):
    return a.reshape(-1, P, a.shape[-1]).transpose(1, 0, 2)


def lay_out(v):
    a = {k: np.asarray(i) for k, i in v.items()}
    ctx = a["ctx_1024"]
    t = {
        "x": a["x"],
        "gates": np.concatenate([a["g_xattn"], a["g_ffn"]]),
        "ctx": ctx,
        "ctx_t": ctx.reshape(-1, 2, P).transpose(2, 1, 0),
        "gate_w": blocks_first(np.concatenate([a["L0_xattn_igate_w"], a["L0_xattn_fgate_w"]]).T),
        "gate_b": np.concatenate([a["L0_xattn_igate_b"], a["L0_xattn_fgate_b"]]),
        "ln_scale": a["L0_xattn_ln_scale"],
        "w_fc_t": blocks_first(a["L0_ffn_W_fc"].T),
        "b_fc": a["L0_ffn_b_fc"].reshape(-1, P).T,
        "a_fc": a["L0_ffn_A_fc"],
        "b_fc_t": a["L0_ffn_B_fc"].T,
        "w_pr_t": blocks_first(a["L0_ffn_W_proj"].T),
        "b_pr": a["L0_ffn_b_proj"],
        "a_pr": a["L0_ffn_A_proj"],
        "b_pr_t": a["L0_ffn_B_proj"].T,
        "wq": blocks_first(a["L1_xattn_Wq"]),
        "wkv": blocks_first(a["L1_xattn_Wkv"]),
        "wc": blocks_first(a["L1_xattn_Wc"]),
        "router_w": blocks_first(a["L1_ffn_router_w"]),
        "router_b": a["L1_ffn_router_b"],
        "w1": np.concatenate([a["L1_ffn_w1"], a["L1_ffn_sw1"]]).reshape(10, 2, P, 512).transpose(0, 2, 1, 3),
        "b1": np.concatenate([a["L1_ffn_b1"], a["L1_ffn_sb1"]]).reshape(10, 4, P).transpose(2, 0, 1),
        "b1_rows": np.concatenate([a["L1_ffn_b1"], a["L1_ffn_sb1"]]),
        "w2": np.concatenate([a["L1_ffn_w2"], a["L1_ffn_sw2"]]).reshape(10, 4, P, 256).transpose(0, 2, 1, 3),
        "b2": np.concatenate([a["L1_ffn_b2"], a["L1_ffn_sb2"]]),
    }
    return {k: np.ascontiguousarray(i) for k, i in t.items()}


def build(nc, t, phases="ABCD"):
    aps = {k: nc.dram_tensor(f"in_{k}", i.shape, F32, kind="ExternalInput").ap() for k, i in t.items()}
    out = nc.dram_tensor("out_x", t["x"].shape, F32, kind="ExternalOutput").ap()
    flamingo_kernel(nc, aps, out, phases)


def kernel(**inputs):
    import concourse.bacc as bacc
    from concourse.bass_utils import run_bass_kernel_spmd

    nc = bacc.Bacc("TRN2", target_bir_lowering=False, num_devices=1)
    t = lay_out(inputs)
    build(nc, t)
    result = run_bass_kernel_spmd(nc, [{f"in_{k}": i for k, i in t.items()}], core_ids=[0])
    return result.results[0]["out_x"]
```

```python
from contextlib import ExitStack

import numpy as np
import concourse.bass as bass
from concourse import mybir
from concourse.alu_op_type import AluOpType as ALU

F32 = mybir.dt.float32
F32R = mybir.dt.float32r
BF16 = mybir.dt.bfloat16
ACT = mybir.ActivationFunctionType
AX = mybir.AxisListType
RMAX = bass.bass_isa.ReduceOp.max
P = 128
LN_EPS = 1e-5
MLSTM_EPS = 1e-6
ROUND = 1.5 * 2.0 ** 23
QMAX = 127.0


def three_passes(tensor, out, lhs, rhs, start, stop):
    (lhs_hi, lhs_lo), (rhs_hi, rhs_lo) = lhs, rhs
    tensor.matmul(out, lhs_hi, rhs_hi, start=start, stop=False)
    tensor.matmul(out, lhs_hi, rhs_lo, start=False, stop=False)
    return tensor.matmul(out, lhs_lo, rhs_hi, start=False, stop=stop)


def after(engine, semaphore, value):
    if not isinstance(value, int) or value > 0:
        engine.wait_ge(semaphore, value)


def alone(engine, semaphore, value, passed):
    if not isinstance(value, int) or value > 0:
        engine.wait_ge(semaphore, value)
        engine.sem_inc(passed, 1)


def cleared_semaphores(nc, ctx, prefix):
    used = []
    ctx.callback(nc.all_engine_barrier)
    ctx.callback(nc.clear_and_free_semaphores, used)

    def semaphore(name):
        used.append(nc.alloc_semaphore(prefix + name))
        return used[-1]

    return semaphore


class Chain:

    def __init__(self, engine, semaphore, per, passed=None):
        self.engine, self.semaphore, self.per, self.passed = engine, semaphore, per, passed

    def begin(self, n):
        self.base, self.step = n * self.per, 0

    def __call__(self, instruction):
        self.step += 1
        assert self.step <= self.per
        instruction.then_inc(self.semaphore, 1)
        if self.passed is None:
            self.engine.wait_ge(self.semaphore, self.base + self.step)
        else:
            alone(self.engine, self.semaphore, self.base + self.step, self.passed)


def pipeline(engine, count, order, parts, head=3):
    offsets = [offset for _, offset in order]
    loops = (count - max(offsets) - head) // 2

    def step(n, u):
        for name, offset in order:
            if name in parts and not (isinstance(n, int) and not 0 <= n + offset < count):
                parts[name](n + offset, (u + offset) % 2)

    for n in range(-max(offsets), head):
        step(n, n % 2)
    with engine.Fori(0, loops) as i:
        for k in range(2):
            step(2 * i + (head + k), (head + k) % 2)
    for n in range(head + 2 * loops, count - min(offsets)):
        step(n, n % 2)


def phase_setup(nc, x, gates, x_all, tanh_g, ident, half_neg):
    with ExitStack() as ctx:
        sem = cleared_semaphores(nc, ctx, "setup_")
        gate_raw = ctx.enter_context(nc.sbuf_tensor("gate_raw", [P, 4], F32))
        x_loaded = sem("x_loaded")
        gates_loaded = sem("gates_loaded")
        filled = sem("filled")
        tanh_done = sem("tanh_done")
        block = ctx.enter_context(nc.Block())
        xv = x.rearrange("b (j p) d -> p (b j) d", p=P)

        @block.sync
        def _(sync):
            for c in range(4):
                sync.dma_start(x_all[:, 8 * c:8 * c + 8, :], xv[:, 8 * c:8 * c + 8, :]).then_inc(x_loaded, 16)
            sync.wait_ge(x_loaded, 64)

        @block.scalar
        def _(act):
            act.dma_start(gate_raw[:], gates.partition_broadcast(P)).then_inc(gates_loaded, 16)
            act.wait_ge(gates_loaded, 16)
            act.activation(tanh_g[:], gate_raw[:], ACT.Tanh).then_inc(tanh_done, 1)
            act.wait_ge(tanh_done, 1)

        @block.gpsimd
        def _(pool):
            pool.memset(half_neg[:], -0.5).then_inc(filled, 1)
            pool.memset(ident[:], 0.0).then_inc(filled, 1)
            pool.wait_ge(filled, 2)
            pool.affine_select(out=ident[:], in_=ident[:], compare_op=ALU.not_equal, fill=1.0, base=0,
                               pattern=[[-1, P]], channel_multiplier=1).then_inc(filled, 1)
            pool.wait_ge(filled, 3)


class Mlstm:
    B, S, D, H = 16, 256, 256, 8
    DH = D // H
    J = S // P
    LO = 32
    ROWS = LO + H


def phase_mlstm(nc, x_all, tanh_g, ident, half_neg, passed, ctx_in, ctx_t, gate_w, gate_b, ln_scale):
    B, S, H, J, ROWS = Mlstm.B, Mlstm.S, Mlstm.H, Mlstm.J, Mlstm.ROWS
    with ExitStack() as ctx:
        qt_all = ctx.enter_context(nc.sbuf_tensor("a_qt_all", [P, J, B * S], F32))
        m_rows = ctx.enter_context(nc.sbuf_tensor("a_m_rows", [P, B, S], F32R))
        tok_all = ctx.enter_context(nc.sbuf_tensor("a_tok_all", [P, 2, J, B * H], F32))
        mlstm_gates(nc, x_all, ident, half_neg, passed, ctx_t, gate_w, gate_b, qt_all, m_rows, tok_all)
        mlstm_heads(nc, x_all, tanh_g, ident, half_neg, passed, ctx_in, ctx_t, ln_scale, qt_all, m_rows, tok_all)


def mlstm_gates(nc, x_all, ident, half_neg, passed, ctx_t, gate_w, gate_b, qt_all, m_rows, tok_all):
    B, S, D, H, J, LO, ROWS = Mlstm.B, Mlstm.S, Mlstm.D, Mlstm.H, Mlstm.J, Mlstm.LO, Mlstm.ROWS
    T = 2 * J
    TOK = T * P
    STEPS = B // 2
    ORDER = (("stats", 2), ("norm", 1), ("turn", 0), ("gates", -1))
    gates_dram = nc.dram_tensor("a_gates", [2, B, H, S], F32, kind="Internal").ap()
    m_dram = nc.dram_tensor("a_maxima", [2, B, H, S], F32, kind="Internal").ap()
    with ExitStack() as ctx:
        def sb(name, shape, dt=F32):
            return ctx.enter_context(nc.sbuf_tensor("ag_" + name, shape, dt))

        sem = cleared_semaphores(nc, ctx, "ag_")

        wg_raw, wg = sb("wg_raw", [P, 6, 2 * H]), sb("wg", [P, 4, ROWS])
        gb = sb("gb", [ROWS, 1])
        kt = [sb(f"kt{u}", [P, 2, TOK]) for u in range(2)]
        z = [sb(f"z{u}", [P, T, D]) for u in range(2)]
        stats = sb("stats", [P, T, 6])
        mean_var, rstd = [sb(f"mean_var{u}", [P, T, 2]) for u in range(2)], [sb(f"rstd{u}", [P, T]) for u in range(2)]
        g_rows = sb("g_rows", [ROWS, B * S])
        zero, f, fabs, lnt, log_f = sb("zero", [P, S]), sb("f", [P, S]), sb("fabs", [P, S]), sb("lnt", [P, S]), sb("log_f", [P, S])
        gate_i, cs, a, m, minus_max, thr = sb("gate_i", [P, S]), sb("cs", [P, S]), sb("a", [P, S]), sb("m", [P, S]), sb("minus_max", [P, S]), sb("thr", [P, S])
        m_hi, m_lo = sb("m_hi", [P, S], F32R), sb("m_lo", [P, S], F32R)
        tz = [[ctx.enter_context(nc.psum_tensor(f"ag_tz{u}_{c}", [P, TOK], F32)) for c in range(2)] for u in range(2)]
        g_ps = [ctx.enter_context(nc.psum_tensor(f"ag_g{u}", [P, TOK], F32)) for u in range(2)]
        tok_ps = ctx.enter_context(nc.psum_tensor("ag_tok", [P, 2, J, P], F32))

        const_loaded, built, ready = sem("const_loaded"), sem("built"), sem("ready")
        kt_loaded = [sem(f"kt_loaded{u}") for u in range(2)]
        stats_done, mv_done, var_eps, rstd_done = sem("stats_done"), sem("mv_done"), sem("var_eps"), sem("rstd_done")
        z_done, tz_done, qt_done, gates_done, rows_done = sem("z_done"), sem("tz_done"), sem("qt_done"), sem("gates_done"), sem("rows_done")
        gates_kept, gates_loaded = sem("gates_kept"), sem("gates_loaded")
        fabs_done, exp_done, ln_done, chain = sem("fabs_done"), sem("exp_done"), sem("ln_done"), sem("chain")
        a_done, max_done, m_lo_done, thr_done = sem("a_done"), sem("max_done"), sem("m_lo_done"), sem("thr_done")
        m_kept, m_loaded, tok_turned, tok_done = sem("m_kept"), sem("m_loaded"), sem("tok_turned"), sem("tok_done")
        block = ctx.enter_context(nc.Block())

        def before(n, u, per):
            return per * (n // 2) if isinstance(n, int) else per // 2 * (n - u)

        @block.sync
        def _(sync):
            def load(n, u):
                after(sync, gates_done, n - 1)
                sync.dma_start(kt[u][:], ctx_t[:, :, bass.ds(n * TOK, TOK)]).then_inc(kt_loaded[u], 16)

            gate_cols = gate_b.rearrange("(n a) -> n a", a=1)
            load(0, 0)
            load(1, 1)
            sync.dma_start(wg_raw[:], gate_w).then_inc(const_loaded, 16)
            sync.wait_ge(built, 1)
            sync.dma_start(gb[0:H, :], gate_cols[H:2 * H, :]).then_inc(const_loaded, 16)
            sync.dma_start(gb[LO:ROWS, :], gate_cols[0:H, :]).then_inc(const_loaded, 16)
            with sync.Fori(0, (STEPS - 2) // 2) as i:
                for u in range(2):
                    load(2 * i + (2 + u), u)
            sync.wait_ge(rows_done, STEPS)
            for k, at in enumerate((0, LO)):
                sync.dma_start(gates_dram[k].rearrange("b h s -> h b s"),
                               g_rows[at:at + H, :].rearrange("h (b s) -> h b s", b=B)).then_inc(gates_kept, 16)
            sync.wait_ge(gates_kept, 32)
            for k, dst in enumerate((f, gate_i)):
                sync.dma_start(dst[:], gates_dram[k].rearrange("b h s -> (b h) s")).then_inc(gates_loaded, 16)
            sync.wait_ge(m_lo_done, 1)
            for k, src in enumerate((m_hi, m_lo)):
                sync.dma_start(m_dram[k].rearrange("b h s -> (b h) s"), src[:].bitcast(F32)).then_inc(m_kept, 16)
            sync.wait_ge(m_kept, 32)
            sync.wait_ge(built, 4)
            for k, at in enumerate((0, LO)):
                sync.dma_start(m_rows[at:at + H].bitcast(F32), m_dram[k].rearrange("b h s -> h b s")).then_inc(m_loaded, 16)
            sync.wait_ge(m_loaded, 32)

        @block.gpsimd
        def _(pool):
            pool.memset(gb[:], 0.0).then_inc(built, 1)
            pool.memset(wg[:], 0.0).then_inc(built, 1)
            pool.memset(zero[:], 0.0).then_inc(built, 1)

            def rstds(n, u):
                alone(pool, mv_done, T * n + T, passed)
                pool.tensor_scalar(rstd[u][:], mean_var[u][:, :, 1], LN_EPS, None, ALU.add).then_inc(var_eps, 1)
                pool.wait_ge(var_eps, n + 1)
                pool.tensor_tensor(rstd[u][:], rstd[u][:], half_neg[:, 0:T], ALU.pow).then_inc(rstd_done, 1)

            pipeline(pool, STEPS, ORDER, {"stats": rstds})
            pool.memset(m_rows[:].rearrange("r b s -> r (b s)").bitcast(F32), 0.0).then_inc(built, 1)
            pool.wait_ge(built, 4)

        @block.scalar
        def _(act):
            act.wait_ge(const_loaded, 48)

            def turn(n, u):
                alone(act, tz_done, n + 1, passed)
                for c in range(2):
                    act.activation(qt_all[:, c, bass.ds(n * TOK, TOK)], tz[u][c][:], ACT.Copy).then_inc(qt_done, 1)

            def gates(n, u):
                alone(act, gates_done, n + 1, passed)
                act.activation(g_rows[:, bass.ds(n * TOK, TOK)], g_ps[u][0:ROWS, :], ACT.Identity, bias=gb[:]).then_inc(rows_done, 1)

            pipeline(act, STEPS, ORDER, {"turn": turn, "gates": gates})
            act.wait_ge(fabs_done, 1)
            act.activation(lnt[:], fabs[:], ACT.Exp, scale=-1.0).then_inc(exp_done, 1)
            act.wait_ge(exp_done, 1)
            act.activation(lnt[:], lnt[:], ACT.Ln, bias=1.0).then_inc(ln_done, 1)
            act.wait_ge(max_done, 1)
            act.activation(thr[:], minus_max[:], ACT.Exp).then_inc(thr_done, 1)

        @block.vector
        def _(dve):
            dve.wait_ge(const_loaded, 48)
            dve.wait_ge(built, 3)
            for at, g in ((0, H), (LO, 0)):
                dve.tensor_copy(wg[:, 0:2, at:at + H], wg_raw[:, 0:2, g:g + H])
                ins = dve.tensor_tensor(wg[:, 2:4, at:at + H], wg_raw[:, 2:4, g:g + H], wg_raw[:, 4:6, g:g + H], ALU.add)
            ins.then_inc(ready, 1)

            def stat(n, u):
                alone(dve, mv_done, T * n, passed)
                for t in range(T):
                    dve.bn_stats(stats[:, t, :], x_all[:, T * n + t, :]).then_inc(stats_done, 1)
                alone(dve, stats_done, T * n + T, passed)
                for t in range(T):
                    dve.bn_aggr(mean_var[u][:, t, :], stats[:, t, :]).then_inc(mv_done, 1)

            def norm(n, u):
                after(dve, tz_done, n - 1)
                dve.wait_ge(rstd_done, n + 1)
                for t in range(T):
                    dve.tensor_scalar(z[u][:, t, :], x_all[:, T * n + t, :], mean_var[u][:, t, 0:1], rstd[u][:, t:t + 1],
                                      ALU.subtract, ALU.mult).then_inc(z_done, 1)

            pipeline(dve, STEPS, ORDER, {"stats": stat, "norm": norm})
            step = Chain(dve, chain, 4)
            step.begin(0)
            dve.wait_ge(gates_loaded, 32)
            dve.scalar_tensor_tensor(out=fabs[:], in0=f[:], scalar=-1.0, in1=f[:], op0=ALU.mult, op1=ALU.max).then_inc(fabs_done, 1)
            dve.wait_ge(ln_done, 1)
            step(dve.scalar_tensor_tensor(out=log_f[:], in0=f[:], scalar=0.0, in1=lnt[:], op0=ALU.min, op1=ALU.subtract))
            step(dve.tensor_tensor_scan(cs[:], log_f[:], zero[:], 0.0, ALU.add, ALU.add))
            dve.tensor_tensor(a[:], gate_i[:], cs[:], ALU.subtract).then_inc(a_done, 1)
            dve.wait_ge(a_done, 1)
            step(dve.tensor_tensor_scan(m[:], a[:], a[:], -3e38, ALU.max, ALU.max))
            dve.scalar_tensor_tensor(out=minus_max[:], in0=cs[:], scalar=-1.0, in1=m[:], op0=ALU.mult, op1=ALU.subtract).then_inc(max_done, 1)
            step(dve.tensor_copy(m_hi[:], m[:]))
            dve.tensor_tensor(m_lo[:], m[:], m_hi[:], ALU.subtract).then_inc(m_lo_done, 1)
            dve.wait_ge(tok_turned, 1)
            dve.tensor_copy(tok_all[:], tok_ps[:]).then_inc(tok_done, 1)
            dve.wait_ge(tok_done, 1)

        @block.tensor
        def _(pe):
            def turn(n, u):
                pe.wait_ge(z_done, T * n + T)
                after(pe, qt_done, 2 * (n - 1))
                for c in range(2):
                    for t in range(T):
                        mm = pe.transpose(tz[u][c][:, t * P:(t + 1) * P], z[u][:, t, c * P:(c + 1) * P], ident[:])
                mm.then_inc(tz_done, 1)

            def gates(n, u):
                pe.wait_ge(kt_loaded[u], before(n, u, 16) + 16)
                after(pe, rows_done, n - 1)
                for c in range(2):
                    pe.matmul(g_ps[u][0:ROWS, :], wg[:, 2 + c, :], kt[u][:, c, :], start=(c == 0), stop=False)
                alone(pe, qt_done, 2 * (n + 1), passed)
                for c in range(2):
                    mm = pe.matmul(g_ps[u][0:ROWS, :], wg[:, c, :], qt_all[:, c, bass.ds(n * TOK, TOK)], start=False, stop=(c == 1))
                mm.then_inc(gates_done, 1)

            pe.wait_ge(ready, 1)
            pipeline(pe, STEPS, ORDER, {"turn": turn, "gates": gates})
            for k, (rows, done) in enumerate(((a, a_done), (thr, thr_done))):
                pe.wait_ge(done, 1)
                for j in range(J):
                    mm = pe.transpose(tok_ps[:, k, j, :], rows[:, j * P:(j + 1) * P], ident[:])
            mm.then_inc(tok_turned, 1)


def mlstm_heads(nc, x_all, tanh_g, ident, half_neg, passed, ctx_in, ctx_t, ln_scale, qt_all, m_rows, tok_all):
    B, S, D, H, DH, J, LO, ROWS = Mlstm.B, Mlstm.S, Mlstm.D, Mlstm.H, Mlstm.DH, Mlstm.J, Mlstm.LO, Mlstm.ROWS
    SCALE = float(DH) ** -0.5
    W = S + P
    R = 2
    LOADS = 16 * (2 + P // DH)
    CR, LAG = 4, 2
    WARM = 4
    SLOT = 2 * DH
    GROUPS = H * SLOT // P
    GH = H // GROUPS
    with ExitStack() as ctx:
        def sb(name, shape, dt=F32):
            return ctx.enter_context(nc.sbuf_tensor("a_" + name, shape, dt))

        sem = cleared_semaphores(nc, ctx, "a_")

        ln_s = sb("ln_s", [P, D])
        mask = sb("mask", [P, P], BF16)
        ident_b = sb("ident_b", [P, P], BF16)
        sel_raw = sb("sel_raw", [P, H, P])
        sel = sb("sel", [P, H, P], F32R)
        c_raw = [sb(f"c_raw{i}", [P, J, D]) for i in range(R)]
        kt = [sb(f"kt{i}", [P, J, S]) for i in range(R)]
        va = [sb(f"va{i}", [P, J, H, SLOT]) for i in range(R)]
        qt = [sb(f"qt{i}", [P, H, S]) for i in range(R)]
        tok = [sb(f"tok{i}", [P, 2, J, H]) for i in range(R)]
        decay = [sb(f"decay{i}", [P, W]) for i in range(R)]
        c_mat = [sb(f"c_mat{i}", [P, W]) for i in range(CR)]
        ot = [sb(f"ot{i}", [P, GROUPS, S]) for i in range(R)]
        nrm, rn = sb("nrm", [P, J, H]), sb("rn", [P, J, H])
        hn = sb("hn", [P, J, H, DH])
        h_stats, h_mv, h_rstd = sb("h_stats", [P, J, 6]), sb("h_mv", [P, J, 2]), sb("h_rstd", [P, J])
        hz = sb("hz", [P, J, D])
        qk = [ctx.enter_context(nc.psum_tensor(f"a_qk{i}", [P, 512], F32)) for i in range(R)]
        ex = [ctx.enter_context(nc.psum_tensor(f"a_ex{i}", [P, 512], F32)) for i in range(R)]
        hp = ctx.enter_context(nc.psum_tensor("a_hp", [P, J, 512], F32))
        hvt = [ctx.enter_context(nc.psum_tensor(f"a_hvt{i}", [P, 512], F32)) for i in range(2)]
        hv = hp[:].rearrange("p j (h d) -> p j h d", d=SLOT)

        const_loaded, built, ready = sem("const_loaded"), sem("built"), sem("ready")
        c_loaded = [sem(f"c_loaded{i}") for i in range(R)]
        va_done = sem("va_done")
        tok_done = sem("tok_done")
        ot_done, turned = sem("ot_done"), sem("turned")
        qk_done, decay_done, c_done, cv_done = sem("qk_done"), sem("decay_done"), sem("c_done"), sem("cv_done")
        post, hp_read, h_stats_done, h_mv_done = sem("post"), sem("hp_read"), sem("h_stats_done"), sem("h_mv_done")
        h_var_eps, h_rstd_done, hz_done = sem("h_var_eps"), sem("h_rstd_done"), sem("hz_done")
        scaled, x_done = sem("scaled"), sem("x_done")
        block = ctx.enter_context(nc.Block())
        cv = ctx_in.rearrange("b (j p) d -> b p j d", p=P)

        def all_batches(engine, body):
            body(0, 0)
            with engine.Fori(0, (B - 2) // 2) as i:
                for u in range(2):
                    body(2 * i + (1 + u), (1 + u) % 2)
            body(B - 1, (B - 1) % 2)

        def first(n):
            return isinstance(n, int) and n == 0

        def below(n, bound):
            return not isinstance(n, int) or n < bound

        @block.sync
        def _(sync):
            sync.dma_start(ln_s[:], ln_scale.partition_broadcast(P)).then_inc(const_loaded, 16)

            def load(n, u):
                if not (isinstance(n, int) and n < R):
                    sync.wait_ge(cv_done, (n - 1) * H)
                    sync.wait_ge(va_done, n - 1)
                sync.dma_start(kt[u][:], ctx_t[:, :, bass.ds(n * S, S)]).then_inc(c_loaded[u], 16)
                for k in range(P // DH):
                    rows = slice(DH * k, DH * (k + 1))
                    sync.dma_start(qt[u][rows, k::P // DH, :], qt_all[rows, :, bass.ds(n * S, S)]).then_inc(c_loaded[u], 16)
                sync.dma_start(c_raw[u][:], cv[bass.ds(n, 1)].rearrange("b p j d -> p (b j) d")).then_inc(c_loaded[u], 16)

            sync.wait_ge(built, 2)
            load(0, 0)
            load(1, 1)
            with sync.Fori(0, (B - R) // 2) as i:
                for u in range(2):
                    load(2 * i + (2 + u), u)

        FILLS = 2 + 2 * R + 1
        BUILT = FILLS + R + 3

        @block.gpsimd
        def _(pool):
            for i in range(R):
                pool.memset(qt[i][:], 0.0).then_inc(built, 1)
            pool.memset(mask[:], 0.0).then_inc(built, 1)
            pool.memset(sel_raw[:], 0.0).then_inc(built, 1)
            for i in range(R):
                pool.memset(va[i][:], 0.0).then_inc(built, 1)
            pool.tensor_copy(ident_b[:], ident[:]).then_inc(built, 1)
            pool.wait_ge(built, FILLS)
            for i in range(R):
                pool.memset(va[i][:, :, :, DH:DH + 1], 1.0).then_inc(built, 1)
            pool.affine_select(out=mask[:], in_=mask[:], compare_op=ALU.is_ge, fill=-1e30, base=0,
                               pattern=[[1, P]], channel_multiplier=-1).then_inc(built, 1)
            for k in range(2):
                pool.affine_select(out=sel_raw[:], in_=sel_raw[:], compare_op=ALU.not_equal, fill=-1.0, base=-LO * k,
                                   pattern=[[-1, H], [0, P]], channel_multiplier=1).then_inc(built, 1)
                pool.wait_ge(built, FILLS + R + 2 + k)

            def values(n, u, loads):
                pool.wait_ge(c_loaded[u], LOADS * loads)
                alone(pool, cv_done, (n - 1) * H, passed)
                pool.tensor_copy(va[u][:, :, :, 0:DH], c_raw[u][:].rearrange("p j (h d) -> p j h d", d=DH)).then_inc(va_done, 1)

            def h_rstds(n):
                alone(pool, h_mv_done, J * n + J, passed)
                pool.tensor_scalar(h_rstd[:], h_mv[:, :, 1], LN_EPS, None, ALU.add).then_inc(h_var_eps, 1)
                pool.wait_ge(h_var_eps, n + 1)
                pool.tensor_tensor(h_rstd[:], h_rstd[:], half_neg[:, 0:J], ALU.pow).then_inc(h_rstd_done, 1)

            def update_x(n):
                pool.wait_ge(hz_done, J * n + J)
                pool.wait_ge(ready, 1)
                for j in range(J):
                    pool.tensor_tensor(hz[:, j, :], hz[:, j, :], ln_s[:], ALU.mult).then_inc(scaled, 1)
                for j in range(J):
                    pool.wait_ge(scaled, J * n + j + 1)
                    xs = x_all[:, J * n + j, :]
                    pool.tensor_tensor(xs, xs, hz[:, j, :], ALU.add).then_inc(x_done, 1)

            values(0, 0, 1)

            def body(n, u, loads):
                if below(n, B - 1):
                    values(n + 1, 1 - u, loads)
                if not first(n):
                    h_rstds(n - 1)
                    update_x(n - 1)

            body(0, 0, 1)
            with pool.Fori(0, (B - 2) // 2) as i:
                for u in range(2):
                    body(2 * i + (1 + u), (1 + u) % 2, i + 2)
            body(B - 1, (B - 1) % 2, 0)
            h_rstds(B - 1)
            update_x(B - 1)
            pool.wait_ge(x_done, B * J)

        @block.scalar
        def _(act):
            def keep_outputs(n, u, g):
                act.wait_ge(cv_done, n * H + GH * (g + 1))
                act.wait_ge(turned, n + 1)
                act.activation(ot[u][:, g, :], hvt[g % 2][:, 0:S], ACT.Copy).then_inc(ot_done, 1)

            def decays(n, u, h):
                act.wait_ge(qk_done, n * H + h + 1)
                after(act, c_done, n * H + h + 1 - R)
                act.activation(decay[h % R][:, 0:S], ex[h % R][:, 0:S], ACT.Exp,
                               bias=tok[u][:, 0, 0, h:h + 1]).then_inc(decay_done, 1)
                act.activation(decay[h % R][:, S:W], ex[h % R][:, S:W], ACT.Exp,
                               bias=tok[u][:, 0, 1, h:h + 1]).then_inc(decay_done, 1)

            def body(n, u):
                act.wait_ge(tok_done, n + 1)
                for h in range(H):
                    decays(n, u, h)
                    if h == LAG - 1 and not first(n):
                        keep_outputs(n - 1, 1 - u, GROUPS - 1)
                    if h >= GH + LAG - 1 and (h - LAG) % GH == GH - 1:
                        keep_outputs(n, u, (h - LAG) // GH)

            all_batches(act, body)
            keep_outputs(B - 1, (B - 1) % 2, GROUPS - 1)

        @block.vector
        def _(dve):
            post_step = Chain(dve, post, 4)
            dve.sem_inc(hp_read, 1)
            dve.wait_ge(const_loaded, 16)
            dve.wait_ge(built, BUILT)
            dve.tensor_scalar(ln_s[:], ln_s[:], tanh_g[:, 0:1], None, ALU.mult).then_inc(ready, 1)
            dve.tensor_copy(sel[:], sel_raw[:]).then_inc(ready, 1)

            def by_tokens(n, u):
                alone(dve, turned, n + 1, passed)
                dve.tensor_copy(tok[u][:], tok_all[:, :, :, bass.ds(n * H, H)]).then_inc(tok_done, 1)

            def weigh(n, h):
                dve.wait_ge(decay_done, 2 * (n * H + h) + 2)
                after(dve, cv_done, n * H + h + 1 - CR)
                dve.scalar_tensor_tensor(out=c_mat[h % CR][:], in0=qk[h % R][:, 0:W], scalar=SCALE, in1=decay[h % R][:],
                                         op0=ALU.mult, op1=ALU.mult).then_inc(c_done, 1)

            def normalise(n, u):
                post_step.begin(n)
                dve.wait_ge(turned, n + 3)
                for sign in (-1.0, 1.0):
                    post_step(dve.scalar_tensor_tensor(out=nrm[:], in0=hv[:, :, :, DH], scalar=sign,
                                                       in1=tok[u][:, 1, :, :] if sign < 0 else nrm[:], op0=ALU.mult, op1=ALU.max))
                post_step(dve.tensor_scalar(nrm[:], nrm[:], MLSTM_EPS, None, ALU.add))
                post_step(dve.reciprocal(rn[:], nrm[:]))
                dve.tensor_tensor(hn[:], hv[:, :, :, 0:DH], rn[:].rearrange("p j (h a) -> p j h a", a=1).broadcast_to([P, J, H, DH]),
                                  ALU.mult).then_inc(hp_read, 1)

            def h_stat(n):
                dve.wait_ge(hp_read, n + 2)
                for j in range(J):
                    dve.bn_stats(h_stats[:, j, :], hn[:, j, :, :].rearrange("p h d -> p (h d)")).then_inc(h_stats_done, 1)
                for j in range(J):
                    alone(dve, h_stats_done, J * n + j + 1, passed)
                    dve.bn_aggr(h_mv[:, j, :], h_stats[:, j, :]).then_inc(h_mv_done, 1)

            def h_norm(n):
                dve.wait_ge(h_rstd_done, n + 1)
                after(dve, x_done, J * n)
                for j in range(J):
                    dve.tensor_scalar(hz[:, j, :], hn[:, j, :, :].rearrange("p h d -> p (h d)"), h_mv[:, j, 0:1],
                                      h_rstd[:, j:j + 1], ALU.subtract, ALU.mult).then_inc(hz_done, 1)

            by_tokens(0, 0)

            def body(n, u):
                for h in range(H):
                    weigh(n, h)
                    if not first(n):
                        if h == 4:
                            normalise(n - 1, 1 - u)
                        if h == 5:
                            h_stat(n - 1)
                        if h == 6:
                            h_norm(n - 1)
                    if h == 7 and below(n, B - 1):
                        by_tokens(n + 1, 1 - u)

            all_batches(dve, body)
            normalise(B - 1, (B - 1) % 2)
            h_stat(B - 1)
            h_norm(B - 1)

        @block.tensor
        def _(pe):
            def turn_outputs(n, u):
                pe.wait_ge(ot_done, GROUPS * (n + 1))
                pe.wait_ge(hp_read, n + 1)
                for g in range(GROUPS):
                    for j in range(J):
                        mm = pe.transpose(hp[:, j, g * P:(g + 1) * P], ot[u][:, g, j * P:(j + 1) * P], ident[:])
                mm.then_inc(turned, 1)

            def scores(n, u, h):
                after(pe, c_done, n * H + h + 1 - R)
                after(pe, decay_done, 2 * (n * H + h + 1 - R))
                c = h * DH // P
                q, k, s, e = qt[u], kt[u], qk[h % R], ex[h % R]
                pe.matmul(s[:, 0:S], k[:, c, 0:P], q[:, h, :], start=True, stop=True)
                pe.matmul(s[:, S:W], k[:, c, P:S], q[:, h, P:S], start=True, stop=True)
                maxima = m_rows[:, bass.ds(n, 1), :].rearrange("r b s -> r (b s)")
                pe.matmul(e[:, 0:S], sel[:, h, :], maxima, start=True, stop=True)
                pe.matmul(e[:, 0:P], ident_b[:], mask[:], start=False, stop=True, skip_group_check=True)
                pe.matmul(e[:, S:W], sel[:, h, :], maxima[:, P:S], start=False, stop=False, skip_group_check=True)
                pe.matmul(e[:, S:W], ident_b[:], mask[:], start=False, stop=True, skip_group_check=True).then_inc(qk_done, 1)

            def values(n, u, h):
                pe.wait_ge(c_done, n * H + h + 1)
                if h == 0:
                    pe.wait_ge(va_done, n + 1)
                g = h // GH
                if h % GH == 0:
                    after(pe, ot_done, GROUPS * n + g - 1)
                c = c_mat[h % CR]
                out = hvt[g % 2][SLOT * (h % GH):SLOT * (h % GH + 1), :]
                pe.matmul(out[:, 0:S], va[u][:, 0, h, :], c[:, 0:S], start=True, stop=True)
                pe.matmul(out[:, P:S], va[u][:, 1, h, :], c[:, S:W], start=False, stop=True, skip_group_check=True).then_inc(cv_done, 1)

            for _ in range(WARM):
                pe.matmul(hp[:, 0, :], ident[:], x_all[:, 0:2, :].rearrange("p j d -> p (j d)"), start=True, stop=True)
            pe.wait_ge(ready, 2)
            pe.wait_ge(built, BUILT)
            pe.sem_inc(turned, 2)

            def body(n, u, loads):
                pe.wait_ge(c_loaded[u], LOADS * loads)
                for h in range(H):
                    scores(n, u, h)
                    if h >= LAG:
                        values(n, u, h - LAG)
                    elif not first(n):
                        values(n - 1, 1 - u, H - LAG + h)
                    if h == 3 and not first(n):
                        turn_outputs(n - 1, 1 - u)

            body(0, 0, 1)
            with pe.Fori(0, (B - 2) // 2) as i:
                for u in range(2):
                    body(2 * i + (1 + u), (1 + u) % 2, i + (1 + u))
            body(B - 1, (B - 1) % 2, B // 2)
            for h in range(H - LAG, H):
                values(B - 1, (B - 1) % 2, h)
            turn_outputs(B - 1, (B - 1) % 2)


def phase_lora_ffn(nc, x_all, tanh_g, ident, half_neg, passed, w_fc_t, b_fc, a_fc, b_fc_t, w_pr_t, b_pr, a_pr, b_pr_t):
    D, FF, R = 256, w_fc_t.shape[2], a_fc.shape[0]
    T = 4
    TOK = T * P
    CHUNKS = x_all.shape[1] // T
    KD, KF = D // P, FF // P
    HR = 4
    GR = 2
    EARLY = 6
    PIECE = 512
    with ExitStack() as ctx:
        def sb(name, shape, dt=F32):
            return ctx.enter_context(nc.sbuf_tensor("b_" + name, shape, dt))

        sem = cleared_semaphores(nc, ctx, "b_")

        w1_hi, w1_lo = sb("w1_hi", [P, KD, FF], F32R), sb("w1_lo", [P, KD, FF], F32R)
        w2_hi, w2_lo = sb("w2_hi", [P, KF, D], F32R), sb("w2_lo", [P, KF, D], F32R)
        w1_raw, w2_raw = sb("w1_raw", [P, KD, FF]), sb("w2_raw", [P, KF, D])
        b1, b2 = sb("b1", [P, KF]), sb("b2", [P, D])
        a1, a2 = sb("a1", [R, D]), sb("a2", [R, FF])
        b1t, b2t = sb("b1t", [R, FF]), sb("b2t", [R, D])
        amax, amax_rows = sb("amax", [P, 2]), sb("amax_rows", [P, 2])
        scale, inv = sb("scale", [P, 2]), sb("inv", [P, 2])
        stats, mean_var = sb("stats", [P, T, 6]), sb("mean_var", [P, T, 2])
        rstd = sb("rstd", [P, T])
        z = sb("z", [P, T, D])
        zt_hi, zt_lo = sb("zt_hi", [P, KD, TOK], F32R), sb("zt_lo", [P, KD, TOK], F32R)
        g_full = sb("g_full", [P, GR, TOK])
        g_hi, g_lo = sb("g_hi", [P, KF, TOK], F32R), sb("g_lo", [P, KF, TOK], F32R)
        hid = [ctx.enter_context(nc.psum_tensor(f"b_hid{i}", [P, TOK], F32)) for i in range(HR)]
        zt = [ctx.enter_context(nc.psum_tensor(f"b_zt{i}", [P, TOK], F32)) for i in range(KD)]
        y = [ctx.enter_context(nc.psum_tensor(f"b_y{i}", [P, 2, D], F32)) for i in range(T // 2)]

        w_loaded, small_loaded = sem("w_loaded"), sem("small_loaded")
        amax_done, amax_all = sem("amax_done"), sem("amax_all")
        prep, lora_done, lora_used, w_ready = sem("prep"), sem("lora_done"), sem("lora_used"), sem("w_ready")
        stats_done, mv_done = sem("stats_done"), sem("mv_done")
        var_eps, rstd_done = sem("var_eps"), sem("rstd_done")
        z_done, zt_done, zt_hi_done, zt_lo_done = sem("z_done"), sem("zt_done"), sem("zt_hi_done"), sem("zt_lo_done")
        hid_done, gelu_full = sem("hid_done"), sem("gelu_full")
        gelu_hi = sem("gelu_hi")
        gelu_lo = sem("gelu_lo")
        y_done, x_added, x_biased = sem("y_done"), sem("x_added"), sem("x_biased")
        block = ctx.enter_context(nc.Block())

        @block.sync
        def _(sync):
            sync.dma_start(w1_raw[:], w_fc_t).then_inc(w_loaded, 16)
            sync.dma_start(w2_raw[:], w_pr_t).then_inc(w_loaded, 16)

        @block.scalar
        def _(act):
            for dst, src in ((a1, a_fc), (a2, a_pr), (b1t, b_fc_t), (b2t, b_pr_t), (b1, b_fc)):
                act.dma_start(dst[:], src).then_inc(small_loaded, 16)
            act.dma_start(b2[:], b_pr.partition_broadcast(P)).then_inc(small_loaded, 16)
            act.sem_inc(gelu_hi, HR)

            def split_zt(n):
                for c in range(KD):
                    act.wait_ge(zt_done, n * KD + c + 1)
                    act.activation(zt_hi[:, c, :], zt[c][:], ACT.Copy).then_inc(zt_hi_done, 1)

            def gelus(n):
                for m in range(KF):
                    act.wait_ge(hid_done, n * KF + m + 1)
                    act.wait_ge(gelu_lo, n * KF + m + 1)
                    act.activation(g_full[:, m % GR, :], hid[m % HR][:], ACT.Gelu,
                                   bias=b1[:, m:m + 1]).then_inc(gelu_full, 1)
                    act.activation(g_hi[:, m, :], hid[m % HR][:], ACT.Gelu,
                                   bias=b1[:, m:m + 1]).then_inc(gelu_hi, 1)

            split_zt(0)
            act.wait_ge(small_loaded, 96)
            with act.Fori(0, CHUNKS - 1) as n:
                gelus(n)
                split_zt(n + 1)
            gelus(CHUNKS - 1)

        @block.gpsimd
        def _(pool):
            def rstds(n):
                alone(pool, mv_done, n * T + T, passed)
                pool.tensor_scalar(rstd[:], mean_var[:, :, 1], LN_EPS, None, ALU.add).then_inc(var_eps, 1)
                pool.wait_ge(var_eps, n + 1)
                pool.tensor_tensor(rstd[:], rstd[:], half_neg[:, 0:T], ALU.pow).then_inc(rstd_done, 1)

            def bias_x(n):
                pool.wait_ge(z_done, n * T + T)
                for t in range(T):
                    xs = x_all[:, n * T + t, :]
                    pool.tensor_tensor(xs, xs, b2[:], ALU.add).then_inc(x_biased, 1)

            rstds(0)
            pool.wait_ge(amax_done, 2)
            pool.partition_all_reduce(amax[:], amax_rows[:], P, RMAX).then_inc(amax_all, 1)
            pool.wait_ge(w_ready, 1)
            bias_x(0)
            with pool.Fori(0, CHUNKS - 1) as n:
                rstds(n + 1)
                bias_x(n + 1)

        @block.vector
        def _(dve):
            steps = [0]

            def chain(ins):
                steps[0] += 1
                ins.then_inc(prep, 1)
                dve.wait_ge(prep, steps[0])

            def stat(n):
                for t in range(T):
                    dve.bn_stats(stats[:, t, :], x_all[:, n * T + t, :]).then_inc(stats_done, 1)
                for t in range(T):
                    alone(dve, stats_done, n * T + t + 1, passed)
                    dve.bn_aggr(mean_var[:, t, :], stats[:, t, :]).then_inc(mv_done, 1)

            def norm(n):
                dve.wait_ge(rstd_done, n + 1)
                for t in range(T):
                    dve.tensor_scalar(z[:, t, :], x_all[:, n * T + t, :], mean_var[:, t, 0:1], rstd[:, t:t + 1],
                                      ALU.subtract, ALU.mult).then_inc(z_done, 1)

            def split_zt(n):
                for c in range(KD):
                    dve.wait_ge(zt_hi_done, n * KD + c + 1)
                    dve.tensor_tensor(zt_lo[:, c, :], zt[c][:], zt_hi[:, c, :], ALU.subtract).then_inc(zt_lo_done, 1)

            def split_gelu(n):
                for m in range(KF):
                    dve.wait_ge(gelu_hi, HR + n * KF + m + 1)
                    dve.wait_ge(gelu_full, n * KF + m + 1)
                    dve.tensor_tensor(g_lo[:, m, :], g_full[:, m % GR, :], g_hi[:, m, :],
                                      ALU.subtract).then_inc(gelu_lo, 1)

            def add_x(n):
                for h in range(T // 2):
                    dve.wait_ge(y_done, n * (T // 2) + h + 1)
                    dve.wait_ge(x_biased, n * T + T)
                    xs = x_all[:, bass.ds(n * T + 2 * h, 2), :]
                    dve.tensor_tensor(xs, xs, y[h][:], ALU.add).then_inc(x_added, 1)

            dve.sem_inc(gelu_lo, GR)
            stat(0)
            dve.wait_ge(w_loaded, 32)
            for i, w in enumerate((w1_raw, w2_raw)):
                dve.tensor_reduce(amax_rows[:, i:i + 1], w[:].rearrange("p a b -> p (a b)"), AX.X, ALU.max,
                                  apply_absolute_value=True).then_inc(amax_done, 1)
            norm(0)
            dve.wait_ge(amax_all, 1)
            chain(dve.tensor_scalar(scale[:], amax[:], 1.0 / QMAX, None, ALU.mult))
            chain(dve.reciprocal(inv[:], scale[:]))
            dve.wait_ge(small_loaded, 96)
            chain(dve.tensor_scalar(b2[:], b2[:], tanh_g[:, 2:3], None, ALU.mult))
            for i, (w, hi, lo) in enumerate(((w1_raw, w1_hi, w1_lo), (w2_raw, w2_hi, w2_lo))):
                flat = w[:].rearrange("p a b -> p (a b)")
                chain(dve.tensor_scalar(flat, flat, inv[:, i:i + 1], ROUND, ALU.mult, ALU.add))
                chain(dve.tensor_scalar(flat, flat, -ROUND, QMAX, ALU.add, ALU.min))
                chain(dve.tensor_scalar(flat, flat, -QMAX - 1.0, scale[:, i:i + 1], ALU.max, ALU.mult))
                for q in range(4):
                    dve.wait_ge(lora_done, 4 * i + q + 1)
                    dst = flat[:, PIECE * q:PIECE * (q + 1)]
                    dve.scalar_tensor_tensor(out=dst, in0=hid[q][:], scalar=2.0, in1=dst,
                                             op0=ALU.mult, op1=ALU.add).then_inc(lora_used, 1)
                dve.wait_ge(lora_used, 4 * i + 4)
                if i == 1:
                    chain(dve.tensor_scalar(flat, flat, tanh_g[:, 2:3], None, ALU.mult))
                chain(dve.tensor_copy(hi[:], w[:]))
                dve.tensor_tensor(lo[:], w[:], hi[:], ALU.subtract).then_inc(w_ready, 1)
            split_zt(0)
            with dve.Fori(0, CHUNKS - 1) as n:
                stat(n + 1)
                norm(n + 1)
                split_gelu(n)
                split_zt(n + 1)
                add_x(n)
            split_gelu(CHUNKS - 1)
            add_x(CHUNKS - 1)
            dve.wait_ge(x_added, CHUNKS * T // 2)

        @block.tensor
        def _(pe):
            def transpose_z(n):
                pe.wait_ge(z_done, n * T + T)
                for c in range(KD):
                    for t in range(T):
                        mm = pe.transpose(zt[c][:, t * P:(t + 1) * P], z[:, t, c * P:(c + 1) * P], ident[:])
                    mm.then_inc(zt_done, 1)

            def lora_products(i):
                if i == 0:
                    pe.wait_ge(small_loaded, 96)
                for q in range(4):
                    if i == 1:
                        pe.wait_ge(lora_used, q + 1)
                    if i == 0:
                        c, cols = q // 2, slice(PIECE * (q % 2), PIECE * (q % 2 + 1))
                        mm = pe.matmul(hid[q][:], a1[:, c * P:(c + 1) * P], b1t[:, cols], start=True, stop=True)
                    else:
                        for k in range(2):
                            m = 2 * q + k
                            mm = pe.matmul(hid[q][:, D * k:D * (k + 1)], a2[:, m * P:(m + 1) * P], b2t[:],
                                           start=True, stop=True)
                    mm.then_inc(lora_done, 1)

            def hidden(n):
                pe.wait_ge(zt_lo_done, n * KD + KD)
                for m in range(KF):
                    pe.wait_ge(gelu_hi, n * KF + m + 1)
                    cols = slice(m * P, (m + 1) * P)
                    for c in range(KD):
                        mm = three_passes(pe, hid[m % HR][:], (w1_hi[:, c, cols], w1_lo[:, c, cols]),
                                          (zt_hi[:, c, :], zt_lo[:, c, :]), c == 0, c == KD - 1)
                    mm.then_inc(hid_done, 1)

            def outputs(n):
                def product(t, m):
                    cols = slice(t * P, (t + 1) * P)
                    return three_passes(pe, y[t // 2][:, t % 2, :], (g_hi[:, m, cols], g_lo[:, m, cols]),
                                        (w2_hi[:, m, :], w2_lo[:, m, :]), m == 0, m == KF - 1)

                pe.wait_ge(x_added, n * (T // 2))
                pe.wait_ge(gelu_lo, GR + n * KF + EARLY)
                for t in range(0, T, 2):
                    for m in range(EARLY):
                        product(t, m)
                pe.wait_ge(gelu_lo, GR + n * KF + KF)
                for t in range(T):
                    for m in range(0 if t % 2 else EARLY, KF):
                        mm = product(t, m)
                    if t % 2:
                        mm.then_inc(y_done, 1)

            lora_products(0)
            transpose_z(0)
            lora_products(1)
            pe.wait_ge(w_ready, 2)
            with pe.Fori(0, CHUNKS - 1) as n:
                hidden(n)
                transpose_z(n + 1)
                outputs(n)
            hidden(CHUNKS - 1)
            outputs(CHUNKS - 1)


def phase_attention(nc, x_all, tanh_g, ident, half_neg, passed, ctx_t, wq_in, wkv_in, wc_in):
    B, S, D, H = 16, 256, 256, 16
    DH = D // H
    J = S // P
    SLOT = 64
    PAIRS = H * SLOT // P
    K3 = 3 * DH
    K_MAX = K3 + 2
    EARLY = 2
    SCALE = float(DH) ** -0.5
    OSLOT = 32
    GH = P // OSLOT
    R = 2
    PR, LAG = 4, 2
    FILLS = PAIRS * J // 4
    FILLS_PER_SLOT = 1
    MAX_SLOTS = {1: (0,), 2: (1,), 4: (2, 3, 4), 5: (5, 6), 6: (7,), 7: (8,), 8: (9, 10), 9: (11,), 10: (12,), 12: (13, 14), 13: (15,)}
    with ExitStack() as ctx:
        def sb(name, shape, dt=F32):
            return ctx.enter_context(nc.sbuf_tensor("c_" + name, shape, dt))

        sem = cleared_semaphores(nc, ctx, "c_")

        w_raw = sb("w_raw", [P, 2, 4 * D])
        w_hi, w_lo = sb("w_hi", [P, 2, 4 * D], F32R), sb("w_lo", [P, 2, 4 * D], F32R)
        sel_raw = sb("sel_raw", [2 * H, EARLY, P])
        sel = sb("sel", [2 * H, EARLY, P], F32R)
        c_raw = [sb(f"c_raw{i}", [P, 2, S]) for i in range(R)]
        ct_hi, ct_lo = sb("ct_hi", [P, 2, S], F32R), sb("ct_lo", [P, 2, S], F32R)
        stats, mean_var, rstd = sb("stats", [P, J, 6]), sb("mean_var", [P, J, 2]), sb("rstd", [P, J])
        z = sb("z", [P, J, D])
        zt_hi, zt_lo = sb("zt_hi", [P, 2, S], F32R), sb("zt_lo", [P, 2, S], F32R)
        q3, k3 = sb("q3", [P, J * H, SLOT], F32R), sb("k3", [P, J * H, SLOT], F32R)
        v_tmp = sb("v_tmp", [P, J, D])
        va = [sb(f"va{i}", [P, J, H, OSLOT]) for i in range(R)]
        qt = [sb(f"qt{i}", [P, PAIRS, S], F32R) for i in range(R)]
        kt = [sb(f"kt{i}", [P, PAIRS, S], F32R) for i in range(R)]
        mx = sb("mx", [P, J, H])
        m_tok = sb("m_tok", [P, J, 2 * H], F32R)
        m_row = [sb(f"m_row{i}", [2 * H, S], F32R) for i in range(R)]
        probs = [sb(f"probs{i}", [P, J, S]) for i in range(PR)]
        ot = sb("ot", [P, 2, 2, S])
        rden = sb("rden", [P, J, H])
        yn = sb("yn", [P, J, H, DH])
        yt_hi, yt_lo = sb("yt_hi", [P, 2, S], F32R), sb("yt_lo", [P, 2, S], F32R)

        def pb(name, shape):
            return ctx.enter_context(nc.psum_tensor("c_" + name, shape, F32))

        s_ps = [pb(f"s{i}", [P, J, S]) for i in range(R)]
        t_ps = [pb(f"t{i}", [P, J, S]) for i in range(R)]
        o_ps = [pb(f"o{i}", [P, 2, S]) for i in range(2)]
        even, odd = pb("even", [P, 2, S]), pb("odd", [P, 2, S])

        w_loaded, w_ready, prep, built = sem("w_loaded"), sem("w_ready"), sem("prep"), sem("built")
        c_loaded = [sem(f"c_loaded{i}") for i in range(R)]
        ct_hi_done, ct_lo_done = sem("ct_hi_done"), sem("ct_lo_done")
        stats_done, mv_done, var_eps, rstd_done = sem("stats_done"), sem("mv_done"), sem("var_eps"), sem("rstd_done")
        z_done, zt_done, zt_hi_done, zt_lo_done = sem("z_done"), sem("zt_done"), sem("zt_hi_done"), sem("zt_lo_done")
        q_done, q_hi_done, q_lo_done = sem("q_done"), sem("q_hi_done"), sem("q_lo_done")
        kv_done, k_hi_done, v_done, k_lo_done = sem("kv_done"), sem("k_hi_done"), sem("v_done"), sem("k_lo_done")
        va_done = sem("va_done")
        turned, q_read, k_read = sem("turned"), sem("q_read"), sem("k_read")
        s_done, max_done, m_hi_done, m_tok_done = sem("s_done"), sem("max_done"), sem("m_hi_done"), sem("m_tok_done")
        m_turned, m_row_done, m_placed = sem("m_turned"), sem("m_row_done"), sem("m_placed")
        t_done, exp_done, pv_done = sem("t_done"), sem("exp_done"), sem("pv_done")
        rden_done, y_done, yt_done, yt_hi_done, yt_lo_done = sem("rden_done"), sem("y_done"), sem("yt_done"), sem("yt_hi_done"), sem("yt_lo_done")
        ot_done, o_turned = sem("ot_done"), sem("o_turned")
        out_done, x_done = sem("out_done"), sem("x_done")
        block = ctx.enter_context(nc.Block())

        def all_batches(engine, body):
            body(0, 0)
            with engine.Fori(0, (B - 4) // 2) as i:
                for u in range(2):
                    body(2 * i + (1 + u), (1 + u) % 2)
            for n in range(B - 3, B):
                body(n, n % 2)

        def has(n, least=None, below=None):
            return not isinstance(n, int) or ((least is None or n >= least) and (below is None or n < below))

        @block.sync
        def _(sync):
            sync.dma_start(w_raw[:, :, 0:D], wq_in).then_inc(w_loaded, 16)
            sync.dma_start(w_raw[:, :, D:3 * D], wkv_in).then_inc(w_loaded, 16)
            sync.dma_start(w_raw[:, :, 3 * D:4 * D], wc_in).then_inc(w_loaded, 16)

            def load(n, u):
                if not (isinstance(n, int) and n < R):
                    sync.wait_ge(ct_lo_done, n - 1)
                sync.dma_start(c_raw[u][:], ctx_t[:, :, bass.ds(n * S, S)]).then_inc(c_loaded[u], 16)

            def place_maxima(n, u):
                sync.wait_ge(m_row_done, n + 1)
                for parity in range(2):
                    for part in range(2):
                        row = SLOT * parity + K3 + part
                        sync.dma_start(qt[u][row:row + 1, EARLY // 2:, :].bitcast(F32),
                                       m_row[u][H * part + EARLY + parity:H * (part + 1):2, :].bitcast(F32)).then_inc(m_placed, 16)

            load(0, 0)
            load(1, 1)
            with sync.Fori(0, (B - R) // 2) as i:
                for u in range(2):
                    load(2 * i + (2 + u), u)
                    place_maxima(2 * i + u, u)
            for n in range(B - R, B):
                place_maxima(n, n % R)

        @block.gpsimd
        def _(pool):
            pool.memset(sel_raw[:], 0.0).then_inc(built, 1)
            pool.memset(q3[:].bitcast(F32), 0.0).then_inc(built, 1)
            pool.memset(k3[:].bitcast(F32), 0.0).then_inc(built, 1)
            for i in range(R):
                pool.memset(va[i][:], 0.0).then_inc(built, 1)
            pool.wait_ge(built, 5)
            pool.memset(k3[:, :, K3:K_MAX].bitcast(F32), -1.0).then_inc(built, 1)
            for i in range(R):
                pool.memset(va[i][:, :, :, DH:DH + 1], 1.0).then_inc(built, 1)
            for k in range(2):
                pool.wait_ge(built, 8 + k)
                pool.affine_select(out=sel_raw[:], in_=sel_raw[:], compare_op=ALU.not_equal, fill=-1.0, base=-H * k,
                                   pattern=[[-1, EARLY], [0, P]], channel_multiplier=1).then_inc(built, 1)

            def split_context(n, u, loads):
                pool.wait_ge(c_loaded[u], 16 * loads)
                alone(pool, kv_done, J * n, passed)
                pool.tensor_copy(ct_hi[:], c_raw[u][:]).then_inc(ct_hi_done, 1)
                pool.wait_ge(ct_hi_done, n + 1)
                pool.tensor_tensor(ct_lo[:], c_raw[u][:], ct_hi[:], ALU.subtract).then_inc(ct_lo_done, 1)

            def rstds(n):
                alone(pool, mv_done, J * n + J, passed)
                pool.tensor_scalar(rstd[:], mean_var[:, :, 1], LN_EPS, None, ALU.add).then_inc(var_eps, 1)
                pool.wait_ge(var_eps, n + 1)
                pool.tensor_tensor(rstd[:], rstd[:], half_neg[:, 0:J], ALU.pow).then_inc(rstd_done, 1)

            def values(n, u):
                pool.wait_ge(v_done, J * n + J)
                alone(pool, pv_done, (n - 1) * H, passed)
                pool.tensor_copy(va[u][:, :, :, 0:DH], v_tmp[:].rearrange("p j (h d) -> p j h d", d=DH)).then_inc(va_done, 1)

            split_context(0, 0, 1)
            rstds(0)
            values(0, 0)
            rstds(1)
            split_context(1, 1, 1)

            def body(n, u, loads):
                if has(n, below=B - 1):
                    values(n + 1, 1 - u)
                if has(n, below=B - 2):
                    rstds(n + 2)
                    split_context(n + 2, u, loads)

            body(0, 0, 2)
            with pool.Fori(0, (B - 4) // 2) as i:
                for u in range(2):
                    body(2 * i + (1 + u), (1 + u) % 2, i + (2 + u))
            for n in range(B - 3, B):
                body(n, n % 2, n // 2 + 2)

        @block.scalar
        def _(act):
            def split_zt(n):
                act.wait_ge(zt_done, n + 1)
                act.activation(zt_hi[:], even[:], ACT.Copy).then_inc(zt_hi_done, 1)

            def three_rows(t3, tiles, at, src, scale):
                out = t3[:, tiles, 0:K3].rearrange("p h (r d) -> p h r d", r=3)[:, :, at, :]
                n = src.shape[1] // DH
                src = src.rearrange("p (h a d) -> p h a d", a=1, d=DH).broadcast_to([P, n, 2, DH])
                return act.activation(out, src, ACT.Copy, scale=scale)

            def split_q(n):
                act.wait_ge(q_done, n + 1)
                three_rows(q3, slice(0, J * H), slice(0, 2), odd[:].rearrange("p j d -> p (j d)"), SCALE).then_inc(q_hi_done, 1)

            def split_kv(n, j):
                act.wait_ge(kv_done, J * n + j + 1)
                after(act, va_done, n)
                bank = (even, odd)[j]
                three_rows(k3, slice(j * H, (j + 1) * H), slice(0, 3, 2), bank[:, 0, :], 1.0).then_inc(k_hi_done, 1)
                act.activation(v_tmp[:, j, :], bank[:, 1, :], ACT.Copy).then_inc(v_done, 1)

            def read_turned(n, u, g):
                act.wait_ge(turned, 2 * (FILLS * n + g) + 1)
                after(act, t_done, (n - 1) * H)
                act.activation(qt[u][:, 2 * g:2 * g + 2, :], even[:], ACT.Copy).then_inc(q_read, 1)

            def max_rows(n, u):
                act.wait_ge(m_turned, n + 1)
                act.activation(m_row[u][:], even[0:2 * H, 0, :], ACT.Copy).then_inc(m_row_done, 1)

            def exps(n, u, h):
                act.wait_ge(t_done, n * H + h + 1)
                after(act, pv_done, n * H + h + 1 - PR)
                act.activation(probs[h % PR][:], t_ps[h % R][:], ACT.Exp).then_inc(exp_done, 1)

            def read_outputs(n, f):
                act.wait_ge(pv_done, n * H + (f + 1) * H // 2)
                after(act, o_turned, 2 * (n - 1) + f + 1)
                act.activation(ot[:, f], o_ps[f][:], ACT.Copy).then_inc(ot_done, 1)

            def split_yt(n):
                act.wait_ge(yt_done, n + 1)
                act.activation(yt_hi[:], even[:], ACT.Copy).then_inc(yt_hi_done, 1)

            act.wait_ge(built, 10)
            for n in range(2):
                split_zt(n)
                split_q(n)
                for j in range(J):
                    split_kv(n, j)
                if n == 0:
                    for g in range(FILLS):
                        read_turned(0, 0, g)
            max_rows(0, 0)

            def body(n, u):
                for h in range(H):
                    exps(n, u, h)
                    if has(n, below=B - 1):
                        for g in range(FILLS)[FILLS_PER_SLOT * h:FILLS_PER_SLOT * (h + 1)]:
                            read_turned(n + 1, 1 - u, g)
                    if has(n, least=1):
                        if h == 2:
                            read_outputs(n - 1, 1)
                        if h == 5:
                            split_yt(n - 1)
                    if h == 10:
                        read_outputs(n, 0)
                    if has(n, below=B - 2):
                        if h == 9:
                            split_zt(n + 2)
                        if h == 11:
                            split_q(n + 2)
                        if h in (12, 13):
                            split_kv(n + 2, h - 12)
                    if has(n, below=B - 1) and h == 15:
                        max_rows(n + 1, 1 - u)

            all_batches(act, body)
            read_outputs(B - 1, 1)
            split_yt(B - 1)

        @block.vector
        def _(dve):
            dve.wait_ge(w_loaded, 48)
            dve.tensor_scalar(w_raw[:, :, 3 * D:], w_raw[:, :, 3 * D:], tanh_g[:, 1:2], None, ALU.mult).then_inc(prep, 1)
            dve.wait_ge(prep, 1)
            dve.tensor_copy(w_hi[:], w_raw[:]).then_inc(prep, 1)
            dve.wait_ge(prep, 2)
            dve.tensor_tensor(w_lo[:], w_raw[:], w_hi[:], ALU.subtract).then_inc(w_ready, 1)
            dve.wait_ge(built, 10)
            dve.tensor_copy(sel[:], sel_raw[:]).then_inc(w_ready, 1)

            def stat(n):
                for j in range(J):
                    dve.bn_stats(stats[:, j, :], x_all[:, J * n + j, :]).then_inc(stats_done, 1)
                for j in range(J):
                    alone(dve, stats_done, J * n + j + 1, passed)
                    dve.bn_aggr(mean_var[:, j, :], stats[:, j, :]).then_inc(mv_done, 1)

            def norm(n):
                dve.wait_ge(rstd_done, n + 1)
                for j in range(J):
                    dve.tensor_scalar(z[:, j, :], x_all[:, J * n + j, :], mean_var[:, j, 0:1], rstd[:, j:j + 1],
                                      ALU.subtract, ALU.mult).then_inc(z_done, 1)

            def split_zt(n):
                dve.wait_ge(zt_hi_done, n + 1)
                dve.tensor_tensor(zt_lo[:], even[:], zt_hi[:], ALU.subtract).then_inc(zt_lo_done, 1)

            def split_q(n):
                dve.wait_ge(q_hi_done, n + 1)
                dve.scalar_tensor_tensor(out=q3[:, :, 2 * DH:K3], in0=odd[:].rearrange("p j (h d) -> p (j h) d", d=DH),
                                         scalar=SCALE, in1=q3[:, :, 0:DH], op0=ALU.mult, op1=ALU.subtract).then_inc(q_lo_done, 1)

            def split_kv(n, j):
                dve.wait_ge(k_hi_done, J * n + j + 1)
                dve.wait_ge(v_done, J * n + j + 1)
                t = slice(j * H, (j + 1) * H)
                dve.tensor_tensor(k3[:, t, DH:2 * DH], (even, odd)[j][:, 0, :].rearrange("p (h d) -> p h d", d=DH),
                                  k3[:, t, 0:DH], ALU.subtract).then_inc(k_lo_done, 1)

            def read_turned(n, u, g):
                dve.wait_ge(turned, 2 * (FILLS * n + g) + 2)
                after(dve, t_done, (n - 1) * H)
                dve.tensor_copy(kt[u][:, 2 * g:2 * g + 2, :], odd[:]).then_inc(k_read, 1)

            def maximum(n, h):
                dve.wait_ge(s_done, n * H + h + 1)
                dve.tensor_reduce(mx[:, :, h:h + 1], s_ps[h % R][:], AX.X, ALU.max).then_inc(max_done, 1)

            def split_max(n):
                dve.wait_ge(max_done, n * H + H)
                dve.tensor_copy(m_tok[:, :, 0:H], mx[:]).then_inc(m_hi_done, 1)
                dve.wait_ge(m_hi_done, n + 1)
                dve.tensor_tensor(m_tok[:, :, H:], mx[:], m_tok[:, :, 0:H], ALU.subtract).then_inc(m_tok_done, 1)

            def normalise(n, f):
                dve.wait_ge(o_turned, 2 * n + f + 1)
                bank = (even, odd)[f][:].rearrange("p a (j g d) -> p a j g d", j=J, g=GH)
                for j in range(J):
                    r = rden[:, j, f * H // 2:(f + 1) * H // 2].rearrange("p (a g) -> p a g", a=2)
                    dve.reciprocal(r, bank[:, :, j, :, DH]).then_inc(rden_done, 1)
                for j in range(J):
                    dve.wait_ge(rden_done, (2 * n + f) * J + j + 1)
                    r = rden[:, j, f * H // 2:(f + 1) * H // 2].rearrange("p (a g x) -> p a g x", a=2, x=1)
                    out = yn[:, j, f * H // 2:(f + 1) * H // 2, :].rearrange("p (a g) d -> p a g d", a=2)
                    dve.tensor_tensor(out, bank[:, :, j, :, 0:DH], r.broadcast_to([P, 2, GH, DH]), ALU.mult).then_inc(y_done, 1)

            def split_yt(n):
                dve.wait_ge(yt_hi_done, n + 1)
                dve.tensor_tensor(yt_lo[:], even[:], yt_hi[:], ALU.subtract).then_inc(yt_lo_done, 1)

            def add_x(n):
                dve.wait_ge(out_done, n + 1)
                xs = x_all[:, bass.ds(J * n, J), :]
                dve.tensor_tensor(xs, xs, odd[:], ALU.add).then_inc(x_done, 1)

            stat(0)
            norm(0)
            for n in range(2):
                split_zt(n)
                split_q(n)
                for j in range(J):
                    split_kv(n, j)
                if n == 0:
                    stat(1)
                    norm(1)
                    for g in range(FILLS):
                        read_turned(0, 0, g)
            for h in range(H):
                maximum(0, h)
            split_max(0)

            def body(n, u):
                for h in range(H):
                    if has(n, below=B - 2):
                        if h == 0:
                            stat(n + 2)
                        if h == 2:
                            norm(n + 2)
                    if has(n, below=B - 1):
                        for g in range(FILLS)[FILLS_PER_SLOT * h:FILLS_PER_SLOT * (h + 1)]:
                            read_turned(n + 1, 1 - u, g)
                        for k in MAX_SLOTS.get(h, ()):
                            maximum(n + 1, k)
                        if h == 14:
                            split_max(n + 1)
                    if has(n, least=1):
                        if h == 4:
                            normalise(n - 1, 0)
                            normalise(n - 1, 1)
                        if h == 7:
                            split_yt(n - 1)
                        if h == 8:
                            add_x(n - 1)
                    if has(n, below=B - 2):
                        if h == 9:
                            split_zt(n + 2)
                        if h == 11:
                            split_q(n + 2)
                        if h in (13, 14):
                            split_kv(n + 2, h - 13)

            all_batches(dve, body)
            normalise(B - 1, 0)
            normalise(B - 1, 1)
            split_yt(B - 1)
            add_x(B - 1)
            dve.wait_ge(x_done, B)

        @block.tensor
        def _(pe):
            def banks_free(n, kinds):
                for s, v in kinds:
                    after(pe, s, v)

            def transpose_z(n):
                pe.wait_ge(z_done, J * n + J)
                after(pe, q_read, FILLS * n)
                after(pe, yt_lo_done, n - 2)
                after(pe, m_row_done, n - 1)
                for c in range(2):
                    for j in range(J):
                        mm = pe.transpose(even[:, c, j * P:(j + 1) * P], z[:, j, c * P:(c + 1) * P], ident[:])
                mm.then_inc(zt_done, 1)

            def project_q(n):
                pe.wait_ge(zt_lo_done, n + 1)
                after(pe, k_read, FILLS * n)
                after(pe, x_done, n - 2)
                for j in range(J):
                    cols = slice(j * P, (j + 1) * P)
                    for c in range(2):
                        mm = three_passes(pe, odd[:, j, :], (zt_hi[:, c, cols], zt_lo[:, c, cols]),
                                          (w_hi[:, c, 0:D], w_lo[:, c, 0:D]), c == 0, c == 1)
                mm.then_inc(q_done, 1)

            def project_kv(n, j):
                bank = (even, odd)[j]
                pe.wait_ge(ct_lo_done, n + 1)
                if j == 0:
                    pe.wait_ge(zt_lo_done, n + 1)
                else:
                    pe.wait_ge(q_lo_done, n + 1)
                cols = slice(j * P, (j + 1) * P)
                for c in range(2):
                    mm = three_passes(pe, bank[:].rearrange("p j d -> p (j d)"), (ct_hi[:, c, cols], ct_lo[:, c, cols]),
                                      (w_hi[:, c, D:3 * D], w_lo[:, c, D:3 * D]), c == 0, c == 1)
                mm.then_inc(kv_done, 1)

            def turn(n, f):
                if f == 0:
                    pe.wait_ge(q_lo_done, n + 1)
                    pe.wait_ge(k_lo_done, J * n + J)
                    after(pe, m_row_done, n)
                else:
                    after(pe, (q_read, k_read)[f % 2], FILLS * n + f // 2)
                g = f // 2
                src, bank = (q3, k3)[f % 2], (even, odd)[f % 2]
                for a in range(2):
                    for j in range(J):
                        h = j * H + 2 * (2 * g + a)
                        mm = pe.transpose(bank[:, a, j * P:(j + 1) * P],
                                          src[:, h:h + 2, :].rearrange("p h r -> p (h r)").bitcast(F32), ident[:])
                mm.then_inc(turned, 1)

            def scores(n, u, h):
                after(pe, max_done, n * H + h + 1 - R)
                pe.wait_ge(q_read, FILLS * n + h // 4 + 1)
                pe.wait_ge(k_read, FILLS * n + h // 4 + 1)
                rows, pair = slice(SLOT * (h % 2), SLOT * (h % 2) + K3), h // 2
                for j in range(J):
                    mm = pe.matmul(s_ps[h % R][:, j, :], qt[u][rows, pair, j * P:(j + 1) * P], kt[u][rows, pair, :],
                                   start=True, stop=True)
                mm.then_inc(s_done, 1)

            def turn_max(n):
                pe.wait_ge(m_tok_done, n + 1)
                pe.wait_ge(q_read, FILLS * n + FILLS)
                after(pe, yt_lo_done, n - 1)
                pe.wait_ge(k_lo_done, min(J * n + 2 * J, J * B) if isinstance(n, int) else J * n + 2 * J)
                for j in range(J):
                    mm = pe.transpose(even[0:2 * H, 0, j * P:(j + 1) * P], m_tok[:, j, :].bitcast(F32), ident[:])
                mm.then_inc(m_turned, 1)

            def shifted_scores(n, u, h):
                after(pe, exp_done, n * H + h + 1 - R)
                if h == 0:
                    pe.wait_ge(m_row_done, n + 1)
                if h == EARLY:
                    pe.wait_ge(m_placed, 64 * (n + 1))
                early = h < EARLY
                rows, pair = slice(SLOT * (h % 2), SLOT * (h % 2) + (K3 if early else K_MAX)), h // 2
                for i in range(J):
                    mm = pe.matmul(t_ps[h % R][:, i, :], kt[u][rows, pair, i * P:(i + 1) * P], qt[u][rows, pair, :],
                                   start=True, stop=not early)
                    if early:
                        mm = pe.matmul(t_ps[h % R][:, i, :], sel[:, h, :], m_row[u][:], start=False, stop=True)
                mm.then_inc(t_done, 1)

            def weigh_values(n, u, h):
                pe.wait_ge(exp_done, n * H + h + 1)
                if h == 0:
                    pe.wait_ge(va_done, n + 1)
                if h % (H // 2) == 0:
                    after(pe, ot_done, 2 * (n - 1) + 2 * h // H + 1)
                out = o_ps[2 * h // H][OSLOT * (h % GH):OSLOT * (h % GH + 1), h // GH % 2, :]
                for i in range(J):
                    mm = pe.matmul(out, va[u][:, i, h, :], probs[h % PR][:, i, :], start=(i == 0), stop=(i == J - 1))
                mm.then_inc(pv_done, 1)

            def turn_outputs(n, f):
                pe.wait_ge(ot_done, 2 * n + f + 1)
                for read in (q_read, k_read):
                    pe.wait_ge(read, min(FILLS * (n + 3), FILLS * B) if isinstance(n, int) else FILLS * (n + 3))
                pe.wait_ge(m_row_done, min(n + 2, B) if isinstance(n, int) else n + 2)
                pe.wait_ge(k_lo_done, min(J * (n + 3), J * B) if isinstance(n, int) else J * (n + 3))
                after(pe, (yt_lo_done, x_done)[f], n)
                for a in range(2):
                    for j in range(J):
                        mm = pe.transpose((even, odd)[f][:, a, j * P:(j + 1) * P], ot[:, f, a, j * P:(j + 1) * P], ident[:])
                mm.then_inc(o_turned, 1)

            def transpose_y(n):
                pe.wait_ge(y_done, 2 * J * n + 2 * J)
                for c in range(2):
                    for j in range(J):
                        mm = pe.transpose(even[:, c, j * P:(j + 1) * P],
                                          yn[:, j].rearrange("p h d -> p (h d)")[:, c * P:(c + 1) * P], ident[:])
                mm.then_inc(yt_done, 1)

            def project_out(n):
                pe.wait_ge(yt_lo_done, n + 1)
                for j in range(J):
                    cols = slice(j * P, (j + 1) * P)
                    for c in range(2):
                        mm = three_passes(pe, odd[:, j, :], (yt_hi[:, c, cols], yt_lo[:, c, cols]),
                                          (w_hi[:, c, 3 * D:], w_lo[:, c, 3 * D:]), c == 0, c == 1)
                mm.then_inc(out_done, 1)

            pe.wait_ge(w_ready, 2)
            for n in range(2):
                transpose_z(n)
                project_q(n)
                for j in range(J):
                    project_kv(n, j)
                if n == 0:
                    for f in range(2 * FILLS):
                        turn(0, f)
            for h in range(H):
                scores(0, 0, h)
            turn_max(0)

            def body(n, u):
                for h in range(H):
                    shifted_scores(n, u, h)
                    if h >= LAG:
                        weigh_values(n, u, h - LAG)
                    elif has(n, least=1):
                        weigh_values(n - 1, 1 - u, H - LAG + h)
                    if has(n, below=B - 1):
                        for f in range(2 * FILLS)[2 * FILLS_PER_SLOT * h:2 * FILLS_PER_SLOT * (h + 1)]:
                            turn(n + 1, f)
                        for k in MAX_SLOTS.get(h, ()):
                            scores(n + 1, 1 - u, k)
                    if has(n, least=1):
                        if h == 4:
                            turn_outputs(n - 1, 0)
                            turn_outputs(n - 1, 1)
                        if h == 6:
                            transpose_y(n - 1)
                        if h == 8:
                            project_out(n - 1)
                    if has(n, below=B - 2):
                        if h == 8:
                            transpose_z(n + 2)
                        if h == 11:
                            project_q(n + 2)
                        if h in (11, 12):
                            project_kv(n + 2, h - 11)
                    if has(n, below=B - 1) and h == 15:
                        turn_max(n + 1)

            all_batches(pe, body)
            for h in range(H - LAG, H):
                weigh_values(B - 1, (B - 1) % R, h)
            turn_outputs(B - 1, 0)
            turn_outputs(B - 1, 1)
            transpose_y(B - 1)
            project_out(B - 1)


def moe_sizes(x_all, router_w, w1_in):
    class S:
        D, E, NE, FF = 256, router_w.shape[2], w1_in.shape[0], w1_in.shape[3]
        TILES = x_all.shape[1]
        T = 2
        TOK = T * P
        CHUNKS = TILES // T
        KD, KF = D // P, FF // P
        TOP = 2
        ROWS = (TILES + 1) * P
        PAIR_TILES = TOP * TILES + E - 1
        BIAS_LO = 32
        BIAS_ROWS = BIAS_LO + NE
    return S


def phase_moe(nc, x_all, tanh_g, ident, half_neg, passed, router_w, router_b, w1_in, b1_in, b1_rows, w2_in, b2_in, out):
    S = moe_sizes(x_all, router_w, w1_in)
    z_rows = nc.dram_tensor("d_z_rows", [(S.E + 1) * S.ROWS, S.D], F32, kind="Internal").ap()
    y_rows = nc.dram_tensor("d_y_rows", [S.PAIR_TILES * P, S.D], F32, kind="Internal").ap()
    zt_kept = nc.dram_tensor("d_zt_kept", [S.CHUNKS, P, 2, S.KD * S.TOK], F32, kind="Internal").ap()
    with ExitStack() as ctx:
        def sb(name, shape, dt=F32):
            return ctx.enter_context(nc.sbuf_tensor("d_" + name, shape, dt))

        class M:
            prob = sb("prob", [P, S.TILES, S.TOP])
            pos = sb("pos", [P, S.TILES, S.TOP], mybir.dt.int32)
            count = sb("count", [P, S.E])
            tiles_at = sb("tiles_at", [1, 2, S.PAIR_TILES], mybir.dt.int32)
            own = sb("own", [S.BIAS_ROWS, S.PAIR_TILES])
            bias1, bias2 = sb("bias1", [S.BIAS_ROWS, S.FF], F32R), sb("bias2", [S.BIAS_ROWS, S.D], F32R)
            ones = sb("ones", [S.BIAS_ROWS, P])
            shared_row = sb("shared_row", [S.BIAS_ROWS, S.NE - S.E, P], F32R)
            rows_of = sb("rows_of", [S.BIAS_ROWS, S.NE])
            half_tanh = sb("half_tanh", [P, 1])
            w1_lo, w2_lo = sb("w1_lo", [P, S.E, S.KD, S.FF], F32R), sb("w2_lo", [P, S.E, S.KF, S.D], F32R)
            experts_loaded = ctx.enter_context(nc.semaphore("d_experts_loaded"))

        moe_route(nc, S, M, x_all, tanh_g, ident, half_neg, passed, router_w, router_b, w1_in, b1_in, b1_rows, w2_in, b2_in,
                  z_rows, zt_kept)
        moe_experts(nc, S, M, ident, passed, z_rows, y_rows)
        moe_combine(nc, S, M, x_all, passed, w1_in, b1_in, w2_in, zt_kept, y_rows, out)


def moe_route(nc, S, M, x_all, tanh_g, ident, half_neg, passed, router_w, router_b, w1_in, b1_in, b1_rows, w2_in, b2_in,
              z_rows, zt_kept):
    E, NE, KD, KF, FF, D, T, TOK, TOP = S.E, S.NE, S.KD, S.KF, S.FF, S.D, S.T, S.TOK, S.TOP
    HR, GR = 4, 4
    I32 = mybir.dt.int32
    ORDER = (("hidden", 0), ("turn", 1), ("rank", 0), ("output0", -1), ("output1", -1), ("gates", 1), ("stats", 2), ("norm", 2))
    with ExitStack() as ctx:
        def sb(name, shape, dt=F32):
            return ctx.enter_context(nc.sbuf_tensor("dr_" + name, shape, dt))

        sem = cleared_semaphores(nc, ctx, "dr_")

        def ps(name, shape):
            return ctx.enter_context(nc.psum_tensor("dr_" + name, shape, F32))

        zt_hi, zt_lo = [sb(f"zt_hi{u}", [P, KD, TOK], F32R) for u in range(2)], [sb(f"zt_lo{u}", [P, KD, TOK], F32R) for u in range(2)]
        rw_raw = sb("rw_raw", [P, KD, E])
        rw_hi, rw_lo = sb("rw_hi", [P, KD, E], F32R), sb("rw_lo", [P, KD, E], F32R)
        rb = sb("rb", [P, E])
        b1 = sb("b1", [P, NE, KF])
        b_raw1, b_raw2 = sb("b_raw1", [S.BIAS_ROWS, FF]), sb("b_raw2", [S.BIAS_ROWS, D])
        expert = sb("expert", [P, E])
        above = sb("above", [P, 2, P], BF16)
        stats, mean_var, rstd = sb("stats", [P, T, 6]), sb("mean_var", [P, T, 2]), sb("rstd", [P, T])
        z = [sb(f"z{u}", [P, T, D]) for u in range(2)]
        gates, top = sb("gates", [P, T, E]), sb("top", [P, T, 8])
        top_i, top_f = sb("top_i", [P, T, 8], mybir.dt.uint32), sb("top_f", [P, T, TOP])
        pick = sb("pick", [P, T, TOP, E])
        both = sb("both", [P, T, E], BF16)
        row, row_k = sb("row", [P, T, E]), sb("row_k", [P, T, TOP, E])
        pos_f = sb("pos_f", [P, T, TOP])
        pos_all, past_region = sb("pos_all", [P, S.TILES, TOP]), sb("past_region", [P, E, S.TILES, TOP])
        pos_u = [[sb(f"pos_u{u}_{k}", [P, 1], I32) for k in range(T * TOP)] for u in range(2)]
        diff, den = sb("diff", [P, S.TILES]), sb("den", [P, S.TILES])
        w1_raw, w2_raw = sb("w1_raw", [P, KD, FF]), sb("w2_raw", [P, KF, D])
        w1_hi, w1_lo = sb("w1_hi", [P, KD, FF], F32R), sb("w1_lo", [P, KD, FF], F32R)
        w2_hi, w2_lo = sb("w2_hi", [P, KF, D], F32R), sb("w2_lo", [P, KF, D], F32R)
        g_full = sb("g_full", [P, GR, TOK])
        g_hi, g_lo = [sb(f"g_hi{u}", [P, KF, TOK], F32R) for u in range(2)], [sb(f"g_lo{u}", [P, KF, TOK], F32R) for u in range(2)]
        zeros = sb("zeros", [P, D])
        tile_no = sb("tile_no", [S.BIAS_ROWS, S.PAIR_TILES])
        cnt, tiles, ends = sb("cnt", [P, E]), sb("tiles", [P, E]), sb("ends", [P, E + 1])
        base, base_step = sb("base", [P, E + 1]), sb("base_step", [P, E])
        mine, bounds = sb("mine", [S.BIAS_ROWS, 2, E]), sb("bounds", [S.BIAS_ROWS, 2])
        past = sb("past", [1, E, S.PAIR_TILES])
        tab = sb("tab", [1, 2, S.PAIR_TILES])
        own_b = sb("own_b", [S.BIAS_ROWS, S.PAIR_TILES])
        zero1 = sb("zero1", [P, E])
        pad_f, pad_i = sb("pad_f", [P, E + 1]), [sb(f"pad_i{e}", [P, 1], I32) for e in range(E + 1)]
        lane = sb("lane", [P, 1])

        hid = [ps(f"hid{i}", [P, 512]) for i in range(HR)]
        y = [ps(f"y{i}", [P, 512]) for i in range(T)]
        zt_ps = ps("zt_ps", [P, KD, TOK])
        r_ps = ps("r_ps", [P, 512])
        rank_ps = r_ps[:, 256:512]

        small_loaded, shared_loaded, ready = sem("small_loaded"), sem("shared_loaded"), sem("ready")
        pool_ready, act_ready, setup_chain = sem("pool_ready"), sem("act_ready"), sem("setup_chain")
        stats_done, mv_done, var_eps, rstd_done = sem("stats_done"), sem("mv_done"), sem("var_eps"), sem("rstd_done")
        z_done, zt_done, zt_hi_done, zt_lo_done = sem("z_done"), sem("zt_done"), sem("zt_hi_done"), sem("zt_lo_done")
        gates_done, both_done, rank_done, pos_done, pos_kept = sem("gates_done"), sem("both_done"), sem("rank_done"), sem("pos_done"), sem("pos_kept")
        route, ranked = sem("route"), sem("ranked")
        hid_done, gelu_hi, gelu_full, gelu_lo = sem("hid_done"), sem("gelu_hi"), sem("gelu_full"), sem("gelu_lo")
        y_done, x_added = sem("y_done"), sem("x_added")
        scattered = [sem(f"scattered{u}") for u in range(2)]
        zt_stored = [sem(f"zt_stored{u}") for u in range(2)]
        padded = sem("padded")
        diff_done, exp_done, last, pads_done = sem("diff_done"), sem("exp_done"), sem("last"), sem("pads_done")
        block = ctx.enter_context(nc.Block())

        def before(n, u, per):
            return per * (n // 2) if isinstance(n, int) else per // 2 * (n - u)

        @block.sync
        def _(sync):
            for dst, src in ((rw_raw[:], router_w), (b1[:], b1_in), (rb[:], router_b.partition_broadcast(P))):
                sync.dma_start(dst, src).then_inc(small_loaded, 16)
            sync.dma_start(w1_raw[:], w1_in[E]).then_inc(shared_loaded, 16)
            sync.dma_start(w2_raw[:], w2_in[E]).then_inc(shared_loaded, 16)
            sync.wait_ge(pool_ready, 1)
            for at in (0, S.BIAS_LO):
                sync.dma_start(b_raw1[at:at + NE, :], b1_rows).then_inc(small_loaded, 16)
                sync.dma_start(b_raw2[at:at + NE, :], b2_in).then_inc(small_loaded, 16)
            for e in range(E):
                sync.dma_start(M.w1_lo[:, e].bitcast(F32), w1_in[e]).then_inc(M.experts_loaded, 16)
                sync.dma_start(M.w2_lo[:, e].bitcast(F32), w2_in[e]).then_inc(M.experts_loaded, 16)

            def keep(n, u):
                sync.wait_ge(zt_lo_done, n + 1)
                for k, part in enumerate((zt_hi, zt_lo)):
                    dst = zt_kept[bass.ds(n, 1), :, k].rearrange("n p f -> p (n f)")
                    sync.dma_start(dst, part[u][:].rearrange("p c t -> p (c t)").bitcast(F32)).then_inc(zt_stored[u], 16)

            with sync.Fori(0, S.CHUNKS // 2) as i:
                for u in range(2):
                    keep(2 * i + u, u)
            for u in range(2):
                sync.wait_ge(zt_stored[u], 32 * S.CHUNKS // 2)

        @block.gpsimd
        def _(pool):
            pool.memset(b_raw1[:], 0.0)
            pool.memset(b_raw2[:], 0.0).then_inc(pool_ready, 1)
            pool.memset(above[:], 1.0).then_inc(pool_ready, 1)
            pool.memset(zeros[:], 0.0)
            pool.memset(M.ones[:], 1.0)
            pool.iota(expert[:], pattern=[[1, E]], base=0, channel_multiplier=0, allow_small_or_imprecise_dtypes=True)
            pool.iota(M.count[:], pattern=[[S.ROWS, E]], base=0, channel_multiplier=0, allow_small_or_imprecise_dtypes=True)
            pool.iota(base[:], pattern=[[S.ROWS, E + 1]], base=0, channel_multiplier=0, allow_small_or_imprecise_dtypes=True)
            pool.iota(tile_no[:], pattern=[[1, S.PAIR_TILES]], base=0, channel_multiplier=0, allow_small_or_imprecise_dtypes=True)
            pool.iota(lane[:], pattern=[[0, 1]], base=0, channel_multiplier=1, allow_small_or_imprecise_dtypes=True)
            pool.wait_ge(pool_ready, 2)
            pool.affine_select(out=above[:, 0, :], in_=above[:, 0, :], compare_op=ALU.is_gt, fill=0.0, base=0,
                               pattern=[[1, P]], channel_multiplier=-1).then_inc(pool_ready, 1)

            def stats_part(n, u):
                alone(pool, mv_done, T * (n + 1), passed)
                pool.tensor_scalar(rstd[:], mean_var[:, :, 1:2].rearrange("p t a -> p (t a)"), LN_EPS, None, ALU.add).then_inc(var_eps, 1)
                pool.wait_ge(var_eps, n + 1)
                pool.tensor_tensor(rstd[:], rstd[:], half_neg[:, 0:T], ALU.pow).then_inc(rstd_done, 1)

            def scatter(n, u):
                alone(pool, pos_done, n + 1, passed)
                for k in range(T * TOP):
                    pool.indirect_dma_start(z_rows, bass.IndirectOffsetOnAxis(ap=pos_u[u][k][:], axis=0),
                                            z[u][:, k // TOP, :], None).then_inc(scattered[u], 16)

            pipeline(pool, S.CHUNKS, ORDER, {"stats": stats_part, "rank": scatter})
            pool.wait_ge(pads_done, E + 1)
            for e in range(E + 1):
                pool.indirect_dma_start(z_rows, bass.IndirectOffsetOnAxis(ap=pad_i[e][:], axis=0), zeros[:],
                                        None).then_inc(padded, 16)
            pool.wait_ge(padded, 16 * (E + 1))
            for u in range(2):
                pool.wait_ge(scattered[u], 16 * T * TOP * S.CHUNKS // 2)

        @block.scalar
        def _(act):
            act.wait_ge(small_loaded, 112)
            act.activation(M.bias1[:], b_raw1[:], ACT.Copy).then_inc(act_ready, 1)
            act.activation(M.bias2[:], b_raw2[:], ACT.Copy).then_inc(act_ready, 1)
            act.wait_ge(shared_loaded, 32)
            act.activation(w1_hi[:], w1_raw[:], ACT.Copy).then_inc(act_ready, 1)
            act.activation(w2_hi[:], w2_raw[:], ACT.Copy).then_inc(act_ready, 1)

            def hidden(n, u):
                for m in range(KF):
                    act.wait_ge(hid_done, n * KF + m + 1)
                    alone(act, gelu_lo, n * KF + m + 1 - GR, passed)
                    if m == 0:
                        after(act, y_done, T * (n - 1))
                    act.activation(g_full[:, m % GR, :], hid[m % HR][:, 0:TOK], ACT.Gelu, bias=b1[:, E, m:m + 1]).then_inc(gelu_full, 1)
                    act.activation(g_hi[u][:, m, :], hid[m % HR][:, 0:TOK], ACT.Gelu, bias=b1[:, E, m:m + 1]).then_inc(gelu_hi, 1)

            def turn(n, u):
                act.wait_ge(zt_done, n + 1)
                after(act, zt_stored[u], before(n, u, 32))
                after(act, hid_done, KF * (n - 1))
                act.activation(zt_hi[u][:], zt_ps[:], ACT.Copy).then_inc(zt_hi_done, 1)

            pipeline(act, S.CHUNKS, ORDER, {"hidden": hidden, "turn": turn})
            act.wait_ge(diff_done, S.CHUNKS)
            act.activation(den[:], diff[:], ACT.Exp).then_inc(exp_done, 1)

        @block.vector
        def _(dve):
            dve.wait_ge(small_loaded, 112)
            dve.tensor_copy(rw_hi[:], rw_raw[:]).then_inc(ready, 1)
            dve.wait_ge(ready, 1)
            dve.tensor_tensor(rw_lo[:], rw_raw[:], rw_hi[:], ALU.subtract).then_inc(ready, 1)
            dve.wait_ge(act_ready, 4)
            lo = slice(S.BIAS_LO, S.BIAS_ROWS)
            dve.tensor_tensor(M.bias1[lo, :], b_raw1[lo, :], M.bias1[lo, :], ALU.subtract).then_inc(ready, 1)
            dve.tensor_tensor(M.bias2[lo, :], b_raw2[lo, :], M.bias2[lo, :], ALU.subtract).then_inc(ready, 1)
            dve.tensor_tensor(w1_lo[:], w1_raw[:], w1_hi[:], ALU.subtract).then_inc(ready, 1)
            dve.tensor_tensor(w2_lo[:], w2_raw[:], w2_hi[:], ALU.subtract).then_inc(ready, 1)
            dve.tensor_scalar(M.half_tanh[:], tanh_g[:, 3:4], 1.0 / (NE - E), None, ALU.mult).then_inc(ready, 1)
            dve.memset(zero1[:], 0.0).then_inc(ready, 1)
            n_rows = S.BIAS_ROWS
            dve.tensor_tensor(M.rows_of[:], ident[0:n_rows, 0:NE], ident[0:n_rows, S.BIAS_LO:S.BIAS_LO + NE], ALU.add).then_inc(ready, 1)
            dve.wait_ge(ready, 9)
            dve.wait_ge(pool_ready, 3)
            for k in range(NE - E):
                dve.tensor_scalar(M.shared_row[:, k, :], M.ones[:], M.rows_of[:, E + k:E + k + 1], None, ALU.mult).then_inc(ready, 1)
            dve.wait_ge(ready, 9 + NE - E)
            step, after_pick = Chain(dve, route, 5, passed), Chain(dve, ranked, 2 + 2 * T, passed)

            def hidden(n, u):
                for m in range(KF):
                    dve.wait_ge(gelu_hi, n * KF + m + 1)
                    dve.wait_ge(gelu_full, n * KF + m + 1)
                    dve.tensor_tensor(g_lo[u][:, m, :], g_full[:, m % GR, :], g_hi[u][:, m, :], ALU.subtract).then_inc(gelu_lo, 1)

            def stats_part(n, u):
                for t in range(T):
                    dve.bn_stats(stats[:, t, :], x_all[:, T * n + t, :]).then_inc(stats_done, 1)
                alone(dve, stats_done, T * (n + 1), passed)
                for t in range(T):
                    dve.bn_aggr(mean_var[:, t, :], stats[:, t, :]).then_inc(mv_done, 1)

            def norm(n, u):
                alone(dve, scattered[u], before(n, u, 16 * T * TOP), passed)
                dve.wait_ge(rstd_done, n + 1)
                for t in range(T):
                    dve.tensor_scalar(z[u][:, t, :], x_all[:, T * n + t, :], mean_var[:, t, 0:1], rstd[:, t:t + 1],
                                      ALU.subtract, ALU.mult).then_inc(z_done, 1)

            def turn(n, u):
                dve.wait_ge(zt_hi_done, n + 1)
                dve.tensor_tensor(zt_lo[u][:], zt_ps[:], zt_hi[u][:], ALU.subtract).then_inc(zt_lo_done, 1)

            def gates_part(n, u):
                step.begin(n)
                dve.wait_ge(gates_done, n + 1)
                step(dve.tensor_tensor(gates[:], r_ps[:, 0:T * E].rearrange("p (t e) -> p t e", t=T),
                                       rb[:].rearrange("p (a e) -> p a e", a=1).broadcast_to([P, T, E]), ALU.add))
                for t in range(T):
                    ins = dve.max(top[:, t, :], gates[:, t, :])
                step(ins)
                for t in range(T):
                    ins = dve.max_index(top_i[:, t, :], top[:, t, :], gates[:, t, :])
                step(ins)
                step(dve.tensor_copy(top_f[:], top_i[:, :, 0:TOP]))
                dve.tensor_tensor(diff[:, bass.ds(T * n, T)], top[:, :, 1:2].rearrange("p t a -> p (t a)"),
                                  top[:, :, 0:1].rearrange("p t a -> p (t a)"), ALU.subtract).then_inc(diff_done, 1)
                step(dve.tensor_tensor(pick[:], expert[:].rearrange("p (a b e) -> p a b e", a=1, b=1).broadcast_to([P, T, TOP, E]),
                                       top_f[:].rearrange("p t (k a) -> p t k a", a=1).broadcast_to([P, T, TOP, E]), ALU.is_equal))
                dve.tensor_tensor(both[:], pick[:, :, 0, :], pick[:, :, 1, :], ALU.add).then_inc(both_done, 1)

            def rank(n, u):
                after_pick.begin(n)
                dve.wait_ge(rank_done, n + 1)
                for t in range(T):
                    after_pick(dve.tensor_tensor(row[:, t, :], rank_ps[:, t * E:(t + 1) * E], M.count[:], ALU.add))
                    after_pick(dve.tensor_tensor(M.count[:], M.count[:], rank_ps[:, (T + t) * E:(T + t + 1) * E], ALU.add))
                after_pick(dve.tensor_tensor(row_k[:], pick[:], row[:].rearrange("p t (a e) -> p t a e", a=1).broadcast_to([P, T, TOP, E]), ALU.mult))
                after_pick(dve.tensor_reduce(pos_f[:], row_k[:], AX.X, ALU.add))
                for k in range(T * TOP):
                    ins = dve.tensor_copy(pos_u[u][k][:], pos_f[:, k // TOP, k % TOP:k % TOP + 1])
                ins.then_inc(pos_done, 1)
                dve.tensor_copy(pos_all[:, bass.ds(T * n, T), :], pos_f[:]).then_inc(pos_kept, 1)

            def output(t, n):
                dve.wait_ge(y_done, T * n + t + 1)
                xs = x_all[:, T * n + t, :]
                dve.scalar_tensor_tensor(out=xs, in0=y[t][:, 0:D], scalar=M.half_tanh[:, 0:1], in1=xs, op0=ALU.mult, op1=ALU.add).then_inc(x_added, 1)

            pipeline(dve, S.CHUNKS, ORDER, {
                "stats": stats_part, "norm": norm, "turn": turn, "gates": gates_part, "rank": rank, "hidden": hidden,
                "output0": lambda n, u: output(0, n), "output1": lambda n, u: output(1, n)})
            dve.wait_ge(pos_kept, S.CHUNKS)
            dve.wait_ge(x_added, S.TILES)
            dve.wait_ge(exp_done, 1)

            chain = Chain(dve, last, 40)
            chain.begin(0)
            second = M.prob[:, :, 1:2].rearrange("p t a -> p (t a)")
            first = M.prob[:, :, 0:1].rearrange("p t a -> p (t a)")
            chain(dve.tensor_scalar(diff[:], den[:], 1.0, None, ALU.add))
            chain(dve.reciprocal(diff[:], diff[:]))
            chain(dve.tensor_scalar(first, diff[:], tanh_g[:, 3:4], None, ALU.mult))
            chain(dve.tensor_tensor(second, first, den[:], ALU.mult))
            chain(dve.tensor_scalar(pad_f[:, 0:E], M.count[:], lane[:, 0:1], None, ALU.add))
            dve.tensor_scalar(pad_f[:, E:E + 1], lane[:], float(E * S.ROWS), None, ALU.add)
            chain(dve.tensor_scalar(cnt[:], expert[:], float(S.ROWS), None, ALU.mult))
            for e in range(E + 1):
                dve.tensor_copy(pad_i[e][:], pad_f[:, e:e + 1]).then_inc(pads_done, 1)
            chain(dve.tensor_tensor(cnt[:], M.count[:], cnt[:], ALU.subtract))
            chain(dve.tensor_scalar(tiles[:], cnt[:], 1.0 / P, (P - 1.0) / P - 0.5 + 0.5 / P, ALU.mult, ALU.add))
            chain(dve.tensor_scalar(tiles[:], tiles[:], ROUND, ROUND, ALU.add, ALU.subtract))
            chain(dve.tensor_copy(ends[:, 0:1], zero1[:, 0:1]))
            chain(dve.tensor_tensor_scan(ends[:, 1:E + 1], tiles[:], zero1[:], 0.0, ALU.add, ALU.add))
            for e in range(E):
                ins = dve.tensor_scalar(past[:, e, :], tile_no[0:1, :], ends[0:1, e + 1:e + 2], None, ALU.is_ge)
            chain(ins)
            chain(dve.scalar_tensor_tensor(out=base[:, 0:E], in0=ends[:, 0:E], scalar=-float(P), in1=base[:, 0:E], op0=ALU.mult, op1=ALU.add))
            chain(dve.tensor_tensor(base_step[:], base[:, 1:E + 1], base[:, 0:E], ALU.subtract))
            dve.tensor_scalar(tab[:, 1, :], tile_no[0:1, :], float(P), None, ALU.mult)
            for e in range(1, E):
                dve.tensor_scalar(past_region[:, e], pos_all[:], float(e * S.ROWS), base_step[:, e - 1:e], ALU.is_ge, ALU.mult)
            chain(dve.tensor_copy(tab[:, 0, :], past[:, 0, :]))
            for e in range(E):
                if e > 0:
                    dve.tensor_tensor(tab[:, 0, :], tab[:, 0, :], past[:, e, :], ALU.add)
                    dve.tensor_tensor(pos_all[:], pos_all[:], past_region[:, e], ALU.subtract)
                chain(dve.scalar_tensor_tensor(out=tab[:, 1, :], in0=past[:, e, :], scalar=base_step[0:1, e:e + 1], in1=tab[:, 1, :],
                                               op0=ALU.mult, op1=ALU.add))
            dve.tensor_copy(M.pos[:], pos_all[:])
            chain(dve.scalar_tensor_tensor(out=past[:, 0, :], in0=tile_no[0:1, :], scalar=-float(P), in1=past[:, E - 1, :], op0=ALU.mult, op1=ALU.mult))
            chain(dve.tensor_tensor(tab[:, 1, :], tab[:, 1, :], past[:, 0, :], ALU.add))
            chain(dve.tensor_scalar(tab[:, 0, :], tab[:, 0, :], float(E - 1), None, ALU.min))
            chain(dve.tensor_copy(M.tiles_at[:], tab[:]))
            for k in range(2):
                ins = dve.tensor_tensor(mine[:, k, :], M.rows_of[:, 0:E], ends[0:n_rows, k:k + E], ALU.mult)
            chain(ins)
            chain(dve.tensor_reduce(bounds[:], mine[:], AX.X, ALU.add))
            dve.tensor_scalar(own_b[:], tile_no[:], bounds[:, 1:2], None, ALU.is_ge)
            chain(dve.tensor_scalar(M.own[:], tile_no[:], bounds[:, 0:1], None, ALU.is_ge))
            chain(dve.tensor_tensor(M.own[:], M.own[:], own_b[:], ALU.subtract))

        @block.tensor
        def _(pe):
            pe.wait_ge(ready, 9 + NE - E)

            def hidden(n, u):
                for m in range(KF):
                    after(pe, gelu_hi, n * KF + m + 1 - HR)
                    cols = slice(m * P, (m + 1) * P)
                    for c in range(KD):
                        mm = three_passes(pe, hid[m % HR][:, 0:TOK], (w1_hi[:, c, cols], w1_lo[:, c, cols]),
                                          (zt_hi[u][:, c, :], zt_lo[u][:, c, :]), c == 0, c == KD - 1)
                    mm.then_inc(hid_done, 1)

            def turn(n, u):
                pe.wait_ge(z_done, T * (n + 1))
                after(pe, zt_lo_done, n)
                for t in range(T):
                    for c in range(KD):
                        mm = pe.transpose(zt_ps[:, c, t * P:(t + 1) * P], z[u][:, t, c * P:(c + 1) * P], ident[:])
                mm.then_inc(zt_done, 1)

            def gates_part(n, u):
                pe.wait_ge(zt_lo_done, n + 1)
                after(pe, pos_done, n)
                for t in range(T):
                    cols = slice(t * P, (t + 1) * P)
                    for c in range(KD):
                        mm = three_passes(pe, r_ps[:, t * E:(t + 1) * E], (zt_hi[u][:, c, cols], zt_lo[u][:, c, cols]),
                                          (rw_hi[:, c, :], rw_lo[:, c, :]), c == 0, c == KD - 1)
                mm.then_inc(gates_done, 1)

            def rank(n, u):
                pe.wait_ge(both_done, n + 1)
                for k in range(2):
                    mm = pe.matmul(rank_ps[:, k * T * E:(k + 1) * T * E], above[:, k, :], both[:].rearrange("p t e -> p (t e)"),
                                   start=True, stop=True)
                mm.then_inc(rank_done, 1)

            def output(t, n, u):
                if t == 0:
                    pe.wait_ge(gelu_lo, (n + 1) * KF)
                after(pe, x_added, T * (n - 1) + t + 1)
                cols = slice(t * P, (t + 1) * P)
                for m in range(KF):
                    three_passes(pe, y[t][:, 0:D], (g_hi[u][:, m, cols], g_lo[u][:, m, cols]),
                                 (w2_hi[:, m, :], w2_lo[:, m, :]), m == 0, False)
                pe.matmul(y[t][:, 0:D], M.shared_row[:, 0, :], M.bias2[:], start=False, stop=True).then_inc(y_done, 1)

            pipeline(pe, S.CHUNKS, ORDER, {"turn": turn, "gates": gates_part, "rank": rank, "hidden": hidden,
                                           "output0": lambda n, u: output(0, n, u), "output1": lambda n, u: output(1, n, u)})


def moe_experts(nc, S, M, ident, passed, z_rows, y_rows):
    E, KD, KF, FF, D = S.E, S.KD, S.KF, S.FF, S.D
    ORDER = (("turn", 0), ("first", 1), ("turn_in", 2), ("second", 0))
    with ExitStack() as ctx:
        def sb(name, shape, dt=F32):
            return [ctx.enter_context(nc.sbuf_tensor(f"de_{name}{u}", shape, dt)) for u in range(2)]

        def ps(name, shape):
            return [ctx.enter_context(nc.psum_tensor(f"de_{name}{u}", shape, F32)) for u in range(2)]

        sem = cleared_semaphores(nc, ctx, "de_")

        w1_hi = ctx.enter_context(nc.sbuf_tensor("de_w1_hi", [P, E, KD, FF], F32R))
        w2_hi = ctx.enter_context(nc.sbuf_tensor("de_w2_hi", [P, E, KF, D], F32R))
        z = sb("z", [P, D])
        own = sb("own", [S.BIAS_ROWS, P], F32R)
        zt_hi, zt_lo = sb("zt_hi", [P, KD, P], F32R), sb("zt_lo", [P, KD, P], F32R)
        g = sb("g", [P, FF])
        gt_hi, gt_lo = sb("gt_hi", [P, KF, P], F32R), sb("gt_lo", [P, KF, P], F32R)
        ys = sb("ys", [P, D])
        h_ps, gt_ps, zt_ps, y_ps = ps("h_ps", [P, FF]), ps("gt_ps", [P, KF, P]), ps("zt_ps", [P, 512]), ps("y_ps", [P, 512])
        z_loaded, stored = [sem(f"z_loaded{u}") for u in range(2)], [sem(f"stored{u}") for u in range(2)]
        hi_done, lo_done = sem("hi_done"), sem("lo_done")
        zt_done, zt_hi_done, zt_lo_done = sem("zt_done"), sem("zt_hi_done"), sem("zt_lo_done")
        own_done, h_done, g_done = sem("own_done"), sem("h_done"), sem("g_done")
        gt_done, gt_hi_done, gt_lo_done = sem("gt_done"), sem("gt_hi_done"), sem("gt_lo_done")
        y_done, y_copied = sem("y_done"), sem("y_copied")
        block = ctx.enter_context(nc.Block())

        def before_last(i, u):
            return 16 * (i // 2) if isinstance(i, int) else 8 * (i - u)

        @block.sync
        def _(sync):
            def store(i, u):
                sync.wait_ge(y_copied, i + 1)
                sync.dma_start(y_rows[bass.ds(i * P, P), :], ys[u][:]).then_inc(stored[u], 16)

            pipeline(sync, S.PAIR_TILES, ORDER, {"second": store})
            for u in range(2):
                sync.wait_ge(stored[u], 16 * ((S.PAIR_TILES + 1 - u) // 2))

        @block.gpsimd
        def _(pool):
            def load(i, u):
                alone(pool, zt_done, i - 1, passed)
                row = pool.value_load(M.tiles_at[:, 1, bass.ds(i, 1)], min_val=0, max_val=(E + 1) * S.ROWS - P)
                pool.dma_start(z[u][:], z_rows[bass.ds(row, P), :]).then_inc(z_loaded[u], 16)

            pipeline(pool, S.PAIR_TILES, ORDER, {"turn_in": load})

        @block.scalar
        def _(act):
            act.wait_ge(M.experts_loaded, 32 * E)
            for e in range(E):
                act.activation(w1_hi[:, e], M.w1_lo[:, e].bitcast(F32), ACT.Copy).then_inc(hi_done, 1)
                act.activation(w2_hi[:, e], M.w2_lo[:, e].bitcast(F32), ACT.Copy).then_inc(hi_done, 1)

            def turn_in(i, u):
                act.wait_ge(zt_done, i + 1)
                after(act, h_done, i - 1)
                act.activation(zt_hi[u][:].rearrange("p c t -> p (c t)"), zt_ps[u][:, 0:D], ACT.Copy).then_inc(zt_hi_done, 1)

            def first(i, u):
                act.wait_ge(h_done, i + 1)
                after(act, gt_done, i - 1)
                act.activation(g[u][:], h_ps[u][:], ACT.Gelu).then_inc(g_done, 1)

            def turn(i, u):
                act.wait_ge(gt_done, i + 1)
                after(act, y_done, i - 1)
                act.activation(gt_hi[u][:], gt_ps[u][:], ACT.Copy).then_inc(gt_hi_done, 1)

            pipeline(act, S.PAIR_TILES, ORDER, {"turn": turn, "first": first, "turn_in": turn_in})

        @block.vector
        def _(dve):
            for e in range(E):
                dve.wait_ge(hi_done, 2 * e + 2)
                for hi, lo in ((w1_hi, M.w1_lo), (w2_hi, M.w2_lo)):
                    dve.tensor_tensor(lo[:, e], lo[:, e].bitcast(F32), hi[:, e], ALU.subtract).then_inc(lo_done, 1)

            def turn_in(i, u):
                dve.wait_ge(zt_hi_done, i + 1)
                dve.tensor_tensor(zt_lo[u][:].rearrange("p c t -> p (c t)"), zt_ps[u][:, 0:D],
                                  zt_hi[u][:].rearrange("p c t -> p (c t)"), ALU.subtract).then_inc(zt_lo_done, 1)

            def turn(i, u):
                dve.wait_ge(gt_hi_done, i + 1)
                dve.tensor_tensor(gt_lo[u][:], gt_ps[u][:], gt_hi[u][:], ALU.subtract).then_inc(gt_lo_done, 1)

            def second(i, u):
                dve.wait_ge(y_done, i + 1)
                after(dve, stored[u], before_last(i, u))
                dve.tensor_copy(ys[u][:], y_ps[u][:, 0:D]).then_inc(y_copied, 1)
                if not (isinstance(i, int) and i + 2 >= S.PAIR_TILES):
                    pick_biases(i + 2, u)

            def pick_biases(i, u):
                after(dve, y_done, i - 1)
                dve.tensor_scalar(own[u][:], M.ones[:], M.own[:, bass.ds(i, 1)], None, ALU.mult).then_inc(own_done, 1)

            for i in range(2):
                pick_biases(i, i)
            pipeline(dve, S.PAIR_TILES, ORDER, {"turn": turn, "turn_in": turn_in, "second": second})

        @block.tensor
        def _(pe):
            def turn_in(i, u):
                after(pe, zt_lo_done, i - 1)
                pe.wait_ge(z_loaded[u], before_last(i, u) + 16)
                for c in range(KD):
                    mm = pe.transpose(zt_ps[u][:, c * P:(c + 1) * P], z[u][:, c * P:(c + 1) * P], ident[:])
                mm.then_inc(zt_done, 1)

            def expert(i):
                return pe.value_load(M.tiles_at[:, 0, bass.ds(i, 1)], min_val=0, max_val=E - 1)

            def first(i, u):
                if isinstance(i, int) and i == 0:
                    pe.wait_ge(lo_done, 2 * E)
                e = expert(i)
                after(pe, g_done, i - 1)
                pe.wait_ge(zt_lo_done, i + 1)
                for c in range(KD):
                    hi, lo = [w[:, bass.ds(e, 1), c, :].rearrange("p e f -> p (e f)") for w in (w1_hi, M.w1_lo)]
                    three_passes(pe, h_ps[u][:], (zt_hi[u][:, c, :], zt_lo[u][:, c, :]), (hi, lo), c == 0, False)
                pe.wait_ge(own_done, i + 1)
                pe.matmul(h_ps[u][:], own[u][:], M.bias1[:], start=False, stop=True).then_inc(h_done, 1)

            def turn(i, u):
                after(pe, gt_lo_done, i - 1)
                pe.wait_ge(g_done, i + 1)
                for m in range(KF):
                    mm = pe.transpose(gt_ps[u][:, m, :], g[u][:, m * P:(m + 1) * P], ident[:])
                mm.then_inc(gt_done, 1)

            def second(i, u):
                e = expert(i)
                after(pe, y_copied, i - 1)
                pe.matmul(y_ps[u][:, 0:D], own[u][:], M.bias2[:], start=True, stop=False)
                pe.wait_ge(gt_lo_done, i + 1)
                for m in range(KF):
                    hi, lo = [w[:, bass.ds(e, 1), m, :].rearrange("p e f -> p (e f)") for w in (w2_hi, M.w2_lo)]
                    mm = three_passes(pe, y_ps[u][:, 0:D], (gt_hi[u][:, m, :], gt_lo[u][:, m, :]), (hi, lo), False, m == KF - 1)
                mm.then_inc(y_done, 1)

            pipeline(pe, S.PAIR_TILES, ORDER, {"turn": turn, "first": first, "turn_in": turn_in, "second": second})


def moe_combine(nc, S, M, x_all, passed, w1_in, b1_in, w2_in, zt_kept, y_rows, out):
    E, NE, KD, KF, FF, D, T, TOK, TOP = S.E, S.NE, S.KD, S.KF, S.FF, S.D, S.T, S.TOK, S.TOP
    HR, GR = 4, 4
    ORDER = (("load", 1), ("hidden", 0), ("outputs", -1))
    with ExitStack() as ctx:
        def sb(name, shape, dt=F32):
            return ctx.enter_context(nc.sbuf_tensor("dc_" + name, shape, dt))

        sem = cleared_semaphores(nc, ctx, "dc_")

        zt = [sb(f"zt{u}", [P, 2, KD, TOK], F32R) for u in range(2)]
        b1 = sb("b1", [P, NE, KF])
        w1_raw, w2_raw = sb("w1_raw", [P, KD, FF]), sb("w2_raw", [P, KF, D])
        w1_hi, w1_lo = sb("w1_hi", [P, KD, FF], F32R), sb("w1_lo", [P, KD, FF], F32R)
        w2_hi, w2_lo = sb("w2_hi", [P, KF, D], F32R), sb("w2_lo", [P, KF, D], F32R)
        g_full = sb("g_full", [P, GR, TOK])
        g_hi, g_lo = [sb(f"g_hi{u}", [P, KF, TOK], F32R) for u in range(2)], [sb(f"g_lo{u}", [P, KF, TOK], F32R) for u in range(2)]
        pos_u = [[sb(f"pos_u{u}_{k}", [P, 1], mybir.dt.int32) for k in range(T * TOP)] for u in range(2)]
        rows = [sb(f"rows{u}", [P, T * TOP, D]) for u in range(2)]
        hid = [ctx.enter_context(nc.psum_tensor(f"dc_hid{i}", [P, 512], F32)) for i in range(HR)]
        y = [ctx.enter_context(nc.psum_tensor(f"dc_y{i}", [P, 512], F32)) for i in range(T)]
        b1_loaded, w_loaded, hi_done, lo_done = sem("b1_loaded"), sem("w_loaded"), sem("hi_done"), sem("lo_done")
        zt_loaded, gathered = [sem(f"zt_loaded{u}") for u in range(2)], [sem(f"gathered{u}") for u in range(2)]
        pos_done, x_stored = sem("pos_done"), sem("x_stored")
        hid_done, gelu_hi, gelu_full, gelu_lo = sem("hid_done"), sem("gelu_hi"), sem("gelu_full"), sem("gelu_lo")
        y_done, weighed, y_added, x_added = sem("y_done"), sem("weighed"), sem("y_added"), sem("x_added")
        block = ctx.enter_context(nc.Block())
        out_tiles = out.rearrange("b (j p) d -> p (b j) d", p=P)

        def before(n, u, per):
            return per * (n // 2) if isinstance(n, int) else per // 2 * (n - u)

        @block.sync
        def _(sync):
            sync.dma_start(w1_raw[:], w1_in[NE - 1]).then_inc(w_loaded, 16)
            sync.dma_start(w2_raw[:], w2_in[NE - 1]).then_inc(w_loaded, 16)
            sync.dma_start(b1[:], b1_in).then_inc(b1_loaded, 16)

            def load(n, u):
                after(sync, hid_done, KF * (n - 1))
                src = zt_kept[bass.ds(n, 1)].rearrange("n p k f -> p (n k f)")
                sync.dma_start(zt[u][:].rearrange("p k c t -> p (k c t)").bitcast(F32), src).then_inc(zt_loaded[u], 16)

            def store(n, u):
                sync.wait_ge(x_added, T * (n + 1))
                sync.dma_start(out_tiles[:, bass.ds(T * n, T), :], x_all[:, bass.ds(T * n, T), :]).then_inc(x_stored, 16)

            pipeline(sync, S.CHUNKS, ORDER, {"load": load, "outputs": store})
            sync.wait_ge(x_stored, 16 * S.CHUNKS)

        @block.gpsimd
        def _(pool):
            def gather(n, u):
                after(pool, x_added, T * (n - 1))
                if not (isinstance(n, int) and n < 2):
                    alone(pool, gathered[u], before(n, u, 16 * T * TOP), passed)
                for k in range(T * TOP):
                    pool.tensor_copy(pos_u[u][k][:], M.pos[:, bass.ds(T * n + k // TOP, 1), k % TOP:k % TOP + 1].rearrange("p t k -> p (t k)")).then_inc(pos_done, 1)
                alone(pool, pos_done, T * TOP * (n + 1), passed)
                for k in range(T * TOP):
                    pool.indirect_dma_start(rows[u][:, k, :], None, y_rows, bass.IndirectOffsetOnAxis(ap=pos_u[u][k][:], axis=0)).then_inc(gathered[u], 16)

            pipeline(pool, S.CHUNKS, ORDER, {"load": gather})

        @block.scalar
        def _(act):
            act.wait_ge(w_loaded, 32)
            act.activation(w1_hi[:], w1_raw[:], ACT.Copy).then_inc(hi_done, 1)
            act.activation(w2_hi[:], w2_raw[:], ACT.Copy).then_inc(hi_done, 1)
            act.wait_ge(b1_loaded, 16)

            def hidden(n, u):
                for m in range(KF):
                    act.wait_ge(hid_done, n * KF + m + 1)
                    alone(act, gelu_lo, n * KF + m + 1 - GR, passed)
                    if m == 0:
                        after(act, y_done, T * (n - 1))
                    act.activation(g_full[:, m % GR, :], hid[m % HR][:, 0:TOK], ACT.Gelu, bias=b1[:, NE - 1, m:m + 1]).then_inc(gelu_full, 1)
                    act.activation(g_hi[u][:, m, :], hid[m % HR][:, 0:TOK], ACT.Gelu, bias=b1[:, NE - 1, m:m + 1]).then_inc(gelu_hi, 1)

            pipeline(act, S.CHUNKS, ORDER, {"hidden": hidden})

        @block.vector
        def _(dve):
            for k, (raw, hi, lo) in enumerate(((w1_raw, w1_hi, w1_lo), (w2_raw, w2_hi, w2_lo))):
                dve.wait_ge(hi_done, k + 1)
                dve.tensor_tensor(lo[:], raw[:], hi[:], ALU.subtract).then_inc(lo_done, 1)

            def hidden(n, u):
                for m in range(KF):
                    dve.wait_ge(gelu_hi, n * KF + m + 1)
                    dve.wait_ge(gelu_full, n * KF + m + 1)
                    dve.tensor_tensor(g_lo[u][:, m, :], g_full[:, m % GR, :], g_hi[u][:, m, :], ALU.subtract).then_inc(gelu_lo, 1)

            def outputs(n, u):
                dve.wait_ge(gathered[u], before(n, u, 16 * T * TOP) + 16 * T * TOP)
                for k in range(TOP):
                    if k > 0:
                        dve.wait_ge(weighed, T * (TOP * n + k))
                    for t in range(T):
                        xs = x_all[:, T * n + t, :]
                        w = M.prob[:, bass.ds(T * n + t, 1), k:k + 1].rearrange("p t k -> p (t k)")
                        dve.scalar_tensor_tensor(out=xs, in0=rows[u][:, t * TOP + k, :], scalar=w, in1=xs, op0=ALU.mult, op1=ALU.add).then_inc(weighed, 1)
                dve.wait_ge(weighed, T * TOP * (n + 1))
                for t in range(T):
                    dve.wait_ge(y_done, T * n + t + 1)
                    xs = x_all[:, T * n + t, :]
                    dve.scalar_tensor_tensor(out=xs, in0=y[t][:, 0:D], scalar=M.half_tanh[:, 0:1], in1=xs, op0=ALU.mult, op1=ALU.add).then_inc(x_added, 1)

            pipeline(dve, S.CHUNKS, ORDER, {"hidden": hidden, "outputs": outputs})

        @block.tensor
        def _(pe):
            pe.wait_ge(lo_done, 2)

            def hidden(n, u):
                pe.wait_ge(zt_loaded[u], before(n, u, 16) + 16)
                for m in range(KF):
                    after(pe, gelu_hi, n * KF + m + 1 - HR)
                    cols = slice(m * P, (m + 1) * P)
                    for c in range(KD):
                        mm = three_passes(pe, hid[m % HR][:, 0:TOK], (w1_hi[:, c, cols], w1_lo[:, c, cols]),
                                          (zt[u][:, 0, c, :], zt[u][:, 1, c, :]), c == 0, c == KD - 1)
                    mm.then_inc(hid_done, 1)

            def outputs(n, u):
                pe.wait_ge(gelu_lo, (n + 1) * KF)
                for t in range(T):
                    after(pe, x_added, T * (n - 1) + t + 1)
                    cols = slice(t * P, (t + 1) * P)
                    for m in range(KF):
                        three_passes(pe, y[t][:, 0:D], (g_hi[u][:, m, cols], g_lo[u][:, m, cols]),
                                     (w2_hi[:, m, :], w2_lo[:, m, :]), m == 0, False)
                    pe.matmul(y[t][:, 0:D], M.shared_row[:, 1, :], M.bias2[:], start=False, stop=True).then_inc(y_done, 1)

            pipeline(pe, S.CHUNKS, ORDER, {"hidden": hidden, "outputs": outputs})


def phase_store(nc, x_all, out):
    with ExitStack() as ctx:
        stored = ctx.enter_context(nc.semaphore("stored"))
        block = ctx.enter_context(nc.Block())
        ov = out.rearrange("b (j p) d -> p (b j) d", p=P)

        @block.sync
        def _(sync):
            for c in range(4):
                sync.dma_start(ov[:, 8 * c:8 * c + 8, :], x_all[:, 8 * c:8 * c + 8, :]).then_inc(stored, 16)
            sync.wait_ge(stored, 64)


def flamingo_kernel(nc, t, out, phases="ABCD"):
    with ExitStack() as ctx:
        x_all = ctx.enter_context(nc.sbuf_tensor("x_all", [P, 32, 256], F32))
        tanh_g = ctx.enter_context(nc.sbuf_tensor("tanh_g", [P, 4], F32))
        ident = ctx.enter_context(nc.sbuf_tensor("ident", [P, P], F32))
        half_neg = ctx.enter_context(nc.sbuf_tensor("half_neg", [P, 8], F32))
        passed = ctx.enter_context(nc.semaphore("passed"))
        common = (nc, x_all, tanh_g, ident, half_neg, passed)
        phase_setup(nc, t["x"], t["gates"], x_all, tanh_g, ident, half_neg)
        if "A" in phases:
            phase_mlstm(*common, t["ctx"], t["ctx_t"], t["gate_w"], t["gate_b"], t["ln_scale"])
        if "B" in phases:
            phase_lora_ffn(*common, t["w_fc_t"], t["b_fc"], t["a_fc"], t["b_fc_t"], t["w_pr_t"], t["b_pr"], t["a_pr"],
                           t["b_pr_t"])
        if "C" in phases:
            phase_attention(*common, t["ctx_t"], t["wq"], t["wkv"], t["wc"])
        if "D" in phases:
            phase_moe(*common, t["router_w"], t["router_b"], t["w1"], t["b1"], t["b1_rows"], t["w2"], t["b2"], out)
        else:
            phase_store(nc, x_all, out)


def blocks_first(a):
    return a.reshape(-1, P, a.shape[-1]).transpose(1, 0, 2)


def lay_out(v):
    a = {k: np.asarray(i) for k, i in v.items()}
    ctx = a["ctx_1024"]
    t = {
        "x": a["x"],
        "gates": np.concatenate([a["g_xattn"], a["g_ffn"]]),
        "ctx": ctx,
        "ctx_t": ctx.reshape(-1, 2, P).transpose(2, 1, 0),
        "gate_w": blocks_first(np.concatenate([a["L0_xattn_igate_w"], a["L0_xattn_fgate_w"]]).T),
        "gate_b": np.concatenate([a["L0_xattn_igate_b"], a["L0_xattn_fgate_b"]]),
        "ln_scale": a["L0_xattn_ln_scale"],
        "w_fc_t": blocks_first(a["L0_ffn_W_fc"].T),
        "b_fc": a["L0_ffn_b_fc"].reshape(-1, P).T,
        "a_fc": a["L0_ffn_A_fc"],
        "b_fc_t": a["L0_ffn_B_fc"].T,
        "w_pr_t": blocks_first(a["L0_ffn_W_proj"].T),
        "b_pr": a["L0_ffn_b_proj"],
        "a_pr": a["L0_ffn_A_proj"],
        "b_pr_t": a["L0_ffn_B_proj"].T,
        "wq": blocks_first(a["L1_xattn_Wq"]),
        "wkv": blocks_first(a["L1_xattn_Wkv"]),
        "wc": blocks_first(a["L1_xattn_Wc"]),
        "router_w": blocks_first(a["L1_ffn_router_w"]),
        "router_b": a["L1_ffn_router_b"],
        "w1": np.concatenate([a["L1_ffn_w1"], a["L1_ffn_sw1"]]).reshape(10, 2, P, 512).transpose(0, 2, 1, 3),
        "b1": np.concatenate([a["L1_ffn_b1"], a["L1_ffn_sb1"]]).reshape(10, 4, P).transpose(2, 0, 1),
        "b1_rows": np.concatenate([a["L1_ffn_b1"], a["L1_ffn_sb1"]]),
        "w2": np.concatenate([a["L1_ffn_w2"], a["L1_ffn_sw2"]]).reshape(10, 4, P, 256).transpose(0, 2, 1, 3),
        "b2": np.concatenate([a["L1_ffn_b2"], a["L1_ffn_sb2"]]),
    }
    return {k: np.ascontiguousarray(i) for k, i in t.items()}


def build(nc, t, phases="ABCD"):
    aps = {k: nc.dram_tensor(f"in_{k}", i.shape, F32, kind="ExternalInput").ap() for k, i in t.items()}
    out = nc.dram_tensor("out_x", t["x"].shape, F32, kind="ExternalOutput").ap()
    flamingo_kernel(nc, aps, out, phases)


def kernel(**inputs):
    import concourse.bacc as bacc
    from concourse.bass_utils import run_bass_kernel_spmd

    nc = bacc.Bacc("TRN2", target_bir_lowering=False, num_devices=1)
    t = lay_out(inputs)
    build(nc, t)
    result = run_bass_kernel_spmd(nc, [{f"in_{k}": i for k, i in t.items()}], core_ids=[0])
    return result.results[0]["out_x"]
```
